# Optimizing a Trainium2 kernel written in Bass

```python
import numpy as np
import jax
import jax.numpy as jnp

def _softmax(x, axis=-1):
    return jax.nn.softmax(x, axis=axis)

def _gelu(x):
    return jax.nn.gelu(x, approximate=True)

def _silu(x):
    return jax.nn.silu(x)

def _sigmoid(x):
    return jax.nn.sigmoid(x)

def _layernorm(x, axis=-1, eps=1e-05):
    m = jnp.mean(x, axis=axis, keepdims=True)
    v = jnp.var(x, axis=axis, keepdims=True)
    return (x - m) / jnp.sqrt(v + eps)

def _scatter_add(tgt, idx, src, axis=0):
    return tgt.at[idx].add(src)

def _segment_sum(src, seg, n):
    return jax.ops.segment_sum(src, seg, n)
kernel_name = 'mk_gnn_preln_d2_gnn_r8_69fad7'

def setup_inputs(seed: int=0):
    np.random.seed(seed)
    _w = jnp.asarray

    def _rec_inputs():
        import jax
        import jax.numpy as jnp
        _gk = jax.random.key(seed)
        x = -0.0003713 + 1 * jax.random.normal(jax.random.fold_in(_gk, 1), (6250, 256), jnp.float32)
        src = jax.random.randint(jax.random.fold_in(_gk, 2), (100000,), 0, 6250, jnp.int32)
        dst = jax.random.randint(jax.random.fold_in(_gk, 3), (100000,), 0, 6250, jnp.int32)
        _o = jnp.argsort(dst, stable=True)
        src = src[_o]
        dst = dst[_o]
        edge_attr_16 = 0.000398945 + 1.00003 * jax.random.normal(jax.random.fold_in(_gk, 11), (100000, 16), jnp.float32)
        return (x, src, dst, edge_attr_16)
    x, src, dst, edge_attr_16 = _rec_inputs()

    def _L0_gnn_setup():
        import jax, jax.numpy as jnp
        import numpy as np
        N = 6250
        E = 100000
        D_IN = 256
        D_H = 512
        D_OUT = 256
        key = jax.random.key(seed)
        ks = jax.random.split(key, 12)
        s = lambda d: 1.0 / np.sqrt(d)
        x = jax.random.normal(ks[0], (N, D_IN), dtype=jnp.float32)
        edge_index = jax.random.randint(ks[1], (2, E), 0, N, dtype=jnp.int64)
        W_rel = jax.random.uniform(ks[2], (D_IN, D_H), jnp.float32, -s(D_IN), s(D_IN))
        b_rel = jax.random.uniform(ks[3], (D_H,), jnp.float32, -s(D_IN), s(D_IN))
        W_root = jax.random.uniform(ks[4], (D_IN, D_H), jnp.float32, -s(D_IN), s(D_IN))
        W_ih = jax.random.uniform(ks[5], (4 * D_H, D_H), jnp.float32, -s(D_H), s(D_H))
        W_hh = jax.random.uniform(ks[6], (4 * D_H, D_H), jnp.float32, -s(D_H), s(D_H))
        b_ih = jax.random.uniform(ks[7], (4 * D_H,), jnp.float32, -s(D_H), s(D_H))
        b_hh = jax.random.uniform(ks[8], (4 * D_H,), jnp.float32, -s(D_H), s(D_H))
        W_fc = jax.random.uniform(ks[9], (D_H, D_OUT), jnp.float32, -s(D_H), s(D_H))
        b_fc = jax.random.uniform(ks[10], (D_OUT,), jnp.float32, -s(D_H), s(D_H))
        return {'x': x, 'edge_index': edge_index, 'W_rel': W_rel, 'b_rel': b_rel, 'W_root': W_root, 'W_ih': W_ih, 'W_hh': W_hh, 'b_ih': b_ih, 'b_hh': b_hh, 'W_fc': W_fc, 'b_fc': b_fc}
    _L0_gnn_all = _L0_gnn_setup()
    _L0_gnn_in = {k: v for k, v in _L0_gnn_all.items() if k in ('W_rel', 'b_rel', 'W_root', 'W_ih', 'W_hh', 'b_ih', 'b_hh', 'W_fc', 'b_fc')}
    del _L0_gnn_all

    def _L1_gnn_setup():
        import jax, jax.numpy as jnp
        import numpy as np
        N, E = (6250, 50000)
        HEADS, DIMS, EDGE_DIM = (4, 64, 16)
        FEAT = HEADS * DIMS
        NEG_SLOPE = 0.2

        def _gatv2(x, edge_index, edge_attr, W_l, b_l, W_r, b_r, W_e, att, bias):
            n = x.shape[0]
            src, dst = (edge_index[0], edge_index[1])
            x_l = (x @ W_l.T + b_l).reshape(n, HEADS, DIMS)
            x_r = (x @ W_r.T + b_r).reshape(n, HEADS, DIMS)
            ones = jnp.ones((src.shape[0],), x.dtype)
            deg = jax.ops.segment_sum(ones, dst, num_segments=n)
            loop_attr = jax.ops.segment_sum(edge_attr, dst, num_segments=n)
            loop_attr = loop_attr / jnp.clip(deg, 1.0, None)[:, None]
            loop = jnp.arange(n, dtype=src.dtype)
            src = jnp.concatenate([src, loop])
            dst = jnp.concatenate([dst, loop])
            e_attr = jnp.concatenate([edge_attr, loop_attr], axis=0)
            e_feat = (e_attr @ W_e.T).reshape(-1, HEADS, DIMS)
            s = x_l[src] + x_r[dst] + e_feat
            s = jax.nn.leaky_relu(s, NEG_SLOPE)
            alpha = jnp.einsum('ehc,hc->eh', s, att)
            amax = jax.ops.segment_max(alpha, dst, num_segments=n)
            ex = jnp.exp(alpha - amax[dst])
            denom = jax.ops.segment_sum(ex, dst, num_segments=n)
            alpha = ex / (denom[dst] + 1e-16)
            out = jax.ops.segment_sum(alpha[..., None] * x_l[src], dst, num_segments=n)
            return out.reshape(n, FEAT) + bias
        key = jax.random.key(seed)
        ks = jax.random.split(key, 10)
        s = 0.05
        return {'x': jax.random.normal(ks[0], (N, FEAT), jnp.float32), 'edge_index': jax.random.randint(ks[1], (2, E), 0, N, jnp.int64), 'edge_attr': jax.random.normal(ks[2], (E, EDGE_DIM), jnp.float32), 'W_l': jax.random.normal(ks[3], (FEAT, FEAT), jnp.float32) * s, 'b_l': jnp.zeros((FEAT,), jnp.float32), 'W_r': jax.random.normal(ks[4], (FEAT, FEAT), jnp.float32) * s, 'b_r': jnp.zeros((FEAT,), jnp.float32), 'W_e': jax.random.normal(ks[5], (FEAT, EDGE_DIM), jnp.float32) * s, 'att': jax.random.normal(ks[6], (HEADS, DIMS), jnp.float32) * s, 'bias': jnp.zeros((FEAT,), jnp.float32)}
    _L1_gnn_all = _L1_gnn_setup()
    _L1_gnn_in = {k: v for k, v in _L1_gnn_all.items() if k in ('W_l', 'b_l', 'W_r', 'b_r', 'W_e', 'att', 'bias')}
    del _L1_gnn_all
    return {'x': x, 'src': src, 'dst': dst, 'edge_attr_16': edge_attr_16, 'L0_gnn_W_rel': _L0_gnn_in['W_rel'], 'L0_gnn_b_rel': _L0_gnn_in['b_rel'], 'L0_gnn_W_root': _L0_gnn_in['W_root'], 'L0_gnn_W_ih': _L0_gnn_in['W_ih'], 'L0_gnn_W_hh': _L0_gnn_in['W_hh'], 'L0_gnn_b_ih': _L0_gnn_in['b_ih'], 'L0_gnn_b_hh': _L0_gnn_in['b_hh'], 'L0_gnn_W_fc': _L0_gnn_in['W_fc'], 'L0_gnn_b_fc': _L0_gnn_in['b_fc'], 'L1_gnn_W_l': _L1_gnn_in['W_l'], 'L1_gnn_b_l': _L1_gnn_in['b_l'], 'L1_gnn_W_r': _L1_gnn_in['W_r'], 'L1_gnn_b_r': _L1_gnn_in['b_r'], 'L1_gnn_W_e': _L1_gnn_in['W_e'], 'L1_gnn_att': _L1_gnn_in['att'], 'L1_gnn_bias': _L1_gnn_in['bias']}

def reference(x, src, dst, edge_attr_16, L0_gnn_W_rel, L0_gnn_b_rel, L0_gnn_W_root, L0_gnn_W_ih, L0_gnn_W_hh, L0_gnn_b_ih, L0_gnn_b_hh, L0_gnn_W_fc, L0_gnn_b_fc, L1_gnn_W_l, L1_gnn_b_l, L1_gnn_W_r, L1_gnn_b_r, L1_gnn_W_e, L1_gnn_att, L1_gnn_bias):
    import jax
    import jax.numpy as jnp

    def _L0_gnn_ref(x, edge_index, W_rel, b_rel, W_root, W_ih, W_hh, b_ih, b_hh, W_fc, b_fc):
        import jax, jax.numpy as jnp
        import numpy as np
        N = 6250
        E = 100000
        D_IN = 256
        D_H = 512
        D_OUT = 256
        src, dst = (edge_index[0], edge_index[1])
        agg = jax.ops.segment_sum(x[src], dst, num_segments=N)
        h = jax.nn.relu(agg @ W_rel + b_rel + x @ W_root)
        gates = h @ W_ih.T + b_ih + b_hh
        i, f, g, o = jnp.split(gates, 4, axis=-1)
        c = jax.nn.sigmoid(i) * jnp.tanh(g)
        h_lstm = jax.nn.sigmoid(o) * jnp.tanh(c)
        return h_lstm @ W_fc + b_fc

    def _L1_gnn_ref(x, edge_index, edge_attr, W_l, b_l, W_r, b_r, W_e, att, bias):
        import jax, jax.numpy as jnp
        import numpy as np
        N, E = (6250, 50000)
        HEADS, DIMS, EDGE_DIM = (4, 64, 16)
        FEAT = HEADS * DIMS
        NEG_SLOPE = 0.2

        def _gatv2(x, edge_index, edge_attr, W_l, b_l, W_r, b_r, W_e, att, bias):
            n = x.shape[0]
            src, dst = (edge_index[0], edge_index[1])
            x_l = (x @ W_l.T + b_l).reshape(n, HEADS, DIMS)
            x_r = (x @ W_r.T + b_r).reshape(n, HEADS, DIMS)
            ones = jnp.ones((src.shape[0],), x.dtype)
            deg = jax.ops.segment_sum(ones, dst, num_segments=n)
            loop_attr = jax.ops.segment_sum(edge_attr, dst, num_segments=n)
            loop_attr = loop_attr / jnp.clip(deg, 1.0, None)[:, None]
            loop = jnp.arange(n, dtype=src.dtype)
            src = jnp.concatenate([src, loop])
            dst = jnp.concatenate([dst, loop])
            e_attr = jnp.concatenate([edge_attr, loop_attr], axis=0)
            e_feat = (e_attr @ W_e.T).reshape(-1, HEADS, DIMS)
            s = x_l[src] + x_r[dst] + e_feat
            s = jax.nn.leaky_relu(s, NEG_SLOPE)
            alpha = jnp.einsum('ehc,hc->eh', s, att)
            amax = jax.ops.segment_max(alpha, dst, num_segments=n)
            ex = jnp.exp(alpha - amax[dst])
            denom = jax.ops.segment_sum(ex, dst, num_segments=n)
            alpha = ex / (denom[dst] + 1e-16)
            out = jax.ops.segment_sum(alpha[..., None] * x_l[src], dst, num_segments=n)
            return out.reshape(n, FEAT) + bias
        h = _gatv2(x, edge_index, edge_attr, W_l, b_l, W_r, b_r, W_e, att, bias)
        h = jax.nn.silu(h)
        return x + h
    edge_index = jnp.stack([src, dst])
    h = jnp.maximum(_layernorm(x, axis=-1), 0.0)
    x = x + _L0_gnn_ref(h, edge_index, L0_gnn_W_rel, L0_gnn_b_rel, L0_gnn_W_root, L0_gnn_W_ih, L0_gnn_W_hh, L0_gnn_b_ih, L0_gnn_b_hh, L0_gnn_W_fc, L0_gnn_b_fc)
    h = jnp.maximum(_layernorm(x, axis=-1), 0.0)
    x = x + _L1_gnn_ref(h, edge_index, edge_attr_16, L1_gnn_W_l, L1_gnn_b_l, L1_gnn_W_r, L1_gnn_b_r, L1_gnn_W_e, L1_gnn_att, L1_gnn_bias)
    return x

_drawn_inputs = setup_inputs


def setup_inputs(seed=0):
    import zlib

    import numpy as np

    out = dict(_drawn_inputs(seed))
    spreads = {'L1_gnn_b_l': (0.0, 0.1), 'L1_gnn_b_r': (0.0, 2.0), 'L1_gnn_bias': (0.0, 0.1)}
    factors = {'edge_attr_16': 8.0,
     'L0_gnn_b_rel': 39.449,
     'L0_gnn_W_root': 3.255,
     'L0_gnn_b_ih': 21.677,
     'L0_gnn_b_hh': 8.0,
     'L1_gnn_W_r': 8.0,
     'L1_gnn_W_e': 8.0,
     'L1_gnn_att': 8.0}
    for name, (base, spread) in spreads.items():
        noise = np.random.default_rng([zlib.crc32(name.encode()), seed]).standard_normal(out[name].shape)
        drawn = base * np.exp(spread * noise) if base else spread * noise
        out[name] = jnp.asarray(drawn.astype(out[name].dtype))
    for name, factor in factors.items():
        out[name] = (out[name] * factor).astype(out[name].dtype)
    return out
```

```python
from contextlib import ExitStack

import numpy as np
import concourse.bass as bass
from concourse import mybir

F32 = mybir.dt.float32
I32 = mybir.dt.int32
ALU = mybir.AluOpType
ACT = mybir.ActivationFunctionType
AX = mybir.AxisListType

N_NODES, N_EDGES = 6250, 100000
D, DH = 256, 512
HEADS, HD = 4, 64
ED = 16
TN = 125
TILES = N_NODES // TN
KT = 17
STEP_E = KT * 128
STEPS_MAX = TILES + -(-N_EDGES // STEP_E)
TABLE = 128
ROUNDS = -(-N_EDGES // STEP_E)
E_PAD = N_EDGES + STEP_E
XW = D + HEADS
AW = D + ED + 1
RECW = 2 * D + HEADS
NJ = DH // 128
BIG = 1.0e30
EPS = 1.0e-5
QS = [range(0, 4), range(4, 8), range(8, 12), range(12, 16), range(16, 17)]
NQ = len(QS)
assert STEPS_MAX + 2 <= TABLE and TILES * TN == N_NODES


class Count:

    def __init__(self):
        self.n = 0

    def one_more(self):
        self.n += 1
        return self.n


def gnn_layers(nc, x, src, dst, attrT, w_rr, b_rel, w_ihT, b_ih, b_hh, w_fc, b_fc, w_lr, b_l, b_r, w_eT, att, bias, out):
    ctx = ExitStack()
    with ctx:
        def sb(name, shape, dt=F32):
            return ctx.enter_context(nc.sbuf_tensor(name, shape, dt))

        def sem(name):
            return ctx.enter_context(nc.semaphore(name))

        def stage_sem(scope, name, engine):
            q = scope.enter_context(nc.semaphore(name))
            to_start.append((engine, q))
            return q

        to_start = []

        def start(eng, engine):
            for of, q in list(to_start):
                if of == engine:
                    eng.sem_inc(q, 1)
                    to_start.remove((of, q))

        h_rows = nc.dram_tensor("h_rows", [N_NODES, D], F32).ap()
        xl_rows = nc.dram_tensor("xl_rows", [N_NODES, D], F32).ap()
        node_rec = nc.dram_tensor("node_rec", [N_NODES, RECW], F32).ap()
        step_list = nc.dram_tensor("step_list", [TABLE, 2], I32).ap()

        bk = [ctx.enter_context(nc.psum_tensor(f"bank{i}", [128, 512], F32)) for i in range(8)]

        wrr = sb("wrr", [128, 4, DH])
        wih = sb("wih", [128, NJ, 3 * DH])
        wfc = sb("wfc", [128, NJ, D])
        wlr = sb("wlr", [128, 2, 2 * D])
        weT = sb("weT", [ED, D])
        brel = sb("brel", [128, NJ])
        bg1 = sb("bg1", [128, 12])
        bg2 = sb("bg2", [128, 12])
        bg = sb("bg", [128, 12])
        bfc = sb("bfc", [128, D])
        blr = sb("blr", [128, 2 * D])
        bout = sb("bout", [128, D])
        attb = sb("attb", [128, D])
        attc = sb("attc", [128, 2, HEADS])
        ident = sb("ident", [128, 128])
        ones = sb("ones", [128, 128])
        iota_n = sb("iota_n", [128, 128])
        iota_p = sb("iota_p", [128, 1])
        table = sb("table", [1, TABLE * 2], I32)
        n_pairs = sb("n_pairs", [1, 2], I32)
        baseT = sb("baseT", [128, TABLE])
        keepT = sb("keepT", [128, TABLE])
        idx_all = sb("idx_all", [128, TABLE * 2 * KT], I32)
        idx = [sb(f"idx{s}", [128, KT], I32) for s in range(2)]
        drel = sb("drel", [128, KT])
        eri = [sb(f"eri{s}", [64, 128], I32) for s in range(2)]
        erf = [sb(f"erf{s}", [64, 128]) for s in range(2)]
        rows = [sb(f"rows{s}", [128, KT * AW]) for s in range(2)]
        rows0 = [r[:, :].rearrange("p (k c) -> p k c", k=KT) for r in rows]
        rows1 = [r[:, 0:KT * XW].rearrange("p (k c) -> p k c", k=KT) for r in rows]
        onehot = [sb(f"onehot{s}", [128, KT, TN]) for s in range(2)]
        attr = [sb(f"attr{s}", [ED, STEP_E]) for s in range(2)]
        small = sb("small", [128, 64])
        stats = [sb(f"stats{s}", [128, 12]) for s in range(2)]

        PS_T, PS_AGG = bk[2:4], bk[0:2]

        setup_in = sem("setup_in")
        setup_c = sem("setup_c")
        dst_in = sem("dst_in")
        setup_t = sem("setup_t")
        counts_ps = sem("counts_ps")
        table_out = sem("table_out")
        table_in = sem("table_in")
        ln_in = [sem(f"ln_in{s}") for s in range(2)]
        ln_v = sem("ln_v")
        ln_var = sem("ln_var")
        ln_std = sem("ln_std")
        ln_out = [sem(f"ln_out{s}") for s in range(2)]
        setup_v = sem("setup_v")
        passed = sem("passed")
        er_in = [sem(f"er_in{s}") for s in range(2)]
        gathered = [sem(f"gathered{s}") for s in range(2)]

        with ExitStack() as sc:
            def tmp(name, shape, dt=F32):
                return sc.enter_context(nc.sbuf_tensor(name, shape, dt))
            dsti = tmp("dsti", [TN, N_EDGES // TN], I32)
            dstf = tmp("dstf", [TN, N_EDGES // TN])
            junk = tmp("junk", [TN, N_EDGES // TN])
            part = tmp("part", [128, TILES + 1])
            first = tmp("first", [128, TILES + 1])
            cnt = tmp("cnt", [128, TILES])
            thr = tmp("thr", [128, ROUNDS])
            over = tmp("over", [128, TILES, ROUNDS])
            rnd = tmp("rnd", [128, TILES])
            cum = tmp("cum", [128, TILES])
            zero = tmp("zero", [128, TILES])
            cmp = tmp("cmp", [128, TILES])
            sel = tmp("sel", [128, TILES])
            col = tmp("col", [128, 12])
            step2 = tmp("step2", [128, 2], I32)
            diag = tmp("diag", [128, 2, 128])
            xt = [tmp(f"xt{s}", [TN, 5, D]) for s in range(2)]
            xh = [tmp(f"xh{s}", [TN, 5, D]) for s in range(2)]
            x5 = x.rearrange("(i p j) c -> i p (j c)", p=TN, j=5)
            h5 = h_rows.rearrange("(i p j) c -> i p (j c)", p=TN, j=5)
            LN_T = N_NODES // (5 * TN)

            block = sc.enter_context(nc.Block())

            @block.sync
            def _(sp):
                sp.dma_start(dsti[:, :], dst[0:N_EDGES].rearrange("(p c) -> p c", p=TN)).then_inc(dst_in, 16)
                for s in range(2):
                    sp.dma_start(xt[s][:, :, :].rearrange("p j c -> p (j c)"), x5[s]).then_inc(ln_in[s], 16)
                loads = [(wrr[:, :, :], w_rr.rearrange("(k p) n -> p k n", p=128)),
                         (wih[:, :, :], w_ihT.rearrange("(k p) n -> p k n", p=128)),
                         (wfc[:, :, :], w_fc.rearrange("(k p) n -> p k n", p=128)),
                         (wlr[:, :, :], w_lr.rearrange("(k p) n -> p k n", p=128)),
                         (weT[:, :], w_eT), (brel[:, :], b_rel), (bg1[:, :], b_ih), (bg2[:, :], b_hh),
                         (bfc[:, :], b_fc.partition_broadcast(128)), (blr[:, 0:D], b_l.partition_broadcast(128)),
                         (blr[:, D:2 * D], b_r.partition_broadcast(128)), (bout[:, :], bias.partition_broadcast(128)),
                         (attb[:, :], att.partition_broadcast(128))]
                for to, of in loads:
                    sp.dma_start(to, of).then_inc(setup_in, 16)
                sp.wait_ge(setup_c, 7)
                for h in range(HEADS):
                    sp.dma_start(attc[64 * (h % 2):64 * (h % 2) + 64, h // 2, h:h + 1],
                                 att[HD * h:HD * h + HD].rearrange("(c a) -> c a", a=1)).then_inc(setup_in, 16)
                for i in range(LN_T):
                    s = i % 2
                    sp.wait_ge(ln_v, i + 1)
                    sp.dma_start(h5[i], xh[s][:, :, :].rearrange("p j c -> p (j c)")).then_inc(ln_out[s], 16)
                    if i + 2 < LN_T:
                        sp.dma_start(xt[s][:, :, :].rearrange("p j c -> p (j c)"), x5[i + 2]).then_inc(ln_in[s], 16)
                sp.wait_ge(setup_t, 1)
                sp.dma_start(step_list, step2[:, :]).then_inc(table_out, 16)
                sp.wait_ge(table_out, 16)
                sp.dma_start(table[:, :], step_list.rearrange("(a n) c -> a (n c)", a=1)).then_inc(table_in, 16)
                sp.wait_ge(table_in, 16)
                sp.wait_ge(setup_in, 16 * 17)
                for s in range(2):
                    sp.wait_ge(ln_out[s], 16 * (LN_T // 2))

            @block.gpsimd
            def _(pool):
                pool.memset(small[:, :], 0.0).then_inc(setup_c, 1)
                pool.memset(ident[:, :], 0.0).then_inc(setup_c, 1)
                pool.memset(ones[:, :], 1.0).then_inc(setup_c, 1)
                pool.memset(idx_all[:, :], 0).then_inc(setup_c, 1)
                pool.memset(attc[:, :, :], 0.0).then_inc(setup_c, 1)
                pool.memset(eri[0][:, :], 0).then_inc(setup_c, 1)
                pool.memset(eri[1][:, :], 0).then_inc(setup_c, 1)
                pool.iota(iota_n[:, :], pattern=[[1, 128]], base=0, channel_multiplier=0,
                          allow_small_or_imprecise_dtypes=True).then_inc(setup_c, 1)
                pool.iota(iota_p[:, :], pattern=[[0, 1]], base=0, channel_multiplier=1,
                          allow_small_or_imprecise_dtypes=True).then_inc(setup_c, 1)
                pool.iota(thr[:, :], pattern=[[STEP_E, ROUNDS]], base=STEP_E, channel_multiplier=0,
                          allow_small_or_imprecise_dtypes=True).then_inc(setup_c, 1)
                pool.wait_ge(setup_c, 10)
                pool.affine_select(out=ident[:, :], in_=ident[:, :], compare_op=ALU.not_equal, fill=1.0,
                                   base=0, pattern=[[-1, 128]], channel_multiplier=1).then_inc(setup_c, 1)

            @block.tensor
            def _(pe):
                pe.wait_ge(setup_c, 11)
                pe.wait_ge(counts_ps, 1)
                pe.matmul(bk[0][:, 0:TILES + 1], ones[0:TN, :], part[0:TN, :], start=True, stop=True).then_inc(counts_ps, 1)
                pe.wait_ge(counts_ps, 3)
                pe.matmul(bk[1][:, 0:256], ones[:, :], diag[:, :, :], start=True, stop=True).then_inc(counts_ps, 1)

            @block.vector
            def _(v):
                signals = Count()

                v.wait_ge(dst_in, 16)
                v.wait_ge(setup_c, 11)
                v.tensor_copy(dstf[:, :], dsti[:, :]).then_inc(setup_v, 1)
                v.wait_ge(setup_v, signals.one_more())
                v.memset(part[:, 0:1], 0.0)
                for t in range(1, TILES):
                    v.tensor_scalar(junk[:, :], dstf[:, :], float(TN * t), 0.0, ALU.is_lt, ALU.add,
                                    accum_out=part[0:TN, t:t + 1]).then_inc(setup_v, 1)
                    v.wait_ge(setup_v, signals.one_more())
                v.memset(part[0:TN, TILES:TILES + 1], float(N_EDGES // TN)).then_inc(counts_ps, 1)
                for i in range(LN_T):
                    s = i % 2
                    v.wait_ge(ln_in[s], 16 * (i // 2 + 1))
                    if i >= 2:
                        v.wait_ge(ln_out[s], 16 * (i // 2))
                    for j in range(5):
                        ins = v.bn_stats(small[0:TN, 6 * j:6 * j + 6], xt[s][:, j, :])
                    ins.then_inc(setup_v, 1)
                    v.wait_ge(setup_v, signals.one_more())
                    for j in range(5):
                        ins = v.bn_aggr(small[0:TN, 32 + 2 * j:34 + 2 * j], small[0:TN, 6 * j:6 * j + 6])
                    ins.then_inc(setup_v, 1)
                    v.wait_ge(setup_v, signals.one_more())
                    mv = small[0:TN, 32:42].rearrange("p (j a) -> p j a", a=2)
                    v.tensor_scalar(small[0:TN, 48:53], mv[:, :, 1], EPS, None, ALU.add).then_inc(ln_var, 1)
                    v.wait_ge(ln_std, i + 1)
                    v.reciprocal(small[0:TN, 56:61], small[0:TN, 42:47]).then_inc(setup_v, 1)
                    v.wait_ge(setup_v, signals.one_more())
                    for j in range(5):
                        ins = v.tensor_scalar(xh[s][:, j, :], xt[s][:, j, :], small[0:TN, 32 + 2 * j:33 + 2 * j],
                                              small[0:TN, 56 + j:57 + j], ALU.subtract, ALU.mult)
                    ins.then_inc(setup_v, 1)
                    v.wait_ge(setup_v, signals.one_more())
                    v.tensor_scalar(xh[s][:, :, :], xh[s][:, :, :], 0.0, None, ALU.max).then_inc(ln_v, 1)
                v.wait_ge(counts_ps, 2)
                v.tensor_copy(first[:, :], bk[0][:, 0:TILES + 1]).then_inc(setup_v, 1)
                v.wait_ge(setup_v, signals.one_more())
                v.tensor_tensor(cnt[:, :], first[:, 1:TILES + 1], first[:, 0:TILES], ALU.subtract).then_inc(setup_v, 1)
                v.wait_ge(setup_v, signals.one_more())
                v.tensor_tensor(over[:, :, :], cnt[:, :].unsqueeze(2).broadcast_to([128, TILES, ROUNDS]),
                                thr[:, :].unsqueeze(1).broadcast_to([128, TILES, ROUNDS]), ALU.is_gt).then_inc(setup_v, 1)
                v.wait_ge(setup_v, signals.one_more())
                v.tensor_reduce(rnd[:, :], over[:, :, :], AX.X, ALU.add).then_inc(setup_v, 1)
                v.wait_ge(setup_v, signals.one_more())
                v.tensor_scalar(rnd[:, :], rnd[:, :], 1.0, None, ALU.add).then_inc(setup_v, 1)
                v.wait_ge(setup_v, signals.one_more())
                v.memset(zero[:, :], 0.0).then_inc(setup_v, 1)
                v.wait_ge(setup_v, signals.one_more())
                v.tensor_tensor_scan(cum[:, :], rnd[:, :], zero[:, :], 0.0, ALU.add, ALU.add).then_inc(setup_v, 1)
                v.wait_ge(setup_v, signals.one_more())
                v.tensor_scalar(cmp[:, :], cum[:, :], iota_p[:, 0:1], None, ALU.is_le).then_inc(setup_v, 1)
                v.wait_ge(setup_v, signals.one_more())
                v.tensor_reduce(col[:, 0:1], cmp[:, :], AX.X, ALU.add).then_inc(setup_v, 1)
                v.wait_ge(setup_v, signals.one_more())
                v.tensor_scalar(col[:, 1:2], col[:, 0:1], float(TILES - 1), None, ALU.min).then_inc(setup_v, 1)
                v.wait_ge(setup_v, signals.one_more())
                v.tensor_scalar(sel[:, :], iota_n[:, 0:TILES], col[:, 1:2], None, ALU.is_equal).then_inc(setup_v, 1)
                v.wait_ge(setup_v, signals.one_more())
                v.tensor_tensor(cmp[:, :], cum[:, :], rnd[:, :], ALU.subtract).then_inc(setup_v, 1)
                v.wait_ge(setup_v, signals.one_more())
                v.tensor_tensor(cmp[:, :], cmp[:, :], sel[:, :], ALU.mult).then_inc(setup_v, 1)
                v.wait_ge(setup_v, signals.one_more())
                v.tensor_reduce(col[:, 2:3], cmp[:, :], AX.X, ALU.add).then_inc(setup_v, 1)
                v.wait_ge(setup_v, signals.one_more())
                v.tensor_tensor(sel[:, :], sel[:, :], first[:, 0:TILES], ALU.mult).then_inc(setup_v, 1)
                v.wait_ge(setup_v, signals.one_more())
                v.tensor_reduce(col[:, 3:4], sel[:, :], AX.X, ALU.add).then_inc(setup_v, 1)
                v.wait_ge(setup_v, signals.one_more())
                v.tensor_tensor(col[:, 4:5], iota_p[:, 0:1], col[:, 2:3], ALU.subtract).then_inc(setup_v, 1)
                v.wait_ge(setup_v, signals.one_more())
                v.tensor_scalar(col[:, 5:6], col[:, 4:5], 0.0, None, ALU.is_gt).then_inc(setup_v, 1)
                v.wait_ge(setup_v, signals.one_more())
                v.tensor_scalar(col[:, 6:7], col[:, 4:5], float(STEP_E), None, ALU.mult).then_inc(setup_v, 1)
                v.wait_ge(setup_v, signals.one_more())
                v.tensor_tensor(col[:, 6:7], col[:, 6:7], col[:, 3:4], ALU.add).then_inc(setup_v, 1)
                v.wait_ge(setup_v, signals.one_more())
                v.tensor_scalar(col[:, 6:7], col[:, 6:7], float(N_EDGES), None, ALU.min).then_inc(setup_v, 1)
                v.wait_ge(setup_v, signals.one_more())
                v.tensor_scalar(col[:, 7:8], col[:, 1:2], float(TN), None, ALU.mult).then_inc(setup_v, 1)
                v.wait_ge(setup_v, signals.one_more())
                v.tensor_copy(step2[:, :], col[:, 6:8]).then_inc(setup_v, 1)
                v.wait_ge(setup_v, signals.one_more())
                v.tensor_scalar(diag[:, 0, :], ident[:, :], col[:, 7:8], None, ALU.mult).then_inc(setup_v, 1)
                v.wait_ge(setup_v, signals.one_more())
                v.tensor_scalar(diag[:, 1, :], ident[:, :], col[:, 5:6], None, ALU.mult).then_inc(counts_ps, 1)
                v.tensor_scalar(junk[0:1, 0:64], iota_n[0:1, 0:64], 2.0, None, ALU.mult).then_inc(setup_v, 1)
                v.wait_ge(setup_v, signals.one_more())
                v.tensor_scalar(junk[0:1, 0:64], junk[0:1, 0:64], cum[0:1, TILES - 1:TILES], None, ALU.is_lt).then_inc(setup_v, 1)
                v.wait_ge(setup_v, signals.one_more())
                v.tensor_reduce(col[0:1, 8:9], junk[0:1, 0:64], AX.X, ALU.add).then_inc(setup_v, 1)
                v.wait_ge(setup_v, signals.one_more())
                v.tensor_scalar(n_pairs[:, 0:1], col[0:1, 8:9], -1.0, None, ALU.add).then_inc(setup_t, 1)
                v.wait_ge(counts_ps, 4)
                v.tensor_copy(baseT[:, :], bk[1][:, 0:128])
                v.tensor_copy(keepT[:, :], bk[1][:, 128:256])
                v.wait_ge(setup_in, 16 * 17)
                v.tensor_tensor(bg[:, :], bg1[:, :], bg2[:, :], ALU.add).then_inc(setup_t, 1)

            @block.scalar
            def _(act):
                for i in range(LN_T):
                    act.wait_ge(ln_var, i + 1)
                    act.activation(small[0:TN, 42:47], small[0:TN, 48:53], ACT.Sqrt).then_inc(ln_std, 1)

        er_v = stage_sem(ctx, "er_v", "vector")
        er_ps = stage_sem(ctx, "er_ps", "tensor")
        with nc.Block() as block:
            def edge_rows(table_of, first_edge):
                return table_of.rearrange("(a n) -> a n", a=1)[:, bass.ds(first_edge, STEP_E)].rearrange(
                    "a (k e) -> (a k) e", e=128)

            @block.sync
            def _(sp):
                start(sp, "sync")
                last_i = sp.value_load(n_pairs[0:1, 0:1], min_val=1, max_val=TABLE // 2 - 2)
                pairs = last_i + 1
                with sp.Fori(0, pairs) as i:
                    for s in range(2):
                        e0 = sp.value_load(table[0:1, bass.ds(i * 4 + 2 * s, 1)], min_val=0, max_val=N_EDGES)
                        sp.wait_ge(er_v, i * 4 + 1)
                        sp.sem_inc(passed, 1)
                        sp.dma_start(eri[s][0:KT, :], edge_rows(src, e0)).then_inc(er_in[s], 16)
                        sp.dma_start(eri[s][32:32 + KT, :], edge_rows(dst, e0)).then_inc(er_in[s], 16)

            @block.vector
            def _(v):
                start(v, "vector")
                last_i = v.value_load(n_pairs[0:1, 0:1], min_val=1, max_val=TABLE // 2 - 2)
                pairs = last_i + 1
                with v.Fori(0, pairs) as i:
                    for s in range(2):
                        v.wait_ge(er_v, i * 4 + 2 * s + 1)
                        v.wait_ge(er_in[s], i * 32 + 32)
                        v.tensor_copy(erf[s][:, :], eri[s][:, :]).then_inc(er_v, 1)
                        v.wait_ge(er_ps, i * 2 + s + 2)
                        v.tensor_copy(
                   idx_all[:, bass.ds(i * (4 * KT) + s * 2 * KT, 2 * KT)].rearrange("p (a k) -> p a k", a=2),
                   bk[s][:, 0:64].rearrange("p (a k) -> p a k", a=2)[:, :, 0:KT]).then_inc(er_v, 1)

            @block.tensor
            def _(pe):
                start(pe, "tensor")
                last_i = pe.value_load(n_pairs[0:1, 0:1], min_val=1, max_val=TABLE // 2 - 2)
                pairs = last_i + 1
                with pe.Fori(0, pairs) as i:
                    for s in range(2):
                        pe.wait_ge(er_v, i * 4 + 2 * s + 2)
                        pe.sem_inc(passed, 1)
                        pe.transpose(bk[s][:, 0:64], erf[s][:, :], ident[0:64, 0:64]).then_inc(er_ps, 1)

        with ExitStack() as sc:
            def tmp(name, shape, dt=F32):
                return sc.enter_context(nc.sbuf_tensor(name, shape, dt))

            def dma_sem(name):
                return sc.enter_context(nc.semaphore(name))

            hin = [tmp(f"hin{s}", [TN, D]) for s in range(2)]
            xin = [tmp(f"xin{s}", [TN, D]) for s in range(2)]
            agg = [tmp(f"agg{s}", [TN, AW]) for s in range(2)]
            mean = [tmp(f"mean{s}", [TN, ED]) for s in range(2)]
            meanT = [tmp(f"meanT{s}", [ED, TN]) for s in range(2)]
            xT = tmp("xT", [128, 4, 2 * TN])
            h1T = tmp("h1T", [128, NJ, 2 * TN])
            gate = [[tmp(f"gate{g}{b}", [128, 2 * TN]) for b in range(2)] for g in "igotc"]
            lstmT = tmp("lstmT", [128, NJ, 2 * TN])
            x1 = [tmp(f"x1{s}", [TN, D]) for s in range(2)]
            h2 = [tmp(f"h2{s}", [TN, D]) for s in range(2)]
            h2T = [tmp(f"h2T{s}", [128, 2, TN]) for s in range(2)]
            xl = [tmp(f"xl{s}", [TN, D]) for s in range(2)]
            rec = [tmp(f"rec{s}", [TN, RECW]) for s in range(2)]
            ss = tmp("ss", [TN, D])
            sk = tmp("sk", [TN, D])

            idx_ready = stage_sem(sc, "idx_ready", "vector")
            norm_v = stage_sem(sc, "norm_v", "vector")
            scale_v = stage_sem(sc, "scale_v", "vector")
            node_v = stage_sem(sc, "node_v", "vector")
            loaded = [dma_sem(f"loaded{s}") for s in range(2)]
            attr_ps = stage_sem(sc, "attr_ps", "tensor")
            attr_sb = stage_sem(sc, "attr_sb", "scalar")
            hot = stage_sem(sc, "hot", "vector")
            agg_ps = stage_sem(sc, "agg_ps", "tensor")
            agg_sb = stage_sem(sc, "agg_sb", "vector")
            xT_ps = stage_sem(sc, "xT_ps", "tensor")
            xT_sb = stage_sem(sc, "xT_sb", "scalar")
            h1_ps = stage_sem(sc, "h1_ps", "tensor")
            h1_sb = stage_sem(sc, "h1_sb", "scalar")
            gate_ps = stage_sem(sc, "gate_ps", "tensor")
            gate_ig = stage_sem(sc, "gate_ig", "scalar")
            gate_to = stage_sem(sc, "gate_to", "scalar")
            cell = stage_sem(sc, "cell", "vector")
            lstm_sb = stage_sem(sc, "lstm_sb", "vector")
            fc_ps = stage_sem(sc, "fc_ps", "tensor")
            var_sb = stage_sem(sc, "var_sb", "vector")
            std_sb = stage_sem(sc, "std_sb", "scalar")
            h2_sb = stage_sem(sc, "h2_sb", "vector")
            h2T_ps = stage_sem(sc, "h2T_ps", "tensor")
            h2T_sb = stage_sem(sc, "h2T_sb", "scalar")
            xlr_ps = stage_sem(sc, "xlr_ps", "tensor")
            node_out = stage_sem(sc, "node_out", "vector")
            stored = dma_sem("stored")
            stored_steps = stage_sem(sc, "stored_steps", "sync")
            block = sc.enter_context(nc.Block())

            @block.sync
            def _(sp):
                start(sp, "sync")
                last_i = sp.value_load(n_pairs[0:1, 0:1], min_val=1, max_val=TABLE // 2 - 2)
                pairs = last_i + 1

                def load(i, s):
                    e0 = sp.value_load(table[0:1, bass.ds(i * 4 + 2 * s, 1)], min_val=0, max_val=N_EDGES)
                    v0 = sp.value_load(table[0:1, bass.ds(i * 4 + 2 * s + 1, 1)], min_val=0, max_val=N_NODES - TN)
                    sp.dma_start(attr[s][:, :], attrT[:, bass.ds(e0, STEP_E)]).then_inc(loaded[s], 16)
                    sp.dma_start(hin[s][:, :], h_rows[bass.ds(v0, TN), :]).then_inc(loaded[s], 16)
                    sp.dma_start(xin[s][:, :], x[bass.ds(v0, TN), :]).then_inc(loaded[s], 16)

                for s in range(2):
                    load(0, s)
                sp.sem_inc(stored_steps, 1)
                with sp.Fori(0, pairs) as i:
                    for s in range(2):
                        v0 = sp.value_load(table[0:1, bass.ds(i * 4 + 2 * s + 1, 1)], min_val=0, max_val=N_NODES - TN)
                        sp.wait_ge(node_out, i * 2 + s + 2)
                        sp.sem_inc(passed, 1)
                        sp.dma_start(xl_rows[bass.ds(v0, TN), :], xl[s][:, :]).then_inc(stored, 16)
                        sp.dma_start(node_rec[bass.ds(v0, TN), :], rec[s][:, :]).then_inc(stored, 16)
                        load(i + 1, s)
                        sp.wait_ge(stored, i * 64 + 32 * s + 32)
                        sp.sem_inc(passed, 1)
                        sp.sem_inc(stored_steps, 1)
                for s in range(2):
                    sp.wait_ge(loaded[s], pairs * 48 + 48)
                    sp.sem_inc(passed, 1)

            @block.gpsimd
            def _(pool):
                last_i = pool.value_load(n_pairs[0:1, 0:1], min_val=1, max_val=TABLE // 2 - 2)
                pairs = last_i + 1
                with pool.Fori(0, pairs) as i:
                    for s in range(2):
                        pool.wait_ge(idx_ready, i * 2 + s + 2)
                        pool.sem_inc(passed, 1)
                        for k in range(KT):
                            pool.indirect_dma_start(rows0[s][:, k, 0:D], None, h_rows,
                                                    bass.IndirectOffsetOnAxis(ap=idx[s][:, k:k + 1], axis=0)
                                                    ).then_inc(gathered[s], 16)

            @block.tensor
            def _(pe):
                start(pe, "tensor")
                last_i = pe.value_load(n_pairs[0:1, 0:1], min_val=1, max_val=TABLE // 2 - 2)
                pairs = last_i + 1
                with pe.Fori(0, pairs) as i:
                    for s in range(2):
                        pe.wait_ge(loaded[s], i * 48 + 48)
                        pe.wait_ge(attr_sb, i * 2 + 1)
                        pe.sem_inc(passed, 1)
                        for k in range(KT):
                            m = pe.transpose(bk[2 + s][:, ED * k:ED * k + ED], attr[s][:, 128 * k:128 * k + 128],
                                             ident[0:ED, 0:ED])
                        m.then_inc(attr_ps, 1)
                    for s in range(2):
                        pe.wait_ge(hot, i * 4 + 2 * s + 3)
                        pe.wait_ge(attr_sb, i * 2 + s + 2)
                        pe.wait_ge(gathered[s], i * (16 * KT) + 16 * KT)
                        for k in range(KT):
                            m = pe.matmul(bk[s][0:TN, 0:AW], onehot[s][:, k, :], rows0[s][:, k, :],
                                          start=(k == 0), stop=(k == KT - 1))
                        m.then_inc(agg_ps, 1)
                    for s in range(2):
                        pe.wait_ge(agg_sb, i * 8 + 4 * s + 5)
                        for c in range(2):
                            pe.transpose(bk[4 + s][:, TN * c:TN * c + TN], agg[s][:, 128 * c:128 * c + 128], ident[0:TN, 0:TN])
                            pe.transpose(bk[4 + s][:, TN * (2 + c):TN * (3 + c)], hin[s][:, 128 * c:128 * c + 128], ident[0:TN, 0:TN])
                        pe.transpose(bk[2 + s][0:ED, 384:384 + TN], mean[s][:, :], ident[0:TN, 0:TN]).then_inc(xT_ps, 1)
                    pe.wait_ge(xT_sb, i * 2 + 3)
                    for f in range(NJ):
                        if f >= 2:
                            pe.wait_ge(h1_sb, i * NJ + f)
                        for c in range(4):
                            m = pe.matmul(bk[6 + f % 2][:, 0:2 * TN], wrr[:, c, 128 * f:128 * f + 128], xT[:, c, :],
                                          start=(c == 0), stop=(c == 3))
                        m.then_inc(h1_ps, 1)
                    pe.wait_ge(h1_sb, i * NJ + NJ + 1)
                    for j in range(NJ):
                        if j >= 2:
                            pe.wait_ge(gate_to, i * NJ + j)
                        for g, to in enumerate((bk[4 + j % 2][:, 0:2 * TN], bk[4 + j % 2][:, 256:256 + 2 * TN],
                                                bk[6 + j % 2][:, 0:2 * TN])):
                            for f in range(NJ):
                                m = pe.matmul(to, wih[:, f, DH * g + 128 * j:DH * g + 128 * j + 128], h1T[:, f, :],
                                              start=(f == 0), stop=(f == NJ - 1))
                        m.then_inc(gate_ps, 1)
                    pe.wait_ge(lstm_sb, i * NJ + NJ + 1)
                    for s in range(2):
                        for j in range(NJ):
                            m = pe.matmul(bk[4 + s][0:TN, 0:D], lstmT[:, j, TN * s:TN * s + TN], wfc[:, j, :],
                                          start=(j == 0), stop=(j == NJ - 1))
                        m.then_inc(fc_ps, 1)
                    for s in range(2):
                        pe.wait_ge(h2_sb, i * 2 + s + 2)
                        for c in range(2):
                            m = pe.transpose(bk[6 + s][:, TN * c:TN * c + TN], h2[s][:, 128 * c:128 * c + 128], ident[0:TN, 0:TN])
                        m.then_inc(h2T_ps, 1)
                    for s in range(2):
                        pe.wait_ge(h2T_sb, i * 2 + s + 2)
                        for c in range(2):
                            pe.matmul(bk[4 + s][0:TN, 0:2 * D], h2T[s][:, c, :], wlr[:, c, :], start=(c == 0), stop=(c == 1))
                        pe.matmul(bk[6 + s][0:TN, 0:D], meanT[s][:, :], weT[:, :], start=True, stop=True).then_inc(xlr_ps, 1)

            @block.scalar
            def _(act):
                start(act, "scalar")
                last_i = act.value_load(n_pairs[0:1, 0:1], min_val=1, max_val=TABLE // 2 - 2)
                pairs = last_i + 1
                gi, gg, go, gt, gc = gate
                with act.Fori(0, pairs) as i:
                    for s in range(2):
                        act.wait_ge(attr_ps, i * 2 + s + 2)
                        act.wait_ge(agg_ps, i * 2 + 1)
                        act.activation(rows0[s][:, :, D:D + ED], bk[2 + s][:, 0:KT * ED].rearrange("p (k c) -> p k c", c=ED),
                                       ACT.Copy).then_inc(attr_sb, 1)
                    for s in range(2):
                        act.wait_ge(xT_ps, i * 2 + s + 2)
                        act.activation(meanT[s][:, :], bk[2 + s][0:ED, 384:384 + TN], ACT.Copy)
                        act.activation(xT[:, :, TN * s:TN * s + TN],
                                       bk[4 + s][:, 0:4 * TN].rearrange("p (c n) -> p c n", c=4), ACT.Copy).then_inc(xT_sb, 1)
                    for f in range(NJ):
                        act.wait_ge(h1_ps, i * NJ + f + 2)
                        act.activation(h1T[:, f, :], bk[6 + f % 2][:, 0:2 * TN], ACT.Relu, bias=brel[:, f:f + 1]).then_inc(h1_sb, 1)
                    for j in range(NJ):
                        b = j % 2
                        act.wait_ge(gate_ps, i * NJ + j + 2)
                        act.wait_ge(lstm_sb, i * NJ + max(j - 1, 0) + 1)
                        act.activation(gi[b][:, :], bk[4 + b][:, 0:2 * TN], ACT.Sigmoid, bias=bg[:, j:j + 1])
                        act.activation(gg[b][:, :], bk[4 + b][:, 256:256 + 2 * TN], ACT.Tanh, bias=bg[:, NJ + j:NJ + j + 1]).then_inc(gate_ig, 1)
                        act.activation(go[b][:, :], bk[6 + b][:, 0:2 * TN], ACT.Sigmoid, bias=bg[:, 2 * NJ + j:2 * NJ + j + 1])
                        act.wait_ge(cell, i * NJ + j + 2)
                        act.activation(gt[b][:, :], gc[b][:, :], ACT.Tanh).then_inc(gate_to, 1)
                    act.wait_ge(var_sb, i * 2 + 3)
                    for s in range(2):
                        ins = act.activation(stats[s][0:TN, 9:10], stats[s][0:TN, 8:9], ACT.Sqrt)
                    ins.then_inc(std_sb, 1)
                    for s in range(2):
                        act.wait_ge(h2T_ps, i * 2 + s + 2)
                        act.activation(h2T[s][:, :, :], bk[6 + s][:, 0:2 * TN].rearrange("p (c n) -> p c n", c=2), ACT.Copy).then_inc(h2T_sb, 1)

            @block.vector
            def _(v):
                start(v, "vector")
                last_i = v.value_load(n_pairs[0:1, 0:1], min_val=1, max_val=TABLE // 2 - 2)
                pairs = last_i + 1
                gi, gg, go, gt, gc = gate

                def indices(i, s):
                    v.tensor_copy(idx[s][:, :], idx_all[:, bass.ds(i * (4 * KT) + s * 2 * KT, KT)]).then_inc(idx_ready, 1)

                def one_hot(i, s):
                    v.wait_ge(hot, i * 4 + 2 * s + 1)
                    v.tensor_scalar(drel[:, :], idx_all[:, bass.ds(i * (4 * KT) + s * 2 * KT + KT, KT)],
                                    baseT[:, bass.ds(i * 2 + s, 1)], None, ALU.subtract).then_inc(hot, 1)
                    v.wait_ge(hot, i * 4 + 2 * s + 2)
                    v.tensor_tensor(onehot[s][:, :, :], iota_n[:, 0:TN].unsqueeze(1).broadcast_to([128, KT, TN]),
                                    drel[:, :].unsqueeze(2).broadcast_to([128, KT, TN]), ALU.is_equal).then_inc(hot, 1)

                for s in range(2):
                    indices(0, s)
                    v.memset(rows0[s][:, :, D + ED:AW], 1.0)
                v.memset(agg[1][:, :], 0.0)
                with v.Fori(0, pairs) as i:
                    for s in range(2):
                        v.wait_ge(agg_ps, i * 2 + 1)
                        one_hot(i, s)
                    for s in range(2):
                        v.wait_ge(agg_ps, i * 2 + s + 2)
                        v.wait_ge(xT_ps, i * 2 + 1)
                        v.wait_ge(agg_sb, i * 8 + 4 * s + 1)
                        v.scalar_tensor_tensor(out=agg[s][:, :], in0=agg[1 - s][:, :], scalar=keepT[0:TN, bass.ds(i * 2 + s, 1)],
                                               in1=bk[s][0:TN, 0:AW], op0=ALU.mult, op1=ALU.add).then_inc(agg_sb, 1)
                        v.wait_ge(agg_sb, i * 8 + 4 * s + 2)
                        v.wait_ge(gathered[s], i * (16 * KT) + 16 * KT)
                        indices(i + 1, s)
                        v.tensor_scalar(small[0:TN, 1:2], agg[s][:, AW - 1:AW], 1.0, None, ALU.max).then_inc(agg_sb, 1)
                        v.wait_ge(agg_sb, i * 8 + 4 * s + 3)
                        v.reciprocal(small[0:TN, 0:1], small[0:TN, 1:2]).then_inc(agg_sb, 1)
                        v.wait_ge(agg_sb, i * 8 + 4 * s + 4)
                        v.tensor_scalar(mean[s][:, :], agg[s][:, D:D + ED], small[0:TN, 0:1], None, ALU.mult).then_inc(agg_sb, 1)
                    for j in range(NJ):
                        b = j % 2
                        v.wait_ge(gate_ig, i * NJ + j + 2)
                        v.tensor_tensor(gc[b][:, :], gi[b][:, :], gg[b][:, :], ALU.mult).then_inc(cell, 1)
                        v.wait_ge(gate_to, i * NJ + j + 2)
                        v.tensor_tensor(lstmT[:, j, :], go[b][:, :], gt[b][:, :], ALU.mult).then_inc(lstm_sb, 1)
                    for s in range(2):
                        v.wait_ge(norm_v, i * 8 + 4 * s + 1)
                        v.wait_ge(fc_ps, i * 2 + s + 2)
                        v.tensor_tensor(x1[s][:, :], bk[4 + s][0:TN, 0:D], xin[s][:, :], ALU.add).then_inc(norm_v, 1)
                        v.wait_ge(norm_v, i * 8 + 4 * s + 2)
                        v.tensor_tensor(x1[s][:, :], x1[s][:, :], bfc[0:TN, :], ALU.add).then_inc(norm_v, 1)
                        v.wait_ge(norm_v, i * 8 + 4 * s + 3)
                        v.bn_stats(stats[s][0:TN, 0:6], x1[s][:, :]).then_inc(norm_v, 1)
                        v.wait_ge(norm_v, i * 8 + 4 * s + 4)
                        v.sem_inc(passed, 1)
                        v.bn_aggr(stats[s][0:TN, 6:8], stats[s][0:TN, 0:6]).then_inc(norm_v, 1)
                        v.wait_ge(norm_v, i * 8 + 4 * s + 5)
                        v.tensor_scalar(stats[s][0:TN, 8:9], stats[s][0:TN, 7:8], EPS, None, ALU.add).then_inc(var_sb, 1)
                    for s in range(2):
                        v.wait_ge(scale_v, i * 4 + 2 * s + 1)
                        v.wait_ge(std_sb, i + 2)
                        v.wait_ge(stored_steps, i * 2 + s + 1)
                        v.reciprocal(stats[s][0:TN, 10:11], stats[s][0:TN, 9:10]).then_inc(scale_v, 1)
                        v.wait_ge(scale_v, i * 4 + 2 * s + 2)
                        v.tensor_scalar(h2[s][:, :], x1[s][:, :], stats[s][0:TN, 6:7], stats[s][0:TN, 10:11], ALU.subtract, ALU.mult).then_inc(scale_v, 1)
                        v.wait_ge(scale_v, i * 4 + 2 * s + 3)
                        v.tensor_scalar(h2[s][:, :], h2[s][:, :], 0.0, None, ALU.max).then_inc(h2_sb, 1)
                        v.wait_ge(h2_sb, i * 2 + s + 2)
                        v.tensor_tensor(rec[s][:, D:2 * D], x1[s][:, :], h2[s][:, :], ALU.add)
                    for s in range(2):
                        v.wait_ge(node_v, i * 12 + 6 * s + 1)
                        v.wait_ge(xlr_ps, i * 2 + s + 2)
                        v.tensor_tensor(xl[s][:, :], bk[4 + s][0:TN, 0:D], blr[0:TN, 0:D], ALU.add).then_inc(node_v, 1)
                        v.tensor_tensor(rec[s][:, 0:D], bk[4 + s][0:TN, D:2 * D], blr[0:TN, D:2 * D], ALU.add).then_inc(node_v, 1)
                        v.wait_ge(node_v, i * 12 + 6 * s + 3)
                        v.tensor_tensor(ss[:, :], xl[s][:, :], rec[s][:, 0:D], ALU.add).then_inc(node_v, 1)
                        v.wait_ge(node_v, i * 12 + 6 * s + 4)
                        v.tensor_tensor(ss[:, :], bk[6 + s][0:TN, 0:D], ss[:, :], ALU.add).then_inc(node_v, 1)
                        v.wait_ge(node_v, i * 12 + 6 * s + 5)
                        v.scalar_tensor_tensor(out=sk[:, :], in0=ss[:, :], scalar=0.2, in1=ss[:, :], op0=ALU.mult, op1=ALU.max).then_inc(node_v, 1)
                        v.wait_ge(node_v, i * 12 + 6 * s + 6)
                        v.tensor_tensor(sk[:, :], sk[:, :], attb[0:TN, :], ALU.mult).then_inc(node_v, 1)
                        v.wait_ge(node_v, i * 12 + 6 * s + 7)
                        v.tensor_reduce(rec[s][:, 2 * D:RECW], sk[:, :].rearrange("p (h c) -> p h c", h=HEADS), AX.X, ALU.add).then_inc(node_out, 1)

        with ExitStack() as sc:
            def tmp(name, shape, dt=F32):
                return sc.enter_context(nc.sbuf_tensor(name, shape, dt))

            def dma_sem(name):
                return sc.enter_context(nc.semaphore(name))

            RW = 5 * KT
            dst85 = [tmp(f"dst85{s}", [RW, 128], I32) for s in range(2)]
            xr = [tmp(f"xr{s}", [TN, D]) for s in range(2)]
            xo = [tmp(f"xo{s}", [TN, D]) for s in range(2)]
            ro = [tmp(f"ro{s}", [TN, D + HEADS]) for s in range(2)]
            hotT = [tmp(f"hotT{s}", [TN, STEP_E]) for s in range(2)]
            relu8 = [tmp(f"relu8{b}", [128, 2, 512]) for b in range(2)]
            leaky = [tmp(f"leaky{b}", [128, 2, 512]) for b in range(2)]
            score = tmp("score", [128, 5, KT])
            begins = tmp("begins", [RW, 129])
            ends = tmp("ends", [RW, 128])
            runmax = tmp("runmax", [RW, 128])
            runT = tmp("runT", [128, 5, KT])
            pen = tmp("pen", [TN, KT])
            cand = tmp("cand", [TN, KT, HEADS])
            stepmax = tmp("stepmax", [TN, HEADS])
            prevmax = tmp("prevmax", [TN, HEADS])
            nmax = [tmp(f"nmax{s}", [TN, HEADS]) for s in range(2)]
            gap = tmp("gap", [TN, HEADS])
            corr = tmp("corr", [TN, HEADS])
            expo = tmp("expo", [128, HEADS, KT])
            ex = tmp("ex", [128, HEADS, KT])
            acc = [tmp(f"acc{s}", [TN, XW]) for s in range(2)]
            scaled = tmp("scaled", [TN, XW])
            selfm = tmp("selfm", [TN, HEADS])
            gap2 = tmp("gap2", [TN, 2, HEADS])
            c2 = tmp("c2", [TN, 2, HEADS])
            tot = tmp("tot", [TN, XW])
            own = tmp("own", [TN, D])
            rden = tmp("rden", [TN, HEADS])
            y = tmp("y", [TN, D])
            em = tmp("em", [TN, D])
            res = [tmp(f"res{s}", [TN, D]) for s in range(2)]

            silu_v = stage_sem(sc, "silu_v", "vector")
            loadedF = [dma_sem(f"loadedF{s}") for s in range(2)]
            loadedB = [dma_sem(f"loadedB{s}") for s in range(2)]
            gathered1 = [dma_sem(f"gathered1_{s}") for s in range(2)]
            idx_ready1 = stage_sem(sc, "idx_ready1", "vector")
            hot1 = stage_sem(sc, "hot1", "vector")
            hotT_ps = stage_sem(sc, "hotT_ps", "tensor")
            hotT_sb = stage_sem(sc, "hotT_sb", "scalar")
            s_ps = stage_sem(sc, "s_ps", "tensor")
            relu_sb = stage_sem(sc, "relu_sb", "scalar")
            leaky_sb = stage_sem(sc, "leaky_sb", "vector")
            score_ps = stage_sem(sc, "score_ps", "tensor")
            score_sb = stage_sem(sc, "score_sb", "vector")
            scoreT_ps = stage_sem(sc, "scoreT_ps", "tensor")
            runs = stage_sem(sc, "runs", "vector")
            runT_ps = stage_sem(sc, "runT_ps", "tensor")
            runT_sb = stage_sem(sc, "runT_sb", "vector")
            cand_ps = stage_sem(sc, "cand_ps", "tensor")
            maxs = stage_sem(sc, "maxs", "vector")
            corr_sb = stage_sem(sc, "corr_sb", "scalar")
            shift_ps = stage_sem(sc, "shift_ps", "tensor")
            expos = stage_sem(sc, "expos", "vector")
            ex_sb = stage_sem(sc, "ex_sb", "scalar")
            weighted = stage_sem(sc, "weighted", "vector")
            out_ps = stage_sem(sc, "out_ps", "tensor")
            fin1 = stage_sem(sc, "fin1", "vector")
            fin1_exp = stage_sem(sc, "fin1_exp", "scalar")
            res_ready = stage_sem(sc, "res_ready", "vector")
            stored1 = dma_sem("stored1")
            stored_steps1 = stage_sem(sc, "stored_steps1", "sync")
            block = sc.enter_context(nc.Block())

            S_PS = [[bk[0], bk[1]], [bk[2], bk[3]]]
            SCORE = bk[6][:, 0:HEADS * KT].rearrange("p (h k) -> p h k", h=HEADS)
            SHIFT = bk[7][:, 128:128 + HEADS * KT].rearrange("p (h k) -> p h k", h=HEADS)
            SCORET = bk[7][0:RW, 272:400]
            RUNT = bk[7][:, 400:400 + RW]
            OUT = bk[7][0:TN, 0:XW]
            CAND = bk[7][0:TN, 0:RW].rearrange("p (k h) -> p k h", k=KT)

            @block.sync
            def _(sp):
                start(sp, "sync")
                last_i = sp.value_load(n_pairs[0:1, 0:1], min_val=1, max_val=TABLE // 2 - 2)
                pairs = last_i + 1

                def load(i, s):
                    e0 = sp.value_load(table[0:1, bass.ds(i * 4 + 2 * s, 1)], min_val=0, max_val=N_EDGES)
                    v0 = sp.value_load(table[0:1, bass.ds(i * 4 + 2 * s + 1, 1)], min_val=0, max_val=N_NODES - TN)
                    sp.dma_start(attr[s][:, :], attrT[:, bass.ds(e0, STEP_E)]).then_inc(loadedF[s], 16)
                    for h in range(5):
                        sp.dma_start(dst85[s][KT * h:KT * h + KT, :], edge_rows(dst, e0)).then_inc(loadedF[s], 16)
                    sp.dma_start(xr[s][:, :], node_rec[bass.ds(v0, TN), 0:D]).then_inc(loadedF[s], 16)
                    sp.dma_start(ro[s][:, :], node_rec[bass.ds(v0, TN), D:RECW]).then_inc(loadedB[s], 16)
                    sp.dma_start(xo[s][:, :], xl_rows[bass.ds(v0, TN), :]).then_inc(loadedB[s], 16)

                for s in range(2):
                    load(0, s)
                sp.sem_inc(stored_steps1, 1)
                with sp.Fori(0, pairs) as i:
                    for s in range(2):
                        v0 = sp.value_load(table[0:1, bass.ds(i * 4 + 2 * s + 1, 1)], min_val=0, max_val=N_NODES - TN)
                        sp.wait_ge(res_ready, i * 2 + s + 2)
                        sp.sem_inc(passed, 1)
                        sp.dma_start(out[bass.ds(v0, TN), :], res[s][:, :]).then_inc(stored1, 16)
                        load(i + 1, s)
                        sp.wait_ge(stored1, i * 32 + 16 * s + 16)
                        sp.sem_inc(passed, 1)
                        sp.sem_inc(stored_steps1, 1)
                for s in range(2):
                    sp.wait_ge(loadedF[s], pairs * 112 + 112)
                    sp.sem_inc(passed, 1)
                    sp.wait_ge(loadedB[s], pairs * 32 + 32)
                    sp.sem_inc(passed, 1)

            @block.gpsimd
            def _(pool):
                last_i = pool.value_load(n_pairs[0:1, 0:1], min_val=1, max_val=TABLE // 2 - 2)
                pairs = last_i + 1
                with pool.Fori(0, pairs) as i:
                    for s in range(2):
                        pool.wait_ge(idx_ready1, i * 2 + s + 2)
                        pool.sem_inc(passed, 1)
                        for k in range(KT):
                            pool.indirect_dma_start(rows1[s][:, k, 0:D], None, xl_rows,
                                                    bass.IndirectOffsetOnAxis(ap=idx[s][:, k:k + 1], axis=0)
                                                    ).then_inc(gathered1[s], 16)

            def later(i, s):
                return s > 0 or not isinstance(i, int)

            def steps(eng, last_i, first, both, last):
                first()
                with eng.Fori(0, last_i) as i:
                    both((i, 0), (i, 1))
                    both((i, 1), (i + 1, 0))
                both((last_i, 0), (last_i, 1))
                last((last_i, 1))

            @block.tensor
            def _(pe):
                start(pe, "tensor")
                last_i = pe.value_load(n_pairs[0:1, 0:1], min_val=1, max_val=TABLE // 2 - 2)
                pairs = last_i + 1

                def turn_hot(i, s):
                    pe.wait_ge(hot1, i * 4 + 2 * s + 3)
                    for q, ks in enumerate(QS):
                        if q >= 2:
                            pe.wait_ge(hotT_sb, i * (2 * NQ) + s * NQ + q)
                        for n, k in enumerate(ks):
                            m = pe.transpose(bk[4 + q % 2][0:TN, 128 * n:128 * n + 128], onehot[s][:, k, :], ident[:, :])
                        m.then_inc(hotT_ps, 1)

                def sums(i, s, q):
                    ks = QS[q]
                    e0, n = 128 * ks[0], 128 * len(ks)
                    if q == 0:
                        pe.wait_ge(loadedF[s], i * 112 + 112)
                        pe.wait_ge(gathered1[s], i * (16 * KT) + 16 * KT)
                    pe.wait_ge(hotT_sb, i * (2 * NQ) + s * NQ + q + 2)
                    if q >= 2:
                        pe.wait_ge(leaky_sb, i * (2 * NQ) + s * NQ + q)
                    else:
                        pe.wait_ge(leaky_sb, i * (2 * NQ) + s * NQ + 1)
                    for c in range(2):
                        to = S_PS[q % 2][c]
                        for m, k in enumerate(ks):
                            pe.matmul(to[:, 128 * m:128 * m + 128],
                                      rows1[s][:, k, 128 * c:128 * c + 128],
                                      ident[:, :], is_transpose=True, start=(m == 0), stop=False, skip_group_check=True)
                        pe.matmul(to[:, 0:n], xr[s][:, 128 * c:128 * c + 128], hotT[s][:, e0:e0 + n], start=False, stop=False, skip_group_check=True)
                        m = pe.matmul(to[:, 0:n], weT[:, 128 * c:128 * c + 128], attr[s][:, e0:e0 + n], start=False, stop=True, skip_group_check=True)
                    m.then_inc(s_ps, 1)

                def scores(i, s, q):
                    pe.wait_ge(leaky_sb, i * (2 * NQ) + s * NQ + q + 2)
                    for n, k in enumerate(QS[q]):
                        for c in range(2):
                            m = pe.matmul(SCORE[:, :, k], leaky[q % 2][:, c, 128 * n:128 * n + 128], attc[:, c, :],
                                          start=(c == 0), stop=(c == 1))
                    m.then_inc(score_ps, 1)

                def turn_scores(i, s):
                    pe.wait_ge(score_sb, i * 2 + s + 2)
                    pe.transpose(SCORET, score[:, :, :], ident[:, :]).then_inc(scoreT_ps, 1)

                def turn_runs(i, s):
                    pe.wait_ge(runs, i * 14 + 7 * s + 8)
                    pe.transpose(RUNT, runmax[:, :], ident[0:RW, 0:RW]).then_inc(runT_ps, 1)

                def candidates(i, s):
                    pe.wait_ge(runT_sb, i * 2 + s + 2)
                    for k in range(KT):
                        m = pe.matmul(CAND[:, k, :], onehot[s][:, k, :], runT[:, :, k], start=True, stop=True)
                    m.then_inc(cand_ps, 1)

                def shifts(i, s):
                    pe.wait_ge(maxs, i * 14 + 7 * s + 8)
                    for k in range(KT):
                        m = pe.matmul(SHIFT[:, :, k], hotT[s][:, 128 * k:128 * k + 128], nmax[s][:, :], start=True, stop=True)
                    m.then_inc(shift_ps, 1)

                def outputs(i, s):
                    pe.wait_ge(weighted, i * 2 + s + 2)
                    for k in range(KT):
                        m = pe.matmul(OUT, onehot[s][:, k, :], rows1[s][:, k, :], start=(k == 0), stop=(k == KT - 1))
                    m.then_inc(out_ps, 1)

                def first():
                    turn_hot(0, 0)
                    sums(0, 0, 0)
                    for q in range(1, NQ):
                        sums(0, 0, q)
                        scores(0, 0, q - 1)
                    scores(0, 0, NQ - 1)

                def both(b, f):
                    turn_scores(*b)
                    turn_hot(*f)
                    turn_runs(*b)
                    sums(*f, 0)
                    candidates(*b)
                    sums(*f, 1)
                    scores(*f, 0)
                    shifts(*b)
                    for q in range(2, NQ):
                        sums(*f, q)
                        scores(*f, q - 1)
                    outputs(*b)
                    scores(*f, NQ - 1)

                def last(b):
                    for stage in (turn_scores, turn_runs, candidates, shifts, outputs):
                        stage(*b)

                steps(pe, last_i, first, both, last)

            @block.scalar
            def _(act):
                start(act, "scalar")
                last_i = act.value_load(n_pairs[0:1, 0:1], min_val=1, max_val=TABLE // 2 - 2)
                pairs = last_i + 1

                def turned(i, s):
                    if later(i, s):
                        act.wait_ge(shift_ps, i * 2 + s)
                    for q, ks in enumerate(QS):
                        n = 128 * len(ks)
                        act.wait_ge(hotT_ps, i * (2 * NQ) + s * NQ + q + 2)
                        act.activation(hotT[s][:, 128 * ks[0]:128 * ks[0] + n], bk[4 + q % 2][0:TN, 0:n], ACT.Copy).then_inc(hotT_sb, 1)

                def relu(i, s, q):
                    n = 128 * len(QS[q])
                    act.wait_ge(s_ps, i * (2 * NQ) + s * NQ + q + 2)
                    act.wait_ge(leaky_sb, i * (2 * NQ) + s * NQ + max(q - 1, 0) + 1)
                    act.activation(relu8[q % 2][:, 0, 0:n], S_PS[q % 2][0][:, 0:n], ACT.Relu, scale=0.8)
                    act.activation(relu8[q % 2][:, 1, 0:n], S_PS[q % 2][1][:, 0:n], ACT.Relu, scale=0.8).then_inc(relu_sb, 1)

                def correction(i, s):
                    act.wait_ge(maxs, i * 14 + 7 * s + 8)
                    act.wait_ge(fin1, i * 30 + 15 * s + 1)
                    act.activation(corr[:, :], gap[:, :], ACT.Exp).then_inc(corr_sb, 1)

                def weights(i, s):
                    act.wait_ge(expos, i * 4 + 2 * s + 3)
                    act.activation(ex[:, :, :], expo[:, :, :], ACT.Exp).then_inc(ex_sb, 1)

                def finals(i, s):
                    act.wait_ge(fin1, i * 30 + 15 * s + 6)
                    act.activation(c2[:, :, :], gap2[:, :, :], ACT.Exp).then_inc(fin1_exp, 1)
                    act.wait_ge(fin1, i * 30 + 15 * s + 16)
                    act.activation(em[:, :], y[:, :], ACT.Exp, scale=-1.0).then_inc(fin1_exp, 1)

                def first():
                    turned(0, 0)
                    for q in range(NQ):
                        relu(0, 0, q)

                def both(b, f):
                    turned(*f)
                    relu(*f, 0)
                    correction(*b)
                    relu(*f, 1)
                    weights(*b)
                    for q in range(2, NQ):
                        relu(*f, q)
                    finals(*b)

                def last(b):
                    for stage in (correction, weights, finals):
                        stage(*b)

                steps(act, last_i, first, both, last)

            @block.vector
            def _(v):
                start(v, "vector")
                last_i = v.value_load(n_pairs[0:1, 0:1], min_val=1, max_val=TABLE // 2 - 2)
                pairs = last_i + 1

                def indices(i, s):
                    v.tensor_copy(idx[s][:, :], idx_all[:, bass.ds(i * (4 * KT) + s * 2 * KT, KT)]).then_inc(idx_ready1, 1)

                def one_hot(i, s):
                    if later(i, s):
                        v.wait_ge(out_ps, i * 2 + s)
                    v.wait_ge(hot1, i * 4 + 2 * s + 1)
                    v.tensor_scalar(drel[:, :], idx_all[:, bass.ds(i * (4 * KT) + s * 2 * KT + KT, KT)],
                                    baseT[:, bass.ds(i * 2 + s, 1)], None, ALU.subtract).then_inc(hot1, 1)
                    v.wait_ge(hot1, i * 4 + 2 * s + 2)
                    v.tensor_tensor(onehot[s][:, :, :], iota_n[:, 0:TN].unsqueeze(1).broadcast_to([128, KT, TN]),
                                    drel[:, :].unsqueeze(2).broadcast_to([128, KT, TN]), ALU.is_equal).then_inc(hot1, 1)

                def leak(i, s, q):
                    n = 128 * len(QS[q])
                    v.wait_ge(relu_sb, i * (2 * NQ) + s * NQ + q + 2)
                    v.wait_ge(score_ps, i * (2 * NQ) + s * NQ + max(q - 1, 0) + 1)
                    for c in range(2):
                        ins = v.scalar_tensor_tensor(out=leaky[q % 2][:, c, 0:n], in0=S_PS[q % 2][c][:, 0:n], scalar=0.2,
                                                     in1=relu8[q % 2][:, c, 0:n], op0=ALU.mult, op1=ALU.add)
                    ins.then_inc(leaky_sb, 1)

                def take_scores(i, s):
                    v.wait_ge(score_ps, i * (2 * NQ) + s * NQ + NQ + 1)
                    v.tensor_copy(score[:, 0:HEADS, :], SCORE).then_inc(score_sb, 1)

                def run_maxima(i, s):
                    v.wait_ge(runs, i * 14 + 7 * s + 1)
                    v.tensor_tensor(begins[:, 1:128], dst85[s][:, 1:128], dst85[s][:, 0:127], ALU.not_equal).then_inc(runs, 1)
                    v.wait_ge(runs, i * 14 + 7 * s + 2)
                    v.tensor_copy(ends[:, :], begins[:, 1:129]).then_inc(runs, 1)
                    v.memset(begins[:, 0:1], 1.0).then_inc(runs, 1)
                    v.wait_ge(runs, i * 14 + 7 * s + 4)
                    v.tensor_scalar(begins[:, 0:128], begins[:, 0:128], -BIG, None, ALU.mult).then_inc(runs, 1)
                    v.wait_ge(runs, i * 14 + 7 * s + 5)
                    v.wait_ge(scoreT_ps, i * 2 + s + 2)
                    v.tensor_tensor_scan(runmax[:, :], begins[:, 0:128], SCORET, 0.0, ALU.add, ALU.max).then_inc(runs, 1)
                    v.wait_ge(runs, i * 14 + 7 * s + 6)
                    v.tensor_tensor(runmax[:, :], runmax[:, :], ends[:, :], ALU.mult).then_inc(runs, 1)
                    v.wait_ge(runs, i * 14 + 7 * s + 7)
                    v.memset(begins[:, 0:1], 1.0).then_inc(runs, 1)

                def take_runs(i, s):
                    v.wait_ge(runT_ps, i * 2 + s + 2)
                    v.tensor_copy(runT[:, :, :], RUNT.rearrange("p (h k) -> p h k", h=5)).then_inc(runT_sb, 1)

                def maxima(i, s):
                    v.wait_ge(maxs, i * 14 + 7 * s + 1)
                    keep = keepT[0:TN, bass.ds(i * 2 + s, 1)]
                    v.wait_ge(cand_ps, i * 2 + s + 2)
                    v.tensor_scalar(pen[:, :], CAND[:, :, HEADS], 1.0, BIG, ALU.subtract, ALU.mult).then_inc(maxs, 1)
                    v.tensor_scalar(prevmax[:, :], keep.broadcast_to([TN, HEADS]), 1.0, BIG, ALU.subtract, ALU.mult).then_inc(maxs, 1)
                    v.wait_ge(maxs, i * 14 + 7 * s + 3)
                    v.scalar_tensor_tensor(out=prevmax[:, :], in0=nmax[1 - s][:, :], scalar=keep, in1=prevmax[:, :],
                                           op0=ALU.mult, op1=ALU.add).then_inc(maxs, 1)
                    v.tensor_tensor(cand[:, :, :], CAND[:, :, 0:HEADS], pen[:, :].unsqueeze(2).broadcast_to([TN, KT, HEADS]), ALU.add).then_inc(maxs, 1)
                    v.wait_ge(maxs, i * 14 + 7 * s + 5)
                    v.tensor_reduce(stepmax[:, :], cand[:, :, :].rearrange("p k h -> p h k"), AX.X, ALU.max).then_inc(maxs, 1)
                    v.wait_ge(maxs, i * 14 + 7 * s + 6)
                    v.tensor_tensor(nmax[s][:, :], stepmax[:, :], prevmax[:, :], ALU.max).then_inc(maxs, 1)
                    v.wait_ge(maxs, i * 14 + 7 * s + 7)
                    v.wait_ge(corr_sb, i * 2 + s + 1)
                    v.tensor_tensor(gap[:, :], prevmax[:, :], nmax[s][:, :], ALU.subtract).then_inc(maxs, 1)
                    v.wait_ge(maxs, i * 14 + 7 * s + 8)

                def exponents(i, s):
                    v.wait_ge(expos, i * 4 + 2 * s + 1)
                    v.wait_ge(shift_ps, i * 2 + s + 2)
                    v.tensor_tensor(expo[:, :, :], score[:, 0:HEADS, :], SHIFT, ALU.subtract).then_inc(expos, 1)
                    v.wait_ge(expos, i * 4 + 2 * s + 2)
                    v.tensor_scalar(expo[:, :, :], expo[:, :, :], 0.0, None, ALU.min).then_inc(expos, 1)

                def weigh(i, s):
                    v.wait_ge(ex_sb, i * 2 + s + 2)
                    r = rows1[s][:, :, 0:D].rearrange("p k (h c) -> p k h c", h=HEADS)
                    by_tile = ex[:, :, :].rearrange("p h k -> p k h")
                    v.tensor_copy(rows1[s][:, :, D:XW], by_tile)
                    v.tensor_tensor(r, r, by_tile.unsqueeze(3).broadcast_to([128, KT, HEADS, HD]), ALU.mult).then_inc(weighted, 1)

                def finish(i, s):
                    v.wait_ge(fin1, i * 30 + 15 * s + 1)
                    keep = keepT[0:TN, bass.ds(i * 2 + s, 1)]

                    def wide(a):
                        return a.unsqueeze(2).broadcast_to([TN, HEADS, HD])

                    def by_head(a):
                        return a.rearrange("p (h c) -> p h c", h=HEADS)

                    v.wait_ge(loadedB[s], i * 32 + 32)
                    v.wait_ge(corr_sb, i * 2 + s + 2)
                    v.tensor_tensor(selfm[:, :], nmax[s][:, :], ro[s][:, D:D + HEADS], ALU.max).then_inc(fin1, 1)
                    v.scalar_tensor_tensor(out=by_head(scaled[:, 0:D]), in0=by_head(acc[1 - s][:, 0:D]), scalar=keep,
                                           in1=wide(corr[:, :]), op0=ALU.mult, op1=ALU.mult).then_inc(fin1, 1)
                    v.scalar_tensor_tensor(out=scaled[:, D:XW], in0=acc[1 - s][:, D:XW], scalar=keep,
                                           in1=corr[:, :], op0=ALU.mult, op1=ALU.mult).then_inc(fin1, 1)
                    v.wait_ge(fin1, i * 30 + 15 * s + 4)
                    v.tensor_tensor(gap2[:, 0, :], nmax[s][:, :], selfm[:, :], ALU.subtract).then_inc(fin1, 1)
                    v.tensor_tensor(gap2[:, 1, :], ro[s][:, D:D + HEADS], selfm[:, :], ALU.subtract).then_inc(fin1, 1)
                    v.wait_ge(out_ps, i * 2 + s + 2)
                    v.tensor_tensor(acc[s][:, :], scaled[:, :], OUT, ALU.add).then_inc(fin1, 1)
                    v.wait_ge(fin1, i * 30 + 15 * s + 7)
                    indices(i + 1, s)
                    v.wait_ge(fin1_exp, i * 4 + 2 * s + 2)
                    v.tensor_tensor(by_head(tot[:, 0:D]), by_head(acc[s][:, 0:D]), wide(c2[:, 0, :]), ALU.mult).then_inc(fin1, 1)
                    v.tensor_tensor(tot[:, D:XW], acc[s][:, D:XW], c2[:, 0, :], ALU.mult).then_inc(fin1, 1)
                    v.tensor_tensor(by_head(own[:, :]), by_head(xo[s][:, :]), wide(c2[:, 1, :]), ALU.mult).then_inc(fin1, 1)
                    v.wait_ge(fin1, i * 30 + 15 * s + 10)
                    v.tensor_tensor(tot[:, 0:D], tot[:, 0:D], own[:, :], ALU.add).then_inc(fin1, 1)
                    v.tensor_tensor(rden[:, :], tot[:, D:XW], c2[:, 1, :], ALU.add).then_inc(fin1, 1)
                    v.wait_ge(fin1, i * 30 + 15 * s + 12)
                    v.tensor_scalar(rden[:, :], rden[:, :], 1e-16, None, ALU.add).then_inc(fin1, 1)
                    v.wait_ge(fin1, i * 30 + 15 * s + 13)
                    v.reciprocal(rden[:, :], rden[:, :]).then_inc(fin1, 1)
                    v.wait_ge(fin1, i * 30 + 15 * s + 14)
                    v.tensor_tensor(by_head(y[:, :]), by_head(tot[:, 0:D]), wide(rden[:, :]), ALU.mult).then_inc(fin1, 1)
                    v.wait_ge(fin1, i * 30 + 15 * s + 15)
                    v.tensor_tensor(y[:, :], y[:, :], bout[0:TN, :], ALU.add).then_inc(fin1, 1)
                    v.wait_ge(silu_v, i * 6 + 3 * s + 1)
                    v.wait_ge(fin1_exp, i * 4 + 2 * s + 3)
                    v.tensor_scalar(em[:, :], em[:, :], 1.0, None, ALU.add).then_inc(silu_v, 1)
                    v.wait_ge(silu_v, i * 6 + 3 * s + 2)
                    v.reciprocal(em[:, :], em[:, :]).then_inc(silu_v, 1)
                    v.wait_ge(silu_v, i * 6 + 3 * s + 3)
                    v.tensor_tensor(em[:, :], em[:, :], y[:, :], ALU.mult).then_inc(silu_v, 1)
                    v.wait_ge(silu_v, i * 6 + 3 * s + 4)
                    v.wait_ge(stored_steps1, i * 2 + s + 1)
                    v.tensor_tensor(res[s][:, :], em[:, :], ro[s][:, 0:D], ALU.add).then_inc(res_ready, 1)

                def first():
                    for s in range(2):
                        indices(0, s)
                    v.memset(score[:, HEADS:, :], 1.0)
                    v.memset(begins[:, 0:1], 1.0)
                    v.memset(begins[:, 128:129], 1.0)
                    v.memset(nmax[1][:, :], 0.0)
                    v.memset(acc[1][:, :], 0.0)
                    one_hot(0, 0)
                    for q in range(NQ):
                        leak(0, 0, q)

                def both(b, f):
                    take_scores(*b)
                    one_hot(*f)
                    run_maxima(*b)
                    take_runs(*b)
                    leak(*f, 0)
                    maxima(*b)
                    leak(*f, 1)
                    exponents(*b)
                    leak(*f, 2)
                    weigh(*b)
                    for q in range(3, NQ):
                        leak(*f, q)
                    finish(*b)

                def last(b):
                    for stage in (take_scores, run_maxima, take_runs, maxima, exponents, weigh, finish):
                        stage(*b)

                steps(v, last_i, first, both, last)


def kernel(**inputs):
    import concourse.bacc as bacc
    from concourse.bass_utils import run_bass_kernel_spmd as run

    a = {k: np.asarray(v) for k, v in inputs.items()}
    order = np.r_[0:DH, 2 * DH:4 * DH]

    def columns(v, n):
        return np.ascontiguousarray(v.reshape(n, 128).T)

    arrays = {
        "x": a["x"],
        "src": np.pad(a["src"], (0, STEP_E)),
        "dst": np.pad(a["dst"], (0, STEP_E), constant_values=N_NODES),
        "attrT": np.ascontiguousarray(np.pad(a["edge_attr_16"], ((0, STEP_E), (0, 0))).T),
        "w_rr": np.concatenate([a["L0_gnn_W_rel"], a["L0_gnn_W_root"]]),
        "b_rel": columns(a["L0_gnn_b_rel"], NJ),
        "w_ihT": np.ascontiguousarray(a["L0_gnn_W_ih"][order].T),
        "b_ih": columns(a["L0_gnn_b_ih"][order], 3 * NJ),
        "b_hh": columns(a["L0_gnn_b_hh"][order], 3 * NJ),
        "w_fc": a["L0_gnn_W_fc"],
        "b_fc": a["L0_gnn_b_fc"],
        "w_lr": np.ascontiguousarray(np.concatenate([a["L1_gnn_W_l"].T, a["L1_gnn_W_r"].T], axis=1)),
        "b_l": a["L1_gnn_b_l"],
        "b_r": a["L1_gnn_b_r"],
        "w_eT": np.ascontiguousarray(a["L1_gnn_W_e"].T),
        "att": np.ascontiguousarray(a["L1_gnn_att"].reshape(-1)),
        "bias": a["L1_gnn_bias"],
    }
    nc = bacc.Bacc("TRN2", target_bir_lowering=False, num_devices=1)
    args = [nc.dram_tensor(k, v.shape, mybir.dt.from_np(v.dtype), kind="ExternalInput").ap() for k, v in arrays.items()]
    out = nc.dram_tensor("out", [N_NODES, D], F32, kind="ExternalOutput").ap()
    gnn_layers(nc, *args, out)
    return run(nc, [arrays], core_ids=[0]).results[0]["out"]
```

```python
from contextlib import ExitStack

import numpy as np
import concourse.bass as bass
from concourse import mybir

F32 = mybir.dt.float32
I32 = mybir.dt.int32
F32R = mybir.dt.float32r
ALU = mybir.AluOpType
ACT = mybir.ActivationFunctionType
AX = mybir.AxisListType

N_NODES, N_EDGES = 6250, 100000
D, DH = 256, 512
HEADS, HD = 4, 64
ED = 16
TN = 128 - ED
TILES = -(-N_NODES // TN)
LAST_BASE = N_NODES - TN
KT = 15
STEP_E = KT * 128
STEPS_MAX = TILES + -(-N_EDGES // STEP_E)
TABLE = 128
ROUNDS = -(-N_EDGES // STEP_E)
E_PAD = N_EDGES + STEP_E
XW = D + HEADS
AW = D + ED + 1
RECW = 2 * D + HEADS
NJ = DH // 128
BIG = 1.0e30
EPS = 1.0e-5
QS = [range(0, 4), range(4, 8), range(8, 12), range(12, 15)]
NQ = len(QS)
P5 = 125
LAST_MAX = -(-STEPS_MAX // 2) - 1
assert 2 * LAST_MAX + 6 <= TABLE and NQ == 4 and N_NODES % (5 * P5) == 0 and N_EDGES % P5 == 0


class Count:

    def __init__(self):
        self.n = 0

    def one_more(self):
        self.n += 1
        return self.n


def gnn_layers(nc, x, src, dst, attrT, w_rr, b_rel, w_ihT, b_ih, b_hh, w_fc, b_fc, w_lr, b_l, b_r, w_eT, att, bias, out):
    ctx = ExitStack()
    with ctx:
        def sb(name, shape, dt=F32):
            return ctx.enter_context(nc.sbuf_tensor(name, shape, dt))

        def sem(name):
            return ctx.enter_context(nc.semaphore(name))

        def stage_sem(scope, name, engine):
            q = scope.enter_context(nc.semaphore(name))
            to_start.append((engine, q))
            return q

        to_start = []

        def start(eng, engine):
            for of, q in list(to_start):
                if of == engine:
                    eng.sem_inc(q, 1)
                    to_start.remove((of, q))

        h_rows = nc.dram_tensor("h_rows", [N_NODES, D], F32).ap()
        xl_rows = nc.dram_tensor("xl_rows", [N_NODES, D], F32).ap()
        node_rec = nc.dram_tensor("node_rec", [N_NODES, RECW], F32).ap()
        step_list = nc.dram_tensor("step_list", [TABLE, 2], I32).ap()

        bk = [ctx.enter_context(nc.psum_tensor(f"bank{i}", [128, 512], F32)) for i in range(8)]

        weT = sb("weT", [ED, D])
        bout = sb("bout", [128, D])
        attc = sb("attc", [128, 2, HEADS])
        ident = sb("ident", [128, 128])
        ones = sb("ones", [128, 128])
        iota_n = sb("iota_n", [128, 128])
        iota_p = sb("iota_p", [128, 1])
        table = sb("table", [1, TABLE * 2], I32)
        n_pairs = sb("n_pairs", [1, 2], I32)
        baseT = sb("baseT", [128, TABLE])
        keepT = sb("keepT", [128, TABLE])
        idx_all = sb("idx_all", [128, TABLE * 2 * KT], I32)
        idx = [sb(f"idx{s}", [128, KT], I32) for s in range(2)]
        drel = sb("drel", [128, KT])
        eri = [sb(f"eri{s}", [64, 128], I32) for s in range(2)]
        erf = [sb(f"erf{s}", [64, 128]) for s in range(2)]
        rows = [sb(f"rows{s}", [128, KT * AW]) for s in range(2)]
        rows0 = [r[:, :].rearrange("p (k c) -> p k c", k=KT) for r in rows]
        rows1 = [r[:, 0:KT * D].rearrange("p (k c) -> p k c", k=KT) for r in rows]
        onehot = [sb(f"onehot{s}", [128, KT, TN]) for s in range(2)]
        attr = [sb(f"attr{s}", [ED, STEP_E]) for s in range(2)]
        small = sb("small", [128, 64])
        stats = [sb(f"stats{s}", [128, 12]) for s in range(2)]

        early = ctx.enter_context(ExitStack())

        def early_sb(name, shape):
            return early.enter_context(nc.sbuf_tensor(name, shape, F32))

        wrr = early_sb("wrr", [128, 4, DH])
        wih = early_sb("wih", [128, NJ, 3 * DH])
        wfc = early_sb("wfc", [128, NJ, D])
        wlr = early_sb("wlr", [128, 2, 2 * D])
        brel = early_sb("brel", [128, NJ])
        bg1 = early_sb("bg1", [128, 12])
        bg2 = early_sb("bg2", [128, 12])
        bg = early_sb("bg", [128, 12])
        bfc = early_sb("bfc", [128, D])
        blr = early_sb("blr", [128, 2 * D])
        attb = early_sb("attb", [128, D])

        setup_in = sem("setup_in")
        setup_c = sem("setup_c")
        dst_in = sem("dst_in")
        setup_t = sem("setup_t")
        counts_ps = sem("counts_ps")
        table_out = sem("table_out")
        table_in = sem("table_in")
        ln_in = [sem(f"ln_in{s}") for s in range(2)]
        ln_v = sem("ln_v")
        ln_var = sem("ln_var")
        ln_std = sem("ln_std")
        ln_out = [sem(f"ln_out{s}") for s in range(2)]
        setup_v = sem("setup_v")
        passed = sem("passed")
        er_in = [sem(f"er_in{s}") for s in range(2)]
        gathered = [sem(f"gathered{s}") for s in range(2)]

        with ExitStack() as sc:
            def tmp(name, shape, dt=F32):
                return sc.enter_context(nc.sbuf_tensor(name, shape, dt))
            dsti = tmp("dsti", [P5, N_EDGES // P5], I32)
            dstf = tmp("dstf", [P5, N_EDGES // P5])
            junk = tmp("junk", [P5, N_EDGES // P5])
            part = tmp("part", [128, TILES + 2])
            counted = tmp("counted", [128, TILES + 2])
            first = tmp("first", [128, TILES])
            cnt = tmp("cnt", [128, TILES])
            thr = tmp("thr", [128, ROUNDS])
            over = tmp("over", [128, TILES, ROUNDS])
            rnd = tmp("rnd", [128, TILES])
            cum = tmp("cum", [128, TILES])
            zero = tmp("zero", [128, TILES])
            cmp = tmp("cmp", [128, TILES])
            sel = tmp("sel", [128, TILES])
            col = tmp("col", [128, 12])
            step2 = tmp("step2", [128, 2], I32)
            diag = tmp("diag", [128, 2, 128])
            xt = [tmp(f"xt{s}", [P5, 5, D]) for s in range(2)]
            xh = [tmp(f"xh{s}", [P5, 5, D]) for s in range(2)]
            x5 = x.rearrange("(i p j) c -> i p (j c)", p=P5, j=5)
            h5 = h_rows.rearrange("(i p j) c -> i p (j c)", p=P5, j=5)
            LN_T = N_NODES // (5 * P5)

            block = sc.enter_context(nc.Block())

            @block.sync
            def _(sp):
                sp.dma_start(dsti[:, :], dst[0:N_EDGES].rearrange("(p c) -> p c", p=P5)).then_inc(dst_in, 16)
                for s in range(2):
                    sp.dma_start(xt[s][:, :, :].rearrange("p j c -> p (j c)"), x5[s]).then_inc(ln_in[s], 16)
                loads = [(wrr[:, :, :], w_rr.rearrange("(k p) n -> p k n", p=128)),
                         (wih[:, :, :], w_ihT.rearrange("(k p) n -> p k n", p=128)),
                         (wfc[:, :, :], w_fc.rearrange("(k p) n -> p k n", p=128)),
                         (wlr[:, :, :], w_lr.rearrange("(k p) n -> p k n", p=128)),
                         (weT[:, :], w_eT), (brel[:, :], b_rel), (bg1[:, :], b_ih), (bg2[:, :], b_hh),
                         (bfc[:, :], b_fc.partition_broadcast(128)), (blr[:, 0:D], b_l.partition_broadcast(128)),
                         (blr[:, D:2 * D], b_r.partition_broadcast(128)), (bout[:, :], bias.partition_broadcast(128)),
                         (attb[:, :], att.partition_broadcast(128))]
                for to, of in loads:
                    sp.dma_start(to, of).then_inc(setup_in, 16)
                sp.wait_ge(setup_c, 7)
                for h in range(HEADS):
                    sp.dma_start(attc[64 * (h % 2):64 * (h % 2) + 64, h // 2, h:h + 1],
                                 att[HD * h:HD * h + HD].rearrange("(c a) -> c a", a=1)).then_inc(setup_in, 16)
                for i in range(LN_T):
                    s = i % 2
                    sp.wait_ge(ln_v, i + 1)
                    sp.dma_start(h5[i], xh[s][:, :, :].rearrange("p j c -> p (j c)")).then_inc(ln_out[s], 16)
                    if i + 2 < LN_T:
                        sp.dma_start(xt[s][:, :, :].rearrange("p j c -> p (j c)"), x5[i + 2]).then_inc(ln_in[s], 16)
                sp.wait_ge(setup_t, 1)
                sp.dma_start(step_list, step2[:, :]).then_inc(table_out, 16)
                sp.wait_ge(table_out, 16)
                sp.dma_start(table[:, :], step_list.rearrange("(a n) c -> a (n c)", a=1)).then_inc(table_in, 16)
                sp.wait_ge(table_in, 16)
                sp.wait_ge(setup_in, 16 * 17)
                for s in range(2):
                    sp.wait_ge(ln_out[s], 16 * (LN_T // 2))

            @block.gpsimd
            def _(pool):
                pool.memset(small[:, :], 0.0).then_inc(setup_c, 1)
                pool.memset(ident[:, :], 0.0).then_inc(setup_c, 1)
                pool.memset(ones[:, :], 1.0).then_inc(setup_c, 1)
                pool.memset(idx_all[:, :], 0).then_inc(setup_c, 1)
                pool.memset(attc[:, :, :], 0.0).then_inc(setup_c, 1)
                pool.memset(eri[0][:, :], 0).then_inc(setup_c, 1)
                pool.memset(eri[1][:, :], 0).then_inc(setup_c, 1)
                pool.iota(iota_n[:, :], pattern=[[1, 128]], base=0, channel_multiplier=0,
                          allow_small_or_imprecise_dtypes=True).then_inc(setup_c, 1)
                pool.iota(iota_p[:, :], pattern=[[0, 1]], base=0, channel_multiplier=1,
                          allow_small_or_imprecise_dtypes=True).then_inc(setup_c, 1)
                pool.iota(thr[:, :], pattern=[[STEP_E, ROUNDS]], base=STEP_E, channel_multiplier=0,
                          allow_small_or_imprecise_dtypes=True).then_inc(setup_c, 1)
                pool.wait_ge(setup_c, 10)
                pool.affine_select(out=ident[:, :], in_=ident[:, :], compare_op=ALU.not_equal, fill=1.0,
                                   base=0, pattern=[[-1, 128]], channel_multiplier=1).then_inc(setup_c, 1)

            @block.tensor
            def _(pe):
                pe.wait_ge(setup_c, 11)
                pe.wait_ge(counts_ps, 1)
                pe.matmul(bk[0][:, 0:TILES + 2], ones[0:P5, :], part[0:P5, :], start=True, stop=True).then_inc(counts_ps, 1)
                pe.wait_ge(counts_ps, 3)
                pe.matmul(bk[1][:, 0:256], ones[:, :], diag[:, :, :], start=True, stop=True).then_inc(counts_ps, 1)

            @block.vector
            def _(v):
                signals = Count()

                v.wait_ge(dst_in, 16)
                v.wait_ge(setup_c, 11)
                v.tensor_copy(dstf[:, :], dsti[:, :]).then_inc(setup_v, 1)
                v.wait_ge(setup_v, signals.one_more())
                v.memset(part[:, 0:1], 0.0)
                for t in range(1, TILES):
                    v.tensor_scalar(junk[:, :], dstf[:, :], float(TN * t), 0.0, ALU.is_lt, ALU.add,
                                    accum_out=part[0:P5, t:t + 1]).then_inc(setup_v, 1)
                    v.wait_ge(setup_v, signals.one_more())
                v.tensor_scalar(junk[:, :], dstf[:, :], float(LAST_BASE), 0.0, ALU.is_lt, ALU.add,
                                accum_out=part[0:P5, TILES:TILES + 1]).then_inc(setup_v, 1)
                v.wait_ge(setup_v, signals.one_more())
                v.memset(part[0:P5, TILES + 1:TILES + 2], float(N_EDGES // P5)).then_inc(counts_ps, 1)
                for i in range(LN_T):
                    s = i % 2
                    v.wait_ge(ln_in[s], 16 * (i // 2 + 1))
                    if i >= 2:
                        v.wait_ge(ln_out[s], 16 * (i // 2))
                    for j in range(5):
                        ins = v.bn_stats(small[0:P5, 6 * j:6 * j + 6], xt[s][:, j, :])
                    ins.then_inc(setup_v, 1)
                    v.wait_ge(setup_v, signals.one_more())
                    for j in range(5):
                        ins = v.bn_aggr(small[0:P5, 32 + 2 * j:34 + 2 * j], small[0:P5, 6 * j:6 * j + 6])
                    ins.then_inc(setup_v, 1)
                    v.wait_ge(setup_v, signals.one_more())
                    mv = small[0:P5, 32:42].rearrange("p (j a) -> p j a", a=2)
                    v.tensor_scalar(small[0:P5, 48:53], mv[:, :, 1], EPS, None, ALU.add).then_inc(ln_var, 1)
                    v.wait_ge(ln_std, i + 1)
                    v.reciprocal(small[0:P5, 56:61], small[0:P5, 42:47]).then_inc(setup_v, 1)
                    v.wait_ge(setup_v, signals.one_more())
                    for j in range(5):
                        ins = v.tensor_scalar(xh[s][:, j, :], xt[s][:, j, :], small[0:P5, 32 + 2 * j:33 + 2 * j],
                                              small[0:P5, 56 + j:57 + j], ALU.subtract, ALU.mult)
                    ins.then_inc(setup_v, 1)
                    v.wait_ge(setup_v, signals.one_more())
                    v.tensor_scalar(xh[s][:, :, :], xh[s][:, :, :], 0.0, None, ALU.max).then_inc(ln_v, 1)
                v.wait_ge(counts_ps, 2)
                v.tensor_copy(counted[:, :], bk[0][:, 0:TILES + 2]).then_inc(setup_v, 1)
                v.wait_ge(setup_v, signals.one_more())
                v.tensor_copy(first[:, 0:TILES - 1], counted[:, 0:TILES - 1]).then_inc(setup_v, 1)
                v.wait_ge(setup_v, signals.one_more())
                v.tensor_copy(first[:, TILES - 1:TILES], counted[:, TILES:TILES + 1]).then_inc(setup_v, 1)
                v.wait_ge(setup_v, signals.one_more())
                v.tensor_tensor(cnt[:, 0:TILES - 1], counted[:, 1:TILES], first[:, 0:TILES - 1], ALU.subtract).then_inc(setup_v, 1)
                v.wait_ge(setup_v, signals.one_more())
                v.tensor_tensor(cnt[:, TILES - 1:TILES], counted[:, TILES + 1:TILES + 2], first[:, TILES - 1:TILES], ALU.subtract).then_inc(setup_v, 1)
                v.wait_ge(setup_v, signals.one_more())
                v.tensor_tensor(over[:, :, :], cnt[:, :].unsqueeze(2).broadcast_to([128, TILES, ROUNDS]),
                                thr[:, :].unsqueeze(1).broadcast_to([128, TILES, ROUNDS]), ALU.is_gt).then_inc(setup_v, 1)
                v.wait_ge(setup_v, signals.one_more())
                v.tensor_reduce(rnd[:, :], over[:, :, :], AX.X, ALU.add).then_inc(setup_v, 1)
                v.wait_ge(setup_v, signals.one_more())
                v.tensor_scalar(rnd[:, :], rnd[:, :], 1.0, None, ALU.add).then_inc(setup_v, 1)
                v.wait_ge(setup_v, signals.one_more())
                v.memset(zero[:, :], 0.0).then_inc(setup_v, 1)
                v.wait_ge(setup_v, signals.one_more())
                v.tensor_tensor_scan(cum[:, :], rnd[:, :], zero[:, :], 0.0, ALU.add, ALU.add).then_inc(setup_v, 1)
                v.wait_ge(setup_v, signals.one_more())
                v.tensor_scalar(cmp[:, :], cum[:, :], iota_p[:, 0:1], None, ALU.is_le).then_inc(setup_v, 1)
                v.wait_ge(setup_v, signals.one_more())
                v.tensor_reduce(col[:, 0:1], cmp[:, :], AX.X, ALU.add).then_inc(setup_v, 1)
                v.wait_ge(setup_v, signals.one_more())
                v.tensor_scalar(col[:, 1:2], col[:, 0:1], float(TILES - 1), None, ALU.min).then_inc(setup_v, 1)
                v.wait_ge(setup_v, signals.one_more())
                v.tensor_scalar(sel[:, :], iota_n[:, 0:TILES], col[:, 1:2], None, ALU.is_equal).then_inc(setup_v, 1)
                v.wait_ge(setup_v, signals.one_more())
                v.tensor_tensor(cmp[:, :], cum[:, :], rnd[:, :], ALU.subtract).then_inc(setup_v, 1)
                v.wait_ge(setup_v, signals.one_more())
                v.tensor_tensor(cmp[:, :], cmp[:, :], sel[:, :], ALU.mult).then_inc(setup_v, 1)
                v.wait_ge(setup_v, signals.one_more())
                v.tensor_reduce(col[:, 2:3], cmp[:, :], AX.X, ALU.add).then_inc(setup_v, 1)
                v.wait_ge(setup_v, signals.one_more())
                v.tensor_tensor(sel[:, :], sel[:, :], first[:, 0:TILES], ALU.mult).then_inc(setup_v, 1)
                v.wait_ge(setup_v, signals.one_more())
                v.tensor_reduce(col[:, 3:4], sel[:, :], AX.X, ALU.add).then_inc(setup_v, 1)
                v.wait_ge(setup_v, signals.one_more())
                v.tensor_tensor(col[:, 4:5], iota_p[:, 0:1], col[:, 2:3], ALU.subtract).then_inc(setup_v, 1)
                v.wait_ge(setup_v, signals.one_more())
                v.tensor_scalar(col[:, 5:6], col[:, 4:5], 0.0, None, ALU.is_gt).then_inc(setup_v, 1)
                v.wait_ge(setup_v, signals.one_more())
                v.tensor_scalar(col[:, 6:7], col[:, 4:5], float(STEP_E), None, ALU.mult).then_inc(setup_v, 1)
                v.wait_ge(setup_v, signals.one_more())
                v.tensor_tensor(col[:, 6:7], col[:, 6:7], col[:, 3:4], ALU.add).then_inc(setup_v, 1)
                v.wait_ge(setup_v, signals.one_more())
                v.tensor_scalar(col[:, 6:7], col[:, 6:7], float(N_EDGES), None, ALU.min).then_inc(setup_v, 1)
                v.wait_ge(setup_v, signals.one_more())
                v.tensor_scalar(col[:, 7:8], col[:, 1:2], float(TN), None, ALU.mult).then_inc(setup_v, 1)
                v.wait_ge(setup_v, signals.one_more())
                v.tensor_scalar(col[:, 7:8], col[:, 7:8], float(LAST_BASE), None, ALU.min).then_inc(setup_v, 1)
                v.wait_ge(setup_v, signals.one_more())
                v.tensor_copy(step2[:, :], col[:, 6:8]).then_inc(setup_v, 1)
                v.wait_ge(setup_v, signals.one_more())
                v.tensor_scalar(diag[:, 0, :], ident[:, :], col[:, 7:8], None, ALU.mult).then_inc(setup_v, 1)
                v.wait_ge(setup_v, signals.one_more())
                v.tensor_scalar(diag[:, 1, :], ident[:, :], col[:, 5:6], None, ALU.mult).then_inc(counts_ps, 1)
                v.tensor_scalar(junk[0:1, 0:64], iota_n[0:1, 0:64], 2.0, None, ALU.mult).then_inc(setup_v, 1)
                v.wait_ge(setup_v, signals.one_more())
                v.tensor_scalar(junk[0:1, 0:64], junk[0:1, 0:64], cum[0:1, TILES - 1:TILES], None, ALU.is_lt).then_inc(setup_v, 1)
                v.wait_ge(setup_v, signals.one_more())
                v.tensor_reduce(col[0:1, 8:9], junk[0:1, 0:64], AX.X, ALU.add).then_inc(setup_v, 1)
                v.wait_ge(setup_v, signals.one_more())
                v.tensor_scalar(n_pairs[:, 0:1], col[0:1, 8:9], -1.0, None, ALU.add).then_inc(setup_t, 1)
                v.wait_ge(counts_ps, 4)
                v.tensor_copy(baseT[:, :], bk[1][:, 0:128])
                v.tensor_copy(keepT[:, :], bk[1][:, 128:256])
                v.wait_ge(setup_in, 16 * 17)
                v.tensor_tensor(bg[:, :], bg1[:, :], bg2[:, :], ALU.add).then_inc(setup_t, 1)

            @block.scalar
            def _(act):
                for i in range(LN_T):
                    act.wait_ge(ln_var, i + 1)
                    act.activation(small[0:P5, 42:47], small[0:P5, 48:53], ACT.Sqrt).then_inc(ln_std, 1)

        er_v = stage_sem(ctx, "er_v", "vector")
        er_ps = stage_sem(ctx, "er_ps", "tensor")
        with nc.Block() as block:
            def edge_rows(table_of, first_edge):
                return table_of.rearrange("(a n) -> a n", a=1)[:, bass.ds(first_edge, STEP_E)].rearrange(
                    "a (k e) -> (a k) e", e=128)

            @block.sync
            def _(sp):
                start(sp, "sync")
                last_i = sp.value_load(n_pairs[0:1, 0:1], min_val=1, max_val=LAST_MAX)
                pairs = last_i + 1
                with sp.Fori(0, pairs) as i:
                    for s in range(2):
                        e0 = sp.value_load(table[0:1, bass.ds(i * 4 + 2 * s, 1)], min_val=0, max_val=N_EDGES)
                        sp.wait_ge(er_v, i * 4 + 1)
                        sp.sem_inc(passed, 1)
                        sp.dma_start(eri[s][0:KT, :], edge_rows(src, e0)).then_inc(er_in[s], 16)
                        sp.dma_start(eri[s][32:32 + KT, :], edge_rows(dst, e0)).then_inc(er_in[s], 16)

            @block.vector
            def _(v):
                start(v, "vector")
                last_i = v.value_load(n_pairs[0:1, 0:1], min_val=1, max_val=LAST_MAX)
                pairs = last_i + 1
                with v.Fori(0, pairs) as i:
                    for s in range(2):
                        v.wait_ge(er_v, i * 4 + 2 * s + 1)
                        v.wait_ge(er_in[s], i * 32 + 32)
                        v.tensor_copy(erf[s][:, :], eri[s][:, :]).then_inc(er_v, 1)
                        v.wait_ge(er_ps, i * 2 + s + 2)
                        v.tensor_copy(
                   idx_all[:, bass.ds(i * (4 * KT) + s * 2 * KT, 2 * KT)].rearrange("p (a k) -> p a k", a=2),
                   bk[s][:, 0:64].rearrange("p (a k) -> p a k", a=2)[:, :, 0:KT]).then_inc(er_v, 1)

            @block.tensor
            def _(pe):
                start(pe, "tensor")
                last_i = pe.value_load(n_pairs[0:1, 0:1], min_val=1, max_val=LAST_MAX)
                pairs = last_i + 1
                with pe.Fori(0, pairs) as i:
                    for s in range(2):
                        pe.wait_ge(er_v, i * 4 + 2 * s + 2)
                        pe.sem_inc(passed, 1)
                        pe.transpose(bk[s][:, 0:64], erf[s][:, :], ident[0:64, 0:64]).then_inc(er_ps, 1)

        with ExitStack() as sc:
            def tmp(name, shape, dt=F32):
                return sc.enter_context(nc.sbuf_tensor(name, shape, dt))

            def dma_sem(name):
                return sc.enter_context(nc.semaphore(name))

            hin = [tmp(f"hin{s}", [TN, D]) for s in range(2)]
            xin = [tmp(f"xin{s}", [TN, D]) for s in range(2)]
            agg = [tmp(f"agg{s}", [TN, AW]) for s in range(2)]
            mean = [tmp(f"mean{s}", [TN, ED]) for s in range(2)]
            meanT = [tmp(f"meanT{s}", [ED, TN]) for s in range(2)]
            xT = tmp("xT", [128, 4, 2 * TN])
            h1T = tmp("h1T", [128, NJ, 2 * TN])
            gate = [[tmp(f"gate{g}{b}", [128, 2 * TN]) for b in range(2)] for g in "igotc"]
            lstmT = tmp("lstmT", [128, NJ, 2 * TN])
            x1 = [tmp(f"x1{s}", [TN, D]) for s in range(2)]
            h2 = [tmp(f"h2{s}", [TN, D]) for s in range(2)]
            h2T = [tmp(f"h2T{s}", [128, 2, TN]) for s in range(2)]
            xl = [tmp(f"xl{s}", [TN, D]) for s in range(2)]
            rec = [tmp(f"rec{s}", [TN, RECW]) for s in range(2)]
            ss = tmp("ss", [TN, D])
            sk = tmp("sk", [TN, D])

            idx_ready = stage_sem(sc, "idx_ready", "vector")
            norm_v = stage_sem(sc, "norm_v", "vector")
            scale_v = stage_sem(sc, "scale_v", "vector")
            node_v = stage_sem(sc, "node_v", "vector")
            loaded = [dma_sem(f"loaded{s}") for s in range(2)]
            x_loaded = [dma_sem(f"x_loaded{s}") for s in range(2)]
            attr_ps = stage_sem(sc, "attr_ps", "tensor")
            attr_sb = stage_sem(sc, "attr_sb", "scalar")
            hot = stage_sem(sc, "hot", "vector")
            agg_ps = stage_sem(sc, "agg_ps", "tensor")
            agg_sb = stage_sem(sc, "agg_sb", "vector")
            xT_ps = stage_sem(sc, "xT_ps", "tensor")
            xT_sb = stage_sem(sc, "xT_sb", "scalar")
            h1_ps = stage_sem(sc, "h1_ps", "tensor")
            h1_sb = stage_sem(sc, "h1_sb", "scalar")
            gate_ps = stage_sem(sc, "gate_ps", "tensor")
            gate_ig = stage_sem(sc, "gate_ig", "scalar")
            gate_to = stage_sem(sc, "gate_to", "scalar")
            cell = stage_sem(sc, "cell", "vector")
            lstm_sb = stage_sem(sc, "lstm_sb", "vector")
            fc_ps = stage_sem(sc, "fc_ps", "tensor")
            var_sb = stage_sem(sc, "var_sb", "vector")
            std_sb = stage_sem(sc, "std_sb", "scalar")
            h2_sb = stage_sem(sc, "h2_sb", "vector")
            h2T_ps = stage_sem(sc, "h2T_ps", "tensor")
            h2T_sb = stage_sem(sc, "h2T_sb", "scalar")
            xlr_ps = stage_sem(sc, "xlr_ps", "tensor")
            node_out = stage_sem(sc, "node_out", "vector")
            stored = dma_sem("stored")
            stored_steps = stage_sem(sc, "stored_steps", "sync")
            block = sc.enter_context(nc.Block())

            @block.sync
            def _(sp):
                start(sp, "sync")
                last_i = sp.value_load(n_pairs[0:1, 0:1], min_val=1, max_val=LAST_MAX)
                pairs = last_i + 1

                def load(i, s):
                    e0 = sp.value_load(table[0:1, bass.ds(i * 4 + 2 * s, 1)], min_val=0, max_val=N_EDGES)
                    v0 = sp.value_load(table[0:1, bass.ds(i * 4 + 2 * s + 1, 1)], min_val=0, max_val=LAST_BASE)
                    sp.dma_start(attr[s][:, :], attrT[:, bass.ds(e0, STEP_E)]).then_inc(loaded[s], 16)
                    sp.dma_start(hin[s][:, :], h_rows[bass.ds(v0, TN), :]).then_inc(loaded[s], 16)

                def load_x(i, s):
                    v0 = sp.value_load(table[0:1, bass.ds(i * 4 + 2 * s + 1, 1)], min_val=0, max_val=LAST_BASE)
                    sp.dma_start(xin[s][:, :], x[bass.ds(v0, TN), :]).then_inc(x_loaded[s], 16)

                for s in range(2):
                    load(0, s)
                    load_x(0, s)
                sp.sem_inc(stored_steps, 1)
                with sp.Fori(0, pairs) as i:
                    for s in range(2):
                        sp.wait_ge(xT_ps, i * 2 + s + 2)
                        sp.sem_inc(passed, 1)
                        load(i + 1, s)
                    for s in range(2):
                        v0 = sp.value_load(table[0:1, bass.ds(i * 4 + 2 * s + 1, 1)], min_val=0, max_val=LAST_BASE)
                        sp.wait_ge(node_out, i * 2 + s + 2)
                        sp.sem_inc(passed, 1)
                        sp.dma_start(xl_rows[bass.ds(v0, TN), :], xl[s][:, :]).then_inc(stored, 16)
                        sp.dma_start(node_rec[bass.ds(v0, TN), :], rec[s][:, :]).then_inc(stored, 16)
                        load_x(i + 1, s)
                        sp.wait_ge(stored, i * 64 + 32 * s + 32)
                        sp.sem_inc(passed, 1)
                        sp.sem_inc(stored_steps, 1)
                for s in range(2):
                    sp.wait_ge(loaded[s], pairs * 32 + 32)
                    sp.sem_inc(passed, 1)
                    sp.wait_ge(x_loaded[s], pairs * 16 + 16)
                    sp.sem_inc(passed, 1)

            @block.gpsimd
            def _(pool):
                last_i = pool.value_load(n_pairs[0:1, 0:1], min_val=1, max_val=LAST_MAX)
                pairs = last_i + 1
                with pool.Fori(0, pairs) as i:
                    for s in range(2):
                        pool.wait_ge(idx_ready, i * 2 + s + 2)
                        pool.sem_inc(passed, 1)
                        for k in range(KT):
                            pool.indirect_dma_start(rows0[s][:, k, 0:D], None, h_rows,
                                                    bass.IndirectOffsetOnAxis(ap=idx[s][:, k:k + 1], axis=0)
                                                    ).then_inc(gathered[s], 16)

            def pairs_of_steps(eng, last_i, first, body):
                first(0)
                with eng.Fori(0, last_i) as i:
                    body(i, i + 1)
                body(last_i, None)

            @block.tensor
            def _(pe):
                start(pe, "tensor")
                last_i = pe.value_load(n_pairs[0:1, 0:1], min_val=1, max_val=LAST_MAX)

                def turn_attr(i, s):
                    pe.wait_ge(loaded[s], i * 32 + 32)
                    pe.wait_ge(attr_sb, i * 2 + 1)
                    pe.sem_inc(passed, 1)
                    for k in range(KT):
                        m = pe.transpose(bk[2 + s][:, ED * k:ED * k + ED], attr[s][:, 128 * k:128 * k + 128],
                                         ident[0:ED, 0:ED])
                    m.then_inc(attr_ps, 1)

                def sum_edges(i, s):
                    pe.wait_ge(hot, i * 4 + 2 * s + 3)
                    pe.wait_ge(attr_sb, i * 2 + s + 2)
                    pe.wait_ge(gathered[s], i * (16 * KT) + 16 * KT)
                    for k in range(KT):
                        m = pe.matmul(bk[s][0:TN, 0:AW], onehot[s][:, k, :], rows0[s][:, k, :],
                                      start=(k == 0), stop=(k == KT - 1))
                    m.then_inc(agg_ps, 1)

                def turn_x(i, s):
                    pe.wait_ge(agg_sb, i * 8 + 4 * s + 5)
                    for c in range(2):
                        pe.transpose(bk[s][:, TN * c:TN * c + TN], agg[s][:, 128 * c:128 * c + 128], ident[0:TN, 0:TN])
                        pe.transpose(bk[s][:, TN * (2 + c):TN * (3 + c)], hin[s][:, 128 * c:128 * c + 128], ident[0:TN, 0:TN])
                    pe.transpose(bk[2 + s][0:ED, 384:384 + TN], mean[s][:, :], ident[0:TN, 0:TN]).then_inc(xT_ps, 1)

                def hidden(i):
                    pe.wait_ge(xT_sb, i * 2 + 3)
                    pe.wait_ge(node_v, i * 12 + 1)
                    for f in range(NJ):
                        if f >= 2:
                            pe.wait_ge(h1_sb, i * NJ + f)
                        for c in range(4):
                            m = pe.matmul(bk[6 + f % 2][:, 0:2 * TN], wrr[:, c, 128 * f:128 * f + 128], xT[:, c, :],
                                          start=(c == 0), stop=(c == 3))
                        m.then_inc(h1_ps, 1)

                def gates(i):
                    pe.wait_ge(h1_sb, i * NJ + NJ + 1)
                    for j in range(NJ):
                        if j >= 2:
                            pe.wait_ge(gate_to, i * NJ + j)
                        for g, to in enumerate((bk[4 + j % 2][:, 0:2 * TN], bk[4 + j % 2][:, 256:256 + 2 * TN],
                                                bk[6 + j % 2][:, 0:2 * TN])):
                            for f in range(NJ):
                                m = pe.matmul(to, wih[:, f, DH * g + 128 * j:DH * g + 128 * j + 128], h1T[:, f, :],
                                              start=(f == 0), stop=(f == NJ - 1))
                        m.then_inc(gate_ps, 1)

                def output(i, s):
                    pe.wait_ge(lstm_sb, i * NJ + NJ + 1)
                    for j in range(NJ):
                        m = pe.matmul(bk[4 + s][0:TN, 0:D], lstmT[:, j, TN * s:TN * s + TN], wfc[:, j, :],
                                      start=(j == 0), stop=(j == NJ - 1))
                    m.then_inc(fc_ps, 1)

                def turn_h2(i, s):
                    pe.wait_ge(h2_sb, i * 2 + s + 2)
                    for c in range(2):
                        m = pe.transpose(bk[6 + s][:, TN * c:TN * c + TN], h2[s][:, 128 * c:128 * c + 128], ident[0:TN, 0:TN])
                    m.then_inc(h2T_ps, 1)

                def project(i, s):
                    pe.wait_ge(h2T_sb, i * 2 + s + 2)
                    for c in range(2):
                        pe.matmul(bk[4 + s][0:TN, 0:2 * D], h2T[s][:, c, :], wlr[:, c, :], start=(c == 0), stop=(c == 1))
                    pe.matmul(bk[6 + s][0:TN, 0:D], meanT[s][:, :], weT[:, :], start=True, stop=True).then_inc(xlr_ps, 1)

                def first(i):
                    for stage in (turn_attr, sum_edges, turn_x):
                        for s in range(2):
                            stage(i, s)

                def body(i, n):
                    hidden(i)
                    if n is not None:
                        for s in range(2):
                            turn_attr(n, s)
                    gates(i)
                    for s in range(2):
                        output(i, s)
                    if n is not None:
                        sum_edges(n, 0)
                    for s in range(2):
                        turn_h2(i, s)
                    if n is not None:
                        sum_edges(n, 1)
                    for s in range(2):
                        project(i, s)
                    if n is not None:
                        for s in range(2):
                            turn_x(n, s)

                pairs_of_steps(pe, last_i, first, body)

            @block.scalar
            def _(act):
                start(act, "scalar")
                last_i = act.value_load(n_pairs[0:1, 0:1], min_val=1, max_val=LAST_MAX)
                gi, gg, go, gt, gc = gate

                def take_attr(i, s):
                    act.wait_ge(attr_ps, i * 2 + s + 2)
                    act.wait_ge(agg_ps, i * 2 + 1)
                    act.activation(rows0[s][:, :, D:D + ED], bk[2 + s][:, 0:KT * ED].rearrange("p (k c) -> p k c", c=ED),
                                   ACT.Copy).then_inc(attr_sb, 1)

                def take_x(i, s):
                    act.wait_ge(xT_ps, i * 2 + s + 2)
                    act.activation(meanT[s][:, :], bk[2 + s][0:ED, 384:384 + TN], ACT.Copy)
                    act.activation(xT[:, :, TN * s:TN * s + TN],
                                   bk[s][:, 0:4 * TN].rearrange("p (c n) -> p c n", c=4), ACT.Copy).then_inc(xT_sb, 1)

                def first(i):
                    for stage in (take_attr, take_x):
                        for s in range(2):
                            stage(i, s)

                def body(i, n):
                    for f in range(NJ):
                        act.wait_ge(h1_ps, i * NJ + f + 2)
                        act.activation(h1T[:, f, :], bk[6 + f % 2][:, 0:2 * TN], ACT.Relu, bias=brel[:, f:f + 1]).then_inc(h1_sb, 1)
                    if n is not None:
                        for s in range(2):
                            take_attr(n, s)
                    for j in range(NJ):
                        b = j % 2
                        act.wait_ge(gate_ps, i * NJ + j + 2)
                        act.wait_ge(lstm_sb, i * NJ + max(j - 1, 0) + 1)
                        act.activation(gi[b][:, :], bk[4 + b][:, 0:2 * TN], ACT.Sigmoid, bias=bg[:, j:j + 1])
                        act.activation(gg[b][:, :], bk[4 + b][:, 256:256 + 2 * TN], ACT.Tanh, bias=bg[:, NJ + j:NJ + j + 1]).then_inc(gate_ig, 1)
                        act.activation(go[b][:, :], bk[6 + b][:, 0:2 * TN], ACT.Sigmoid, bias=bg[:, 2 * NJ + j:2 * NJ + j + 1])
                        act.wait_ge(cell, i * NJ + j + 2)
                        act.activation(gt[b][:, :], gc[b][:, :], ACT.Tanh).then_inc(gate_to, 1)
                    act.wait_ge(var_sb, i * 2 + 3)
                    for s in range(2):
                        ins = act.activation(stats[s][0:TN, 9:10], stats[s][0:TN, 8:9], ACT.Sqrt)
                    ins.then_inc(std_sb, 1)
                    for s in range(2):
                        act.wait_ge(h2T_ps, i * 2 + s + 2)
                        act.activation(h2T[s][:, :, :], bk[6 + s][:, 0:2 * TN].rearrange("p (c n) -> p c n", c=2), ACT.Copy).then_inc(h2T_sb, 1)
                    if n is not None:
                        for s in range(2):
                            take_x(n, s)

                pairs_of_steps(act, last_i, first, body)

            @block.vector
            def _(v):
                start(v, "vector")
                last_i = v.value_load(n_pairs[0:1, 0:1], min_val=1, max_val=LAST_MAX)
                pairs = last_i + 1
                gi, gg, go, gt, gc = gate

                def indices(i, s):
                    v.tensor_copy(idx[s][:, :], idx_all[:, bass.ds(i * (4 * KT) + s * 2 * KT, KT)]).then_inc(idx_ready, 1)

                def one_hot(i, s):
                    v.wait_ge(hot, i * 4 + 2 * s + 1)
                    v.tensor_scalar(drel[:, :], idx_all[:, bass.ds(i * (4 * KT) + s * 2 * KT + KT, KT)],
                                    baseT[:, bass.ds(i * 2 + s, 1)], None, ALU.subtract).then_inc(hot, 1)
                    v.wait_ge(hot, i * 4 + 2 * s + 2)
                    v.tensor_tensor(onehot[s][:, :, :].bitcast(F32R), iota_n[:, 0:TN].unsqueeze(1).broadcast_to([128, KT, TN]),
                                    drel[:, :].unsqueeze(2).broadcast_to([128, KT, TN]), ALU.is_equal).then_inc(hot, 1)

                for s in range(2):
                    indices(0, s)
                    v.memset(rows0[s][:, :, D + ED:AW], 1.0)
                v.memset(agg[1][:, :], 0.0)

                def hot_of(i):
                    for s in range(2):
                        v.wait_ge(agg_ps, i * 2 + 1)
                        one_hot(i, s)

                def take_sums(i, s):
                    v.wait_ge(agg_ps, i * 2 + s + 2)
                    v.wait_ge(xT_ps, i * 2 + 1)
                    v.wait_ge(agg_sb, i * 8 + 4 * s + 1)
                    v.scalar_tensor_tensor(out=agg[s][:, :], in0=agg[1 - s][:, :], scalar=keepT[0:TN, bass.ds(i * 2 + s, 1)],
                                           in1=bk[s][0:TN, 0:AW], op0=ALU.mult, op1=ALU.add).then_inc(agg_sb, 1)
                    v.wait_ge(agg_sb, i * 8 + 4 * s + 2)
                    v.wait_ge(gathered[s], i * (16 * KT) + 16 * KT)
                    indices(i + 1, s)
                    v.tensor_scalar(small[0:TN, 1:2], agg[s][:, AW - 1:AW], 1.0, None, ALU.max).then_inc(agg_sb, 1)
                    v.wait_ge(agg_sb, i * 8 + 4 * s + 3)
                    v.reciprocal(small[0:TN, 0:1], small[0:TN, 1:2]).then_inc(agg_sb, 1)
                    v.wait_ge(agg_sb, i * 8 + 4 * s + 4)
                    v.tensor_scalar(mean[s][:, :], agg[s][:, D:D + ED], small[0:TN, 0:1], None, ALU.mult).then_inc(agg_sb, 1)

                def first(i):
                    hot_of(i)
                    for s in range(2):
                        take_sums(i, s)

                def body(i, n):
                    if n is not None:
                        hot_of(n)
                    for j in range(NJ):
                        b = j % 2
                        v.wait_ge(gate_ig, i * NJ + j + 2)
                        v.tensor_tensor(gc[b][:, :], gi[b][:, :], gg[b][:, :], ALU.mult).then_inc(cell, 1)
                        v.wait_ge(gate_to, i * NJ + j + 2)
                        v.tensor_tensor(lstmT[:, j, :], go[b][:, :], gt[b][:, :], ALU.mult).then_inc(lstm_sb, 1)
                    for s in range(2):
                        v.wait_ge(norm_v, i * 8 + 4 * s + 1)
                        v.wait_ge(x_loaded[s], i * 16 + 16)
                        v.wait_ge(fc_ps, i * 2 + s + 2)
                        v.tensor_tensor(x1[s][:, :], bk[4 + s][0:TN, 0:D], xin[s][:, :], ALU.add).then_inc(norm_v, 1)
                        v.wait_ge(norm_v, i * 8 + 4 * s + 2)
                        v.tensor_tensor(x1[s][:, :], x1[s][:, :], bfc[0:TN, :], ALU.add).then_inc(norm_v, 1)
                        v.wait_ge(norm_v, i * 8 + 4 * s + 3)
                        v.bn_stats(stats[s][0:TN, 0:6], x1[s][:, :]).then_inc(norm_v, 1)
                        v.wait_ge(norm_v, i * 8 + 4 * s + 4)
                        v.sem_inc(passed, 1)
                        v.bn_aggr(stats[s][0:TN, 6:8], stats[s][0:TN, 0:6]).then_inc(norm_v, 1)
                        v.wait_ge(norm_v, i * 8 + 4 * s + 5)
                        v.tensor_scalar(stats[s][0:TN, 8:9], stats[s][0:TN, 7:8], EPS, None, ALU.add).then_inc(var_sb, 1)
                    for s in range(2):
                        v.wait_ge(scale_v, i * 4 + 2 * s + 1)
                        v.wait_ge(std_sb, i + 2)
                        v.wait_ge(stored_steps, i * 2 + s + 1)
                        v.reciprocal(stats[s][0:TN, 10:11], stats[s][0:TN, 9:10]).then_inc(scale_v, 1)
                        v.wait_ge(scale_v, i * 4 + 2 * s + 2)
                        v.tensor_scalar(h2[s][:, :], x1[s][:, :], stats[s][0:TN, 6:7], stats[s][0:TN, 10:11], ALU.subtract, ALU.mult).then_inc(scale_v, 1)
                        v.wait_ge(scale_v, i * 4 + 2 * s + 3)
                        v.tensor_scalar(h2[s][:, :], h2[s][:, :], 0.0, None, ALU.max).then_inc(h2_sb, 1)
                        v.wait_ge(h2_sb, i * 2 + s + 2)
                        v.tensor_tensor(rec[s][:, D:2 * D], x1[s][:, :], h2[s][:, :], ALU.add)
                    if n is not None:
                        for s in range(2):
                            take_sums(n, s)
                    for s in range(2):
                        v.wait_ge(node_v, i * 12 + 6 * s + 1)
                        v.wait_ge(xlr_ps, i * 2 + s + 2)
                        v.tensor_tensor(xl[s][:, :], bk[4 + s][0:TN, 0:D], blr[0:TN, 0:D], ALU.add).then_inc(node_v, 1)
                        v.tensor_tensor(rec[s][:, 0:D], bk[4 + s][0:TN, D:2 * D], blr[0:TN, D:2 * D], ALU.add).then_inc(node_v, 1)
                        v.wait_ge(node_v, i * 12 + 6 * s + 3)
                        v.tensor_tensor(ss[:, :], xl[s][:, :], rec[s][:, 0:D], ALU.add).then_inc(node_v, 1)
                        v.wait_ge(node_v, i * 12 + 6 * s + 4)
                        v.tensor_tensor(ss[:, :], bk[6 + s][0:TN, 0:D], ss[:, :], ALU.add).then_inc(node_v, 1)
                        v.wait_ge(node_v, i * 12 + 6 * s + 5)
                        v.scalar_tensor_tensor(out=sk[:, :], in0=ss[:, :], scalar=0.2, in1=ss[:, :], op0=ALU.mult, op1=ALU.max).then_inc(node_v, 1)
                        v.wait_ge(node_v, i * 12 + 6 * s + 6)
                        v.tensor_tensor(sk[:, :], sk[:, :], attb[0:TN, :], ALU.mult).then_inc(node_v, 1)
                        v.wait_ge(node_v, i * 12 + 6 * s + 7)
                        v.tensor_reduce(rec[s][:, 2 * D:RECW], sk[:, :].rearrange("p (h c) -> p h c", h=HEADS), AX.X, ALU.add).then_inc(node_out, 1)

                pairs_of_steps(v, last_i, first, body)

        early.close()
        with ExitStack() as sc:
            def tmp(name, shape, dt=F32):
                return sc.enter_context(nc.sbuf_tensor(name, shape, dt))

            def dma_sem(name):
                return sc.enter_context(nc.semaphore(name))

            RW = 5 * KT
            dst85 = [tmp(f"dst85{s}", [RW, 128], I32) for s in range(2)]
            xr_we = [tmp(f"xr_we{s}", [128, D]) for s in range(2)]
            xo = [tmp(f"xo{s}", [TN, D]) for s in range(2)]
            ro = [tmp(f"ro{s}", [TN, D + HEADS]) for s in range(2)]
            hotT = [tmp(f"hotT{s}", [128, STEP_E]) for s in range(2)]
            relu8 = [tmp(f"relu8{b}", [128, 2, 512]) for b in range(2)]
            leaky = [tmp(f"leaky{b}", [128, 2, 512]) for b in range(2)]
            weighed = tmp("weighed", [128, KT, XW])
            score = tmp("score", [128, 5, KT])
            begins = tmp("begins", [RW, 129])
            ends = tmp("ends", [RW, 128])
            runmax = tmp("runmax", [RW, 128])
            runT = tmp("runT", [128, 10, KT], F32R)
            pen = tmp("pen", [TN, KT])
            cand = tmp("cand", [TN, KT, HEADS])
            stepmax = tmp("stepmax", [TN, HEADS])
            prevmax = tmp("prevmax", [TN, HEADS])
            nmax = [tmp(f"nmax{s}", [TN, HEADS]) for s in range(2)]
            gap = tmp("gap", [TN, HEADS])
            corr = tmp("corr", [TN, HEADS])
            expo = tmp("expo", [128, HEADS, KT])
            ex = tmp("ex", [128, HEADS, KT])
            acc = [tmp(f"acc{s}", [TN, XW]) for s in range(2)]
            scaled = tmp("scaled", [TN, XW])
            selfm = tmp("selfm", [TN, HEADS])
            gap2 = tmp("gap2", [TN, 2, HEADS])
            c2 = tmp("c2", [TN, 2, HEADS])
            tot = tmp("tot", [TN, XW])
            own = tmp("own", [TN, D])
            rden = tmp("rden", [TN, HEADS])
            y = tmp("y", [TN, D])
            em = tmp("em", [TN, D])
            res = [tmp(f"res{s}", [TN, D]) for s in range(2)]

            silu_v = stage_sem(sc, "silu_v", "vector")
            loadedF = [dma_sem(f"loadedF{s}") for s in range(2)]
            loadedB = [dma_sem(f"loadedB{s}") for s in range(2)]
            gathered1 = [dma_sem(f"gathered1_{s}") for s in range(2)]
            idx_ready1 = stage_sem(sc, "idx_ready1", "vector")
            hot1 = stage_sem(sc, "hot1", "vector")
            hotT_ps = stage_sem(sc, "hotT_ps", "tensor")
            hotT_sb = stage_sem(sc, "hotT_sb", "scalar")
            s_ps = stage_sem(sc, "s_ps", "tensor")
            relu_sb = stage_sem(sc, "relu_sb", "scalar")
            leaky_sb = stage_sem(sc, "leaky_sb", "vector")
            score_ps = stage_sem(sc, "score_ps", "tensor")
            score_sb = stage_sem(sc, "score_sb", "vector")
            scoreT_ps = stage_sem(sc, "scoreT_ps", "tensor")
            runs = stage_sem(sc, "runs", "vector")
            runT_ps = stage_sem(sc, "runT_ps", "tensor")
            runT_sb = stage_sem(sc, "runT_sb", "vector")
            cand_ps = stage_sem(sc, "cand_ps", "tensor")
            maxs = stage_sem(sc, "maxs", "vector")
            corr_sb = stage_sem(sc, "corr_sb", "scalar")
            shift_ps = stage_sem(sc, "shift_ps", "tensor")
            expos = stage_sem(sc, "expos", "vector")
            ex_sb = stage_sem(sc, "ex_sb", "scalar")
            weighted = stage_sem(sc, "weighted", "vector")
            out_ps = stage_sem(sc, "out_ps", "tensor")
            fin1 = stage_sem(sc, "fin1", "vector")
            self_exp = stage_sem(sc, "self_exp", "scalar")
            y_exp = stage_sem(sc, "y_exp", "scalar")
            res_ready = stage_sem(sc, "res_ready", "vector")
            we_in = dma_sem("we_in")
            stored1 = dma_sem("stored1")
            stored_steps1 = stage_sem(sc, "stored_steps1", "sync")
            block = sc.enter_context(nc.Block())

            NMAX = 9
            S_PS = [[bk[0], bk[1]], [bk[2], bk[3]]]
            SCORE = bk[6][:, 0:HEADS * KT].rearrange("p (h k) -> p h k", h=HEADS)
            SHIFT = bk[7][:, 152:152 + HEADS * KT].rearrange("p (k h) -> p k h", k=KT)
            SCORET = bk[7][0:RW, 272:400]
            RUNT = bk[7][:, 400:400 + RW]
            OUT = bk[7][0:TN, 0:XW]
            CAND = bk[7][0:TN, 0:2 * RW].rearrange("p (k h) -> p k h", k=KT)

            @block.sync
            def _(sp):
                start(sp, "sync")
                last_i = sp.value_load(n_pairs[0:1, 0:1], min_val=1, max_val=LAST_MAX)
                pairs = last_i + 1

                def load_front(i, s):
                    e0 = sp.value_load(table[0:1, bass.ds(i * 4 + 2 * s, 1)], min_val=0, max_val=N_EDGES)
                    v0 = sp.value_load(table[0:1, bass.ds(i * 4 + 2 * s + 1, 1)], min_val=0, max_val=LAST_BASE)
                    sp.dma_start(hotT[s][TN:128, :], attrT[:, bass.ds(e0, STEP_E)]).then_inc(loadedF[s], 16)
                    for h in range(5):
                        sp.dma_start(dst85[s][KT * h:KT * h + KT, :], edge_rows(dst, e0)).then_inc(loadedF[s], 16)
                    sp.dma_start(xr_we[s][0:TN, :], node_rec[bass.ds(v0, TN), 0:D]).then_inc(loadedF[s], 16)

                def load_back(i, s):
                    v0 = sp.value_load(table[0:1, bass.ds(i * 4 + 2 * s + 1, 1)], min_val=0, max_val=LAST_BASE)
                    sp.dma_start(ro[s][:, :], node_rec[bass.ds(v0, TN), D:RECW]).then_inc(loadedB[s], 16)
                    sp.dma_start(xo[s][:, :], xl_rows[bass.ds(v0, TN), :]).then_inc(loadedB[s], 16)

                for s in range(2):
                    sp.dma_start(xr_we[s][TN:128, :], w_eT).then_inc(we_in, 16)
                    load_front(0, s)
                    load_back(0, s)
                sp.sem_inc(stored_steps1, 1)
                with sp.Fori(0, pairs) as i:
                    for s in range(2):
                        sp.wait_ge(weighted, i * 2 + s + 2)
                        sp.sem_inc(passed, 1)
                        load_front(i + 1, s)
                    for s in range(2):
                        v0 = sp.value_load(table[0:1, bass.ds(i * 4 + 2 * s + 1, 1)], min_val=0, max_val=LAST_BASE)
                        sp.wait_ge(res_ready, i * 2 + s + 2)
                        sp.sem_inc(passed, 1)
                        sp.dma_start(out[bass.ds(v0, TN), :], res[s][:, :]).then_inc(stored1, 16)
                        load_back(i + 1, s)
                        sp.wait_ge(stored1, i * 32 + 16 * s + 16)
                        sp.sem_inc(passed, 1)
                        sp.sem_inc(stored_steps1, 1)
                sp.wait_ge(we_in, 32)
                for s in range(2):
                    sp.wait_ge(loadedF[s], pairs * 112 + 112)
                    sp.sem_inc(passed, 1)
                    sp.wait_ge(loadedB[s], pairs * 32 + 32)
                    sp.sem_inc(passed, 1)

            @block.gpsimd
            def _(pool):
                last_i = pool.value_load(n_pairs[0:1, 0:1], min_val=1, max_val=LAST_MAX)
                pairs = last_i + 1
                with pool.Fori(0, pairs) as i:
                    for s in range(2):
                        pool.wait_ge(idx_ready1, i * 2 + s + 2)
                        pool.sem_inc(passed, 1)
                        for k in range(KT):
                            pool.indirect_dma_start(rows1[s][:, k, :], None, xl_rows,
                                                    bass.IndirectOffsetOnAxis(ap=idx[s][:, k:k + 1], axis=0)
                                                    ).then_inc(gathered1[s], 16)

            def later(i, s):
                return not isinstance(i, int) or i * 2 + s > 0

            def steps(eng, last_i, first, turn, last):
                first()
                turn((0, 0), (0, 1), (1, 0), None)
                with eng.Fori(0, last_i) as i:
                    turn((i, 1), (i + 1, 0), (i + 1, 1), (i, 0))
                    turn((i + 1, 0), (i + 1, 1), (i + 2, 0), (i, 1))
                last((last_i, 1), (last_i, 0))

            @block.tensor
            def _(pe):
                start(pe, "tensor")
                last_i = pe.value_load(n_pairs[0:1, 0:1], min_val=1, max_val=LAST_MAX)
                pairs = last_i + 1

                def turn_hot(i, s):
                    pe.wait_ge(hot1, i * 4 + 2 * s + 3)
                    for q, ks in enumerate(QS):
                        if q >= 2:
                            pe.wait_ge(hotT_sb, i * (2 * NQ) + s * NQ + q)
                        for n, k in enumerate(ks):
                            m = pe.transpose(bk[4 + q % 2][0:TN, 128 * n:128 * n + 128], onehot[s][:, k, :], ident[:, :])
                        m.then_inc(hotT_ps, 1)

                def sums(i, s, q):
                    ks = QS[q]
                    e0, n = 128 * ks[0], 128 * len(ks)
                    if q == 0:
                        pe.wait_ge(loadedF[s], i * 112 + 112)
                        pe.wait_ge(gathered1[s], i * (16 * KT) + 16 * KT)
                    pe.wait_ge(hotT_sb, i * (2 * NQ) + s * NQ + q + 2)
                    if q >= 2:
                        pe.wait_ge(leaky_sb, i * (2 * NQ) + s * NQ + q)
                    else:
                        pe.wait_ge(leaky_sb, i * (2 * NQ) + s * NQ + 1)
                    for c in range(2):
                        to = S_PS[q % 2][c]
                        for m, k in enumerate(ks):
                            pe.matmul(to[:, 128 * m:128 * m + 128],
                                      rows1[s][:, k, 128 * c:128 * c + 128],
                                      ident[:, :], is_transpose=True, start=(m == 0), stop=False, skip_group_check=True)
                        m = pe.matmul(to[:, 0:n], xr_we[s][:, 128 * c:128 * c + 128], hotT[s][:, e0:e0 + n],
                                      start=False, stop=True, skip_group_check=True)
                    m.then_inc(s_ps, 1)

                def scores(i, s, q):
                    pe.wait_ge(leaky_sb, i * (2 * NQ) + s * NQ + q + 2)
                    for n, k in enumerate(QS[q]):
                        for c in range(2):
                            m = pe.matmul(SCORE[:, :, k], leaky[q % 2][:, c, 128 * n:128 * n + 128], attc[:, c, :],
                                          start=(c == 0), stop=(c == 1))
                    m.then_inc(score_ps, 1)

                def turn_scores(i, s):
                    pe.wait_ge(score_sb, i * 2 + s + 2)
                    pe.transpose(SCORET, score[:, :, :], ident[:, :]).then_inc(scoreT_ps, 1)

                def turn_runs(i, s):
                    pe.wait_ge(runs, i * 14 + 7 * s + 8)
                    pe.transpose(RUNT, runmax[:, :], ident[0:RW, 0:RW]).then_inc(runT_ps, 1)

                def candidates(i, s):
                    pe.wait_ge(runT_sb, i * 4 + 2 * s + 3)
                    for k in range(KT):
                        m = pe.matmul(CAND[:, k, :], onehot[s][:, k, :].bitcast(F32R), runT[:, :, k], start=True, stop=True)
                    m.then_inc(cand_ps, 1)

                def shifts(i, s):
                    pe.wait_ge(maxs, i * (2 * NMAX) + s * NMAX + NMAX)
                    for k in range(KT):
                        m = pe.matmul(SHIFT[:, k, :], hotT[s][0:TN, 128 * k:128 * k + 128], nmax[s][:, :], start=True, stop=True)
                    m.then_inc(shift_ps, 1)

                def outputs(i, s):
                    pe.wait_ge(weighted, i * 2 + s + 2)
                    for k in range(KT):
                        m = pe.matmul(OUT, onehot[s][:, k, :], weighed[:, k, :], start=(k == 0), stop=(k == KT - 1))
                    m.then_inc(out_ps, 1)

                def first():
                    turn_hot(0, 0)
                    sums(0, 0, 0)
                    for q in range(1, NQ):
                        sums(0, 0, q)
                        scores(0, 0, q - 1)
                    scores(0, 0, NQ - 1)

                def turn(b, f, g, p):
                    turn_scores(*b)
                    turn_hot(*f)
                    turn_runs(*b)
                    candidates(*b)
                    sums(*f, 0)
                    shifts(*b)
                    sums(*f, 1)
                    scores(*f, 0)
                    sums(*f, 2)
                    scores(*f, 1)
                    outputs(*b)
                    sums(*f, 3)
                    scores(*f, 2)
                    scores(*f, 3)

                def last(b, p):
                    for stage in (turn_scores, turn_runs, candidates, shifts, outputs):
                        stage(*b)

                steps(pe, last_i, first, turn, last)

            @block.scalar
            def _(act):
                start(act, "scalar")
                last_i = act.value_load(n_pairs[0:1, 0:1], min_val=1, max_val=LAST_MAX)
                pairs = last_i + 1

                def turned(i, s):
                    if later(i, s):
                        act.wait_ge(shift_ps, i * 2 + s)
                    for q, ks in enumerate(QS):
                        n = 128 * len(ks)
                        act.wait_ge(hotT_ps, i * (2 * NQ) + s * NQ + q + 2)
                        act.activation(hotT[s][0:TN, 128 * ks[0]:128 * ks[0] + n], bk[4 + q % 2][0:TN, 0:n], ACT.Copy).then_inc(hotT_sb, 1)

                def relu(i, s, q):
                    n = 128 * len(QS[q])
                    act.wait_ge(s_ps, i * (2 * NQ) + s * NQ + q + 2)
                    act.wait_ge(leaky_sb, i * (2 * NQ) + s * NQ + max(q - 1, 0) + 1)
                    act.activation(relu8[q % 2][:, 0, 0:n], S_PS[q % 2][0][:, 0:n], ACT.Relu, scale=0.8)
                    act.activation(relu8[q % 2][:, 1, 0:n], S_PS[q % 2][1][:, 0:n], ACT.Relu, scale=0.8).then_inc(relu_sb, 1)

                def correction(i, s):
                    act.wait_ge(maxs, i * (2 * NMAX) + s * NMAX + NMAX + 1)
                    if later(i, s):
                        act.wait_ge(fin1, i * 30 + 15 * s - 11)
                    act.activation(corr[:, :], gap[:, :], ACT.Exp).then_inc(corr_sb, 1)

                def weights(i, s):
                    act.wait_ge(expos, i * 4 + 2 * s + 3)
                    act.activation(ex[:, :, :], expo[:, :, :], ACT.Exp).then_inc(ex_sb, 1)

                def self_weights(i, s):
                    act.wait_ge(fin1, i * 30 + 15 * s + 6)
                    act.activation(c2[:, :, :], gap2[:, :, :], ACT.Exp).then_inc(self_exp, 1)

                def silu_exp(i, s):
                    act.wait_ge(fin1, i * 30 + 15 * s + 16)
                    act.activation(em[:, :], y[:, :], ACT.Exp, scale=-1.0).then_inc(y_exp, 1)

                def first():
                    turned(0, 0)
                    for q in range(NQ):
                        relu(0, 0, q)

                def turn(b, f, g, p):
                    turned(*f)
                    correction(*b)
                    relu(*f, 0)
                    weights(*b)
                    relu(*f, 1)
                    if p:
                        silu_exp(*p)
                    relu(*f, 2)
                    relu(*f, 3)
                    self_weights(*b)

                def last(b, p):
                    correction(*b)
                    weights(*b)
                    silu_exp(*p)
                    self_weights(*b)
                    silu_exp(*b)

                steps(act, last_i, first, turn, last)

            @block.vector
            def _(v):
                start(v, "vector")
                last_i = v.value_load(n_pairs[0:1, 0:1], min_val=1, max_val=LAST_MAX)
                pairs = last_i + 1

                def indices(i, s):
                    v.tensor_copy(idx[s][:, :], idx_all[:, bass.ds(i * (4 * KT) + s * 2 * KT, KT)]).then_inc(idx_ready1, 1)

                def one_hot(i, s):
                    if later(i, s):
                        v.wait_ge(out_ps, i * 2 + s)
                    v.wait_ge(hot1, i * 4 + 2 * s + 1)
                    v.tensor_scalar(drel[:, :], idx_all[:, bass.ds(i * (4 * KT) + s * 2 * KT + KT, KT)],
                                    baseT[:, bass.ds(i * 2 + s, 1)], None, ALU.subtract).then_inc(hot1, 1)
                    v.wait_ge(hot1, i * 4 + 2 * s + 2)
                    v.tensor_tensor(onehot[s][:, :, :].bitcast(F32R), iota_n[:, 0:TN].unsqueeze(1).broadcast_to([128, KT, TN]),
                                    drel[:, :].unsqueeze(2).broadcast_to([128, KT, TN]), ALU.is_equal).then_inc(hot1, 1)

                def leak(i, s, q):
                    n = 128 * len(QS[q])
                    v.wait_ge(relu_sb, i * (2 * NQ) + s * NQ + q + 2)
                    v.wait_ge(score_ps, i * (2 * NQ) + s * NQ + max(q - 1, 0) + 1)
                    for c in range(2):
                        ins = v.scalar_tensor_tensor(out=leaky[q % 2][:, c, 0:n], in0=S_PS[q % 2][c][:, 0:n], scalar=0.2,
                                                     in1=relu8[q % 2][:, c, 0:n], op0=ALU.mult, op1=ALU.add)
                    ins.then_inc(leaky_sb, 1)

                def take_scores(i, s):
                    v.wait_ge(score_ps, i * (2 * NQ) + s * NQ + NQ + 1)
                    v.tensor_copy(score[:, 0:HEADS, :], SCORE).then_inc(score_sb, 1)

                def run_maxima(i, s):
                    v.wait_ge(runs, i * 14 + 7 * s + 1)
                    v.tensor_tensor(begins[:, 1:128], dst85[s][:, 1:128], dst85[s][:, 0:127], ALU.not_equal).then_inc(runs, 1)
                    v.wait_ge(runs, i * 14 + 7 * s + 2)
                    v.tensor_copy(ends[:, :], begins[:, 1:129]).then_inc(runs, 1)
                    v.memset(begins[:, 0:1], 1.0).then_inc(runs, 1)
                    v.wait_ge(runs, i * 14 + 7 * s + 4)
                    v.tensor_scalar(begins[:, 0:128], begins[:, 0:128], -BIG, None, ALU.mult).then_inc(runs, 1)
                    v.wait_ge(runs, i * 14 + 7 * s + 5)
                    v.wait_ge(scoreT_ps, i * 2 + s + 2)
                    v.tensor_tensor_scan(runmax[:, :], begins[:, 0:128], SCORET, 0.0, ALU.add, ALU.max).then_inc(runs, 1)
                    v.wait_ge(runs, i * 14 + 7 * s + 6)
                    v.tensor_tensor(runmax[:, :], runmax[:, :], ends[:, :], ALU.mult).then_inc(runs, 1)
                    v.wait_ge(runs, i * 14 + 7 * s + 7)
                    v.memset(begins[:, 0:1], 1.0).then_inc(runs, 1)

                def take_runs(i, s):
                    v.wait_ge(runT_ps, i * 2 + s + 2)
                    v.tensor_copy(runT[:, 0:5, :], RUNT.rearrange("p (h k) -> p h k", h=5)).then_inc(runT_sb, 1)
                    v.wait_ge(runT_sb, i * 4 + 2 * s + 2)
                    v.tensor_tensor(runT[:, 5:10, :], RUNT.rearrange("p (h k) -> p h k", h=5), runT[:, 0:5, :],
                                    ALU.subtract).then_inc(runT_sb, 1)

                def maxima(i, s):
                    n = i * (2 * NMAX) + s * NMAX
                    keep = keepT[0:TN, bass.ds(i * 2 + s, 1)]
                    v.wait_ge(maxs, n + 1)
                    v.wait_ge(cand_ps, i * 2 + s + 2)
                    v.tensor_scalar(pen[:, :], CAND[:, :, HEADS], 1.0, BIG, ALU.subtract, ALU.mult).then_inc(maxs, 1)
                    v.tensor_scalar(prevmax[:, :], keep.broadcast_to([TN, HEADS]), 1.0, BIG, ALU.subtract, ALU.mult).then_inc(maxs, 1)
                    v.tensor_copy(cand[:, :, :], CAND[:, :, 0:HEADS]).then_inc(maxs, 1)
                    v.wait_ge(maxs, n + 4)
                    v.scalar_tensor_tensor(out=prevmax[:, :], in0=nmax[1 - s][:, :], scalar=keep, in1=prevmax[:, :],
                                           op0=ALU.mult, op1=ALU.add).then_inc(maxs, 1)
                    v.tensor_tensor(cand[:, :, :], CAND[:, :, 5:5 + HEADS], cand[:, :, :], ALU.add).then_inc(maxs, 1)
                    v.wait_ge(maxs, n + 6)
                    v.tensor_tensor(cand[:, :, :], cand[:, :, :], pen[:, :].unsqueeze(2).broadcast_to([TN, KT, HEADS]), ALU.add).then_inc(maxs, 1)
                    v.wait_ge(maxs, n + 7)
                    v.tensor_reduce(stepmax[:, :], cand[:, :, :].rearrange("p k h -> p h k"), AX.X, ALU.max).then_inc(maxs, 1)
                    v.wait_ge(maxs, n + 8)
                    v.tensor_tensor(nmax[s][:, :], stepmax[:, :], prevmax[:, :], ALU.max).then_inc(maxs, 1)
                    v.wait_ge(maxs, n + 9)
                    v.wait_ge(corr_sb, i * 2 + s + 1)
                    v.tensor_tensor(gap[:, :], prevmax[:, :], nmax[s][:, :], ALU.subtract).then_inc(maxs, 1)

                def exponents(i, s):
                    v.wait_ge(expos, i * 4 + 2 * s + 1)
                    v.wait_ge(shift_ps, i * 2 + s + 2)
                    v.tensor_tensor(expo[:, :, :], score[:, 0:HEADS, :], SHIFT.rearrange("p k h -> p h k"),
                                    ALU.subtract).then_inc(expos, 1)
                    v.wait_ge(expos, i * 4 + 2 * s + 2)
                    v.tensor_scalar(expo[:, :, :], expo[:, :, :], 0.0, None, ALU.min).then_inc(expos, 1)

                def weigh(i, s):
                    v.wait_ge(ex_sb, i * 2 + s + 2)
                    if later(i, s):
                        v.wait_ge(out_ps, i * 2 + s + 1)
                    by_tile = ex[:, :, :].rearrange("p h k -> p k h")
                    v.tensor_copy(weighed[:, :, D:XW], by_tile)
                    v.tensor_tensor(weighed[:, :, 0:D].rearrange("p k (h c) -> p k h c", h=HEADS),
                                    rows1[s][:, :, :].rearrange("p k (h c) -> p k h c", h=HEADS),
                                    by_tile.unsqueeze(3).broadcast_to([128, KT, HEADS, HD]), ALU.mult).then_inc(weighted, 1)
                    indices(i + 1, s)

                def by_head(a):
                    return a.rearrange("p (h c) -> p h c", h=HEADS)

                def wide(a):
                    return a.unsqueeze(2).broadcast_to([TN, HEADS, HD])

                def add_up(i, s):
                    v.wait_ge(fin1, i * 30 + 15 * s + 1)
                    keep = keepT[0:TN, bass.ds(i * 2 + s, 1)]

                    v.wait_ge(loadedB[s], i * 32 + 32)
                    v.wait_ge(corr_sb, i * 2 + s + 2)
                    v.tensor_tensor(selfm[:, :], nmax[s][:, :], ro[s][:, D:D + HEADS], ALU.max).then_inc(fin1, 1)
                    v.scalar_tensor_tensor(out=by_head(scaled[:, 0:D]), in0=by_head(acc[1 - s][:, 0:D]), scalar=keep,
                                           in1=wide(corr[:, :]), op0=ALU.mult, op1=ALU.mult).then_inc(fin1, 1)
                    v.scalar_tensor_tensor(out=scaled[:, D:XW], in0=acc[1 - s][:, D:XW], scalar=keep,
                                           in1=corr[:, :], op0=ALU.mult, op1=ALU.mult).then_inc(fin1, 1)
                    v.wait_ge(fin1, i * 30 + 15 * s + 4)
                    v.tensor_tensor(gap2[:, 0, :], nmax[s][:, :], selfm[:, :], ALU.subtract).then_inc(fin1, 1)
                    v.tensor_tensor(gap2[:, 1, :], ro[s][:, D:D + HEADS], selfm[:, :], ALU.subtract).then_inc(fin1, 1)
                    v.wait_ge(out_ps, i * 2 + s + 2)
                    v.tensor_tensor(acc[s][:, :], scaled[:, :], OUT, ALU.add).then_inc(fin1, 1)
                    v.wait_ge(fin1, i * 30 + 15 * s + 7)

                def finish(i, s):
                    v.wait_ge(self_exp, i * 2 + s + 2)
                    v.tensor_tensor(by_head(tot[:, 0:D]), by_head(acc[s][:, 0:D]), wide(c2[:, 0, :]), ALU.mult).then_inc(fin1, 1)
                    v.tensor_tensor(tot[:, D:XW], acc[s][:, D:XW], c2[:, 0, :], ALU.mult).then_inc(fin1, 1)
                    v.tensor_tensor(by_head(own[:, :]), by_head(xo[s][:, :]), wide(c2[:, 1, :]), ALU.mult).then_inc(fin1, 1)
                    v.wait_ge(fin1, i * 30 + 15 * s + 10)
                    v.tensor_tensor(tot[:, 0:D], tot[:, 0:D], own[:, :], ALU.add).then_inc(fin1, 1)
                    v.tensor_tensor(rden[:, :], tot[:, D:XW], c2[:, 1, :], ALU.add).then_inc(fin1, 1)
                    v.wait_ge(fin1, i * 30 + 15 * s + 12)
                    v.tensor_scalar(rden[:, :], rden[:, :], 1e-16, None, ALU.add).then_inc(fin1, 1)
                    v.wait_ge(fin1, i * 30 + 15 * s + 13)
                    v.reciprocal(rden[:, :], rden[:, :]).then_inc(fin1, 1)
                    v.wait_ge(fin1, i * 30 + 15 * s + 14)
                    v.tensor_tensor(by_head(y[:, :]), by_head(tot[:, 0:D]), wide(rden[:, :]), ALU.mult).then_inc(fin1, 1)
                    v.wait_ge(fin1, i * 30 + 15 * s + 15)
                    v.tensor_tensor(y[:, :], y[:, :], bout[0:TN, :], ALU.add).then_inc(fin1, 1)

                def silu(i, s):
                    v.wait_ge(silu_v, i * 6 + 3 * s + 1)
                    v.wait_ge(y_exp, i * 2 + s + 2)
                    v.tensor_scalar(em[:, :], em[:, :], 1.0, None, ALU.add).then_inc(silu_v, 1)
                    v.wait_ge(silu_v, i * 6 + 3 * s + 2)
                    v.reciprocal(em[:, :], em[:, :]).then_inc(silu_v, 1)
                    v.wait_ge(silu_v, i * 6 + 3 * s + 3)
                    v.tensor_tensor(em[:, :], em[:, :], y[:, :], ALU.mult).then_inc(silu_v, 1)
                    v.wait_ge(silu_v, i * 6 + 3 * s + 4)
                    v.wait_ge(stored_steps1, i * 2 + s + 1)
                    v.tensor_tensor(res[s][:, :], em[:, :], ro[s][:, 0:D], ALU.add).then_inc(res_ready, 1)

                def first():
                    for s in range(2):
                        indices(0, s)
                    v.memset(score[:, HEADS:, :], 1.0)
                    v.memset(begins[:, 0:1], 1.0)
                    v.memset(begins[:, 128:129], 1.0)
                    v.memset(nmax[1][:, :], 0.0)
                    v.memset(acc[1][:, :], 0.0)
                    one_hot(0, 0)
                    for q in range(NQ):
                        leak(0, 0, q)
                    one_hot(0, 1)
                    take_scores(0, 0)

                def turn(b, f, g, p):
                    run_maxima(*b)
                    take_runs(*b)
                    maxima(*b)
                    leak(*f, 0)
                    exponents(*b)
                    weigh(*b)
                    leak(*f, 1)
                    if p:
                        finish(*p)
                    leak(*f, 2)
                    if p:
                        silu(*p)
                    leak(*f, 3)
                    add_up(*b)
                    one_hot(*g)
                    take_scores(*f)

                def last(b, p):
                    for stage in (run_maxima, take_runs, maxima, exponents, weigh):
                        stage(*b)
                    finish(*p)
                    silu(*p)
                    add_up(*b)
                    finish(*b)
                    silu(*b)

                steps(v, last_i, first, turn, last)


def kernel(**inputs):
    import concourse.bacc as bacc
    from concourse.bass_utils import run_bass_kernel_spmd as run

    a = {k: np.asarray(v) for k, v in inputs.items()}
    order = np.r_[0:DH, 2 * DH:4 * DH]

    def columns(v, n):
        return np.ascontiguousarray(v.reshape(n, 128).T)

    arrays = {
        "x": a["x"],
        "src": np.pad(a["src"], (0, STEP_E)),
        "dst": np.pad(a["dst"], (0, STEP_E), constant_values=N_NODES),
        "attrT": np.ascontiguousarray(np.pad(a["edge_attr_16"], ((0, STEP_E), (0, 0))).T),
        "w_rr": np.concatenate([a["L0_gnn_W_rel"], a["L0_gnn_W_root"]]),
        "b_rel": columns(a["L0_gnn_b_rel"], NJ),
        "w_ihT": np.ascontiguousarray(a["L0_gnn_W_ih"][order].T),
        "b_ih": columns(a["L0_gnn_b_ih"][order], 3 * NJ),
        "b_hh": columns(a["L0_gnn_b_hh"][order], 3 * NJ),
        "w_fc": a["L0_gnn_W_fc"],
        "b_fc": a["L0_gnn_b_fc"],
        "w_lr": np.ascontiguousarray(np.concatenate([a["L1_gnn_W_l"].T, a["L1_gnn_W_r"].T], axis=1)),
        "b_l": a["L1_gnn_b_l"],
        "b_r": a["L1_gnn_b_r"],
        "w_eT": np.ascontiguousarray(a["L1_gnn_W_e"].T),
        "att": np.ascontiguousarray(a["L1_gnn_att"].reshape(-1)),
        "bias": a["L1_gnn_bias"],
    }
    nc = bacc.Bacc("TRN2", target_bir_lowering=False, num_devices=1)
    args = [nc.dram_tensor(k, v.shape, mybir.dt.from_np(v.dtype), kind="ExternalInput").ap() for k, v in arrays.items()]
    out = nc.dram_tensor("out", [N_NODES, D], F32, kind="ExternalOutput").ap()
    gnn_layers(nc, *args, out)
    return run(nc, [arrays], core_ids=[0]).results[0]["out"]
```

```python
from contextlib import ExitStack

import numpy as np
import concourse.bass as bass
from concourse import mybir

F32 = mybir.dt.float32
I32 = mybir.dt.int32
F32R = mybir.dt.float32r
ALU = mybir.AluOpType
ACT = mybir.ActivationFunctionType
AX = mybir.AxisListType

N_NODES, N_EDGES = 6250, 100000
D, DH = 256, 512
HEADS, HD = 4, 64
ED = 16
TN = 128 - 2 * ED
TILES = -(-N_NODES // TN)
N_PAD = TILES * TN
LAST_BASE = N_PAD - TN
KT = 13
STEP_E = KT * 128
STEPS_MAX = TILES + (N_EDGES - TILES) // STEP_E
TABLE = 128
TABLE_PAD = TABLE + 8
ROUNDS = -(-N_EDGES // STEP_E)
E_PAD = N_EDGES + STEP_E
XW = D + HEADS
AW = D + ED + 2
RECW = 2 * D + HEADS
NJ = DH // 128
BIG = 1.0e30
EPS = 1.0e-5
QS = [range(0, 4), range(4, 8), range(8, 12), range(12, 13)]
NQ = len(QS)
P5 = 125
LAST_MAX = 2 * -(-STEPS_MAX // 4) - 1
assert STEPS_MAX <= TABLE and 2 * LAST_MAX + 6 <= TABLE_PAD and NQ == 4 and N_NODES % (5 * P5) == 0 and N_EDGES % P5 == 0


class Count:

    def __init__(self):
        self.n = 0

    def one_more(self):
        self.n += 1
        return self.n


def gnn_layers(nc, x, edges, attr, w_rr, b_rel, w_ihT, b_ih, b_hh, w_fc, b_fc, w_lr, b_l, b_r, w_eT, att, bias, out):
    ctx = ExitStack()
    with ctx:
        def sb(name, shape, dt=F32):
            return ctx.enter_context(nc.sbuf_tensor(name, shape, dt))

        def sem(name):
            return ctx.enter_context(nc.semaphore(name))

        def stage_sem(scope, name, engine):
            q = scope.enter_context(nc.semaphore(name))
            to_start.append((engine, q))
            return q

        to_start = []

        def start(eng, engine):
            for of, q in list(to_start):
                if of == engine:
                    eng.sem_inc(q, 1)
                    to_start.remove((of, q))

        h_rows = nc.dram_tensor("h_rows", [N_PAD, D], F32).ap()
        xl_rows = nc.dram_tensor("xl_rows", [N_PAD, D], F32).ap()
        node_rec = nc.dram_tensor("node_rec", [N_PAD, RECW], F32).ap()
        step_list = nc.dram_tensor("step_list", [TABLE, 2], I32).ap()

        bk = [ctx.enter_context(nc.psum_tensor(f"bank{i}", [128, 512], F32)) for i in range(8)]

        weT = sb("weT", [ED, D])
        bout = sb("bout", [128, D])
        attc = sb("attc", [128, 2, HEADS])
        ident = sb("ident", [128, 128])
        ones = sb("ones", [128, 128])
        iota_n = sb("iota_n", [128, 128])
        iota_p = sb("iota_p", [128, 1])
        table = sb("table", [1, TABLE_PAD * 2], I32)
        n_pairs = sb("n_pairs", [1, 2], I32)
        baseT = sb("baseT", [128, TABLE_PAD])
        keepT = sb("keepT", [128, TABLE_PAD])
        idx_all = sb("idx_all", [128, TABLE_PAD * 2 * KT], I32)
        idx = [sb(f"idx{s}", [128, KT], I32) for s in range(2)]
        drel = sb("drel", [128, KT])
        eri = [sb(f"eri{s}", [8 * KT, 128], I32) for s in range(2)]
        erf = [sb(f"erf{s}", [8 * KT, 128]) for s in range(2)]
        rows = [sb(f"rows{s}", [128, KT * AW]) for s in range(2)]
        rows0 = [r[:, :].rearrange("p (k c) -> p k c", k=KT) for r in rows]
        onehot = [sb(f"onehot{s}", [128, KT, 128]) for s in range(2)]
        small = sb("small", [128, 64])
        stats = [sb(f"stats{s}", [128, 12]) for s in range(2)]

        early = ctx.enter_context(ExitStack())

        def early_sb(name, shape):
            return early.enter_context(nc.sbuf_tensor(name, shape, F32))

        wrr = early_sb("wrr", [128, 4, DH])
        wih = early_sb("wih", [128, NJ, 3 * DH])
        wfc = early_sb("wfc", [128, NJ, D])
        wlr = early_sb("wlr", [128, 2, 2 * D])
        brel = early_sb("brel", [128, NJ])
        bg1 = early_sb("bg1", [128, 12])
        bg2 = early_sb("bg2", [128, 12])
        bg = early_sb("bg", [128, 12])
        bfc = early_sb("bfc", [128, D])
        blr = early_sb("blr", [128, 2 * D])
        attb = early_sb("attb", [128, D])

        setup_in = sem("setup_in")
        setup_c = sem("setup_c")
        dst_in = sem("dst_in")
        setup_t = sem("setup_t")
        counts_ps = sem("counts_ps")
        table_out = sem("table_out")
        table_in = sem("table_in")
        ln_in = [sem(f"ln_in{s}") for s in range(2)]
        ln_v = sem("ln_v")
        ln_scale = sem("ln_scale")
        ln_var = sem("ln_var")
        ln_std = sem("ln_std")
        ln_out = [sem(f"ln_out{s}") for s in range(2)]
        setup_v = sem("setup_v")
        passed = sem("passed")
        er_in = [sem(f"er_in{s}") for s in range(2)]
        gathered = [sem(f"gathered{s}") for s in range(2)]

        with ExitStack() as sc:
            def tmp(name, shape, dt=F32):
                return sc.enter_context(nc.sbuf_tensor(name, shape, dt))
            dsti = tmp("dsti", [P5, N_EDGES // P5], I32)
            dstf = tmp("dstf", [P5, N_EDGES // P5])
            junk = tmp("junk", [P5, N_EDGES // P5])
            part = tmp("part", [128, TILES + 1])
            counted = tmp("counted", [128, TILES + 1])
            rstd = tmp("rstd", [P5, 10])
            shift = tmp("shift", [P5, 10])
            padding = tmp("padding", [N_PAD - N_NODES, D])
            cnt = tmp("cnt", [128, TILES])
            thr = tmp("thr", [128, ROUNDS])
            over = tmp("over", [128, TILES, ROUNDS])
            rnd = tmp("rnd", [128, TILES])
            cum = tmp("cum", [128, TILES])
            zero = tmp("zero", [128, TILES])
            cmp = tmp("cmp", [128, TILES])
            sel = tmp("sel", [128, TILES])
            col = tmp("col", [128, 12])
            step2 = tmp("step2", [128, 2], I32)
            diag = tmp("diag", [128, 2, 128])
            xt = [tmp(f"xt{s}", [P5, 5, D]) for s in range(2)]
            xh = [tmp(f"xh{s}", [P5, 5, D]) for s in range(2)]
            x5 = x[0:N_NODES, :].rearrange("(i p j) c -> i p (j c)", p=P5, j=5)
            h5 = h_rows[0:N_NODES, :].rearrange("(i p j) c -> i p (j c)", p=P5, j=5)
            LN_T = N_NODES // (5 * P5)

            block = sc.enter_context(nc.Block())

            @block.sync
            def _(sp):
                sp.dma_start(dsti[:, :], edges[1, 0:N_EDGES].rearrange("(p c) -> p c", p=P5)).then_inc(dst_in, 16)
                for s in range(2):
                    sp.dma_start(xt[s][:, :, :].rearrange("p j c -> p (j c)"), x5[s]).then_inc(ln_in[s], 16)
                loads = [(wrr[:, :, :], w_rr.rearrange("(k p) n -> p k n", p=128)),
                         (wih[:, :, :], w_ihT.rearrange("(k p) n -> p k n", p=128)),
                         (wfc[:, :, :], w_fc.rearrange("(k p) n -> p k n", p=128)),
                         (wlr[:, :, :], w_lr.rearrange("(k p) n -> p k n", p=128)),
                         (weT[:, :], w_eT), (brel[:, :], b_rel), (bg1[:, :], b_ih), (bg2[:, :], b_hh),
                         (bfc[:, :], b_fc.partition_broadcast(128)), (blr[:, 0:D], b_l.partition_broadcast(128)),
                         (blr[:, D:2 * D], b_r.partition_broadcast(128)), (bout[:, :], bias.partition_broadcast(128)),
                         (attb[:, :], att.partition_broadcast(128))]
                for to, of in loads:
                    sp.dma_start(to, of).then_inc(setup_in, 16)
                sp.wait_ge(setup_c, 11)
                sp.dma_start(h_rows[N_NODES:N_PAD, :], padding[:, :]).then_inc(setup_in, 16)
                for h in range(HEADS):
                    sp.dma_start(attc[64 * (h % 2):64 * (h % 2) + 64, h // 2, h:h + 1],
                                 att[HD * h:HD * h + HD].rearrange("(c a) -> c a", a=1)).then_inc(setup_in, 16)
                for i in range(LN_T):
                    s = i % 2
                    sp.wait_ge(ln_v, i + 1)
                    sp.dma_start(h5[i], xh[s][:, :, :].rearrange("p j c -> p (j c)")).then_inc(ln_out[s], 16)
                    if i + 2 < LN_T:
                        sp.dma_start(xt[s][:, :, :].rearrange("p j c -> p (j c)"), x5[i + 2]).then_inc(ln_in[s], 16)
                sp.wait_ge(setup_t, 1)
                sp.dma_start(step_list, step2[:, :]).then_inc(table_out, 16)
                sp.wait_ge(table_out, 16)
                sp.dma_start(table[:, 0:2 * TABLE], step_list.rearrange("(a n) c -> a (n c)", a=1)).then_inc(table_in, 16)
                sp.wait_ge(table_in, 16)
                sp.wait_ge(setup_in, 16 * 18)
                for s in range(2):
                    sp.wait_ge(ln_out[s], 16 * (LN_T // 2))

            @block.gpsimd
            def _(pool):
                pool.memset(small[:, :], 0.0).then_inc(setup_c, 1)
                pool.memset(ident[:, :], 0.0).then_inc(setup_c, 1)
                pool.memset(ones[:, :], 1.0).then_inc(setup_c, 1)
                pool.memset(idx_all[:, :], 0).then_inc(setup_c, 1)
                pool.memset(attc[:, :, :], 0.0).then_inc(setup_c, 1)
                pool.memset(eri[0][:, :], 0).then_inc(setup_c, 1)
                pool.memset(eri[1][:, :], 0).then_inc(setup_c, 1)
                pool.memset(padding[:, :], 0.0).then_inc(setup_c, 1)
                pool.memset(table[:, :], 0).then_inc(setup_c, 1)
                pool.memset(baseT[:, :], 0.0).then_inc(setup_c, 1)
                pool.memset(keepT[:, :], 0.0).then_inc(setup_c, 1)
                pool.iota(iota_n[:, :], pattern=[[1, 128]], base=0, channel_multiplier=0,
                          allow_small_or_imprecise_dtypes=True).then_inc(setup_c, 1)
                pool.iota(iota_p[:, :], pattern=[[0, 1]], base=0, channel_multiplier=1,
                          allow_small_or_imprecise_dtypes=True).then_inc(setup_c, 1)
                pool.iota(thr[:, :], pattern=[[STEP_E, ROUNDS]], base=STEP_E, channel_multiplier=0,
                          allow_small_or_imprecise_dtypes=True).then_inc(setup_c, 1)
                pool.wait_ge(setup_c, 14)
                pool.affine_select(out=ident[:, :], in_=ident[:, :], compare_op=ALU.not_equal, fill=1.0,
                                   base=0, pattern=[[-1, 128]], channel_multiplier=1).then_inc(setup_c, 1)

            @block.tensor
            def _(pe):
                pe.wait_ge(setup_c, 15)
                pe.wait_ge(counts_ps, 1)
                pe.matmul(bk[0][:, 0:TILES + 1], ones[0:P5, :], part[0:P5, :], start=True, stop=True).then_inc(counts_ps, 1)
                pe.wait_ge(counts_ps, 3)
                pe.matmul(bk[1][:, 0:256], ones[:, :], diag[:, :, :], start=True, stop=True).then_inc(counts_ps, 1)

            @block.vector
            def _(v):
                signals = Count()

                v.wait_ge(dst_in, 16)
                v.wait_ge(setup_c, 15)
                v.tensor_copy(dstf[:, :], dsti[:, :]).then_inc(setup_v, 1)
                v.wait_ge(setup_v, signals.one_more())
                v.memset(part[:, 0:1], 0.0)
                for t in range(1, TILES):
                    v.tensor_scalar(junk[:, :], dstf[:, :], float(TN * t), 0.0, ALU.is_lt, ALU.add,
                                    accum_out=part[0:P5, t:t + 1]).then_inc(setup_v, 1)
                    v.wait_ge(setup_v, signals.one_more())
                v.memset(part[0:P5, TILES:TILES + 1], float(N_EDGES // P5)).then_inc(counts_ps, 1)
                for i in range(LN_T):
                    s = i % 2
                    v.wait_ge(ln_in[s], 16 * (i // 2 + 1))
                    if i >= 2:
                        v.wait_ge(ln_v, i - 1)
                    for j in range(5):
                        ins = v.bn_stats(small[0:P5, 6 * j:6 * j + 6], xt[s][:, j, :])
                    ins.then_inc(setup_v, 1)
                    v.wait_ge(setup_v, signals.one_more())
                    for j in range(5):
                        ins = v.bn_aggr(small[0:P5, 32 + 2 * j:34 + 2 * j], small[0:P5, 6 * j:6 * j + 6])
                    ins.then_inc(setup_v, 1)
                    v.wait_ge(setup_v, signals.one_more())
                    mv = small[0:P5, 32:42].rearrange("p (j a) -> p j a", a=2)
                    v.tensor_scalar(small[0:P5, 48:53], mv[:, :, 1], EPS, None, ALU.add).then_inc(ln_var, 1)
                    v.wait_ge(ln_std, i + 1)
                    v.reciprocal(rstd[:, 5 * s:5 * s + 5], small[0:P5, 42:47]).then_inc(setup_v, 1)
                    v.wait_ge(setup_v, signals.one_more())
                    v.scalar_tensor_tensor(out=shift[:, 5 * s:5 * s + 5], in0=mv[:, :, 0], scalar=-1.0,
                                           in1=rstd[:, 5 * s:5 * s + 5], op0=ALU.mult, op1=ALU.mult).then_inc(ln_scale, 1)
                v.wait_ge(counts_ps, 2)
                v.tensor_copy(counted[:, :], bk[0][:, 0:TILES + 1]).then_inc(setup_v, 1)
                v.wait_ge(setup_v, signals.one_more())
                v.tensor_tensor(cnt[:, :], counted[:, 1:TILES + 1], counted[:, 0:TILES], ALU.subtract).then_inc(setup_v, 1)
                v.wait_ge(setup_v, signals.one_more())
                v.tensor_tensor(over[:, :, :], cnt[:, :].unsqueeze(2).broadcast_to([128, TILES, ROUNDS]),
                                thr[:, :].unsqueeze(1).broadcast_to([128, TILES, ROUNDS]), ALU.is_gt).then_inc(setup_v, 1)
                v.wait_ge(setup_v, signals.one_more())
                v.tensor_reduce(rnd[:, :], over[:, :, :], AX.X, ALU.add).then_inc(setup_v, 1)
                v.wait_ge(setup_v, signals.one_more())
                v.tensor_scalar(rnd[:, :], rnd[:, :], 1.0, None, ALU.add).then_inc(setup_v, 1)
                v.wait_ge(setup_v, signals.one_more())
                v.memset(zero[:, :], 0.0).then_inc(setup_v, 1)
                v.wait_ge(setup_v, signals.one_more())
                v.tensor_tensor_scan(cum[:, :], rnd[:, :], zero[:, :], 0.0, ALU.add, ALU.add).then_inc(setup_v, 1)
                v.wait_ge(setup_v, signals.one_more())
                v.tensor_scalar(cmp[:, :], cum[:, :], iota_p[:, 0:1], None, ALU.is_le).then_inc(setup_v, 1)
                v.wait_ge(setup_v, signals.one_more())
                v.tensor_reduce(col[:, 0:1], cmp[:, :], AX.X, ALU.add).then_inc(setup_v, 1)
                v.wait_ge(setup_v, signals.one_more())
                v.tensor_scalar(col[:, 1:2], col[:, 0:1], float(TILES - 1), None, ALU.min).then_inc(setup_v, 1)
                v.wait_ge(setup_v, signals.one_more())
                v.tensor_scalar(sel[:, :], iota_n[:, 0:TILES], col[:, 1:2], None, ALU.is_equal).then_inc(setup_v, 1)
                v.wait_ge(setup_v, signals.one_more())
                v.tensor_tensor(cmp[:, :], cum[:, :], rnd[:, :], ALU.subtract).then_inc(setup_v, 1)
                v.wait_ge(setup_v, signals.one_more())
                v.tensor_tensor(cmp[:, :], cmp[:, :], sel[:, :], ALU.mult).then_inc(setup_v, 1)
                v.wait_ge(setup_v, signals.one_more())
                v.tensor_reduce(col[:, 2:3], cmp[:, :], AX.X, ALU.add).then_inc(setup_v, 1)
                v.wait_ge(setup_v, signals.one_more())
                v.tensor_tensor(sel[:, :], sel[:, :], counted[:, 0:TILES], ALU.mult).then_inc(setup_v, 1)
                v.wait_ge(setup_v, signals.one_more())
                v.tensor_reduce(col[:, 3:4], sel[:, :], AX.X, ALU.add).then_inc(setup_v, 1)
                v.wait_ge(setup_v, signals.one_more())
                v.tensor_tensor(col[:, 4:5], iota_p[:, 0:1], col[:, 2:3], ALU.subtract).then_inc(setup_v, 1)
                v.wait_ge(setup_v, signals.one_more())
                v.tensor_scalar(col[:, 5:6], col[:, 4:5], 0.0, None, ALU.is_gt).then_inc(setup_v, 1)
                v.wait_ge(setup_v, signals.one_more())
                v.tensor_scalar(col[:, 6:7], col[:, 4:5], float(STEP_E), None, ALU.mult).then_inc(setup_v, 1)
                v.wait_ge(setup_v, signals.one_more())
                v.tensor_tensor(col[:, 6:7], col[:, 6:7], col[:, 3:4], ALU.add).then_inc(setup_v, 1)
                v.wait_ge(setup_v, signals.one_more())
                v.tensor_scalar(col[:, 6:7], col[:, 6:7], float(N_EDGES), None, ALU.min).then_inc(setup_v, 1)
                v.wait_ge(setup_v, signals.one_more())
                v.tensor_scalar(col[:, 7:8], col[:, 1:2], float(TN), None, ALU.mult).then_inc(setup_v, 1)
                v.wait_ge(setup_v, signals.one_more())
                v.tensor_copy(step2[:, :], col[:, 6:8]).then_inc(setup_v, 1)
                v.wait_ge(setup_v, signals.one_more())
                v.tensor_scalar(diag[:, 0, :], ident[:, :], col[:, 7:8], None, ALU.mult).then_inc(setup_v, 1)
                v.wait_ge(setup_v, signals.one_more())
                v.tensor_scalar(diag[:, 1, :], ident[:, :], col[:, 5:6], None, ALU.mult).then_inc(counts_ps, 1)
                v.tensor_scalar(junk[0:1, 0:64], iota_n[0:1, 0:64], 4.0, None, ALU.mult).then_inc(setup_v, 1)
                v.wait_ge(setup_v, signals.one_more())
                v.tensor_scalar(junk[0:1, 0:64], junk[0:1, 0:64], cum[0:1, TILES - 1:TILES], None, ALU.is_lt).then_inc(setup_v, 1)
                v.wait_ge(setup_v, signals.one_more())
                v.tensor_reduce(col[0:1, 8:9], junk[0:1, 0:64], AX.X, ALU.add).then_inc(setup_v, 1)
                v.wait_ge(setup_v, signals.one_more())
                v.tensor_scalar(n_pairs[:, 0:1], col[0:1, 8:9], 2.0, -1.0, ALU.mult, ALU.add).then_inc(setup_t, 1)
                v.wait_ge(counts_ps, 4)
                v.tensor_copy(baseT[:, 0:TABLE], bk[1][:, 0:128])
                v.tensor_copy(keepT[:, 0:TABLE], bk[1][:, 128:256])
                v.wait_ge(setup_in, 16 * 18)
                v.tensor_tensor(bg[:, :], bg1[:, :], bg2[:, :], ALU.add).then_inc(setup_t, 1)

            @block.scalar
            def _(act):
                for i in range(LN_T):
                    act.wait_ge(ln_var, i + 1)
                    act.activation(small[0:P5, 42:47], small[0:P5, 48:53], ACT.Sqrt).then_inc(ln_std, 1)
                    s = i % 2
                    act.wait_ge(ln_scale, i + 1)
                    if i >= 2:
                        act.wait_ge(ln_out[s], 16 * (i // 2))
                    for j in range(5):
                        ins = act.activation(xh[s][:, j, :], xt[s][:, j, :], ACT.Relu, bias=shift[:, 5 * s + j:5 * s + j + 1],
                                             scale=rstd[:, 5 * s + j:5 * s + j + 1])
                    ins.then_inc(ln_v, 1)

        er_v = stage_sem(ctx, "er_v", "vector")
        er_ps = stage_sem(ctx, "er_ps", "tensor")
        with nc.Block() as block:
            def edge_rows(a0, first_edge):
                return edges[a0:2, bass.ds(first_edge, STEP_E)].rearrange("a (k e) -> a k e", e=128)

            def load_edges(eng, i, q):
                for n in range(4):
                    e0 = eng.value_load(table[0:1, bass.ds(i * 4 + 8 * q + 2 * n, 1)], min_val=0, max_val=N_EDGES)
                    if n == 0:
                        eng.wait_ge(er_v, i + 1)
                        eng.sem_inc(passed, 1)
                    row = 2 * KT * n
                    eng.dma_start(eri[q][row:row + 2 * KT, :], edge_rows(0, e0)).then_inc(er_in[q], 16)

            @block.sync
            def _(sp):
                start(sp, "sync")
                last_i = sp.value_load(n_pairs[0:1, 0:1], min_val=1, max_val=LAST_MAX)
                with sp.Fori(0, last_i + 1, 4) as i:
                    load_edges(sp, i, 0)

            @block.scalar
            def _(act):
                start(act, "scalar")
                last_i = act.value_load(n_pairs[0:1, 0:1], min_val=1, max_val=LAST_MAX)
                with act.Fori(0, last_i + 1, 4) as i:
                    load_edges(act, i, 1)

            @block.vector
            def _(v):
                start(v, "vector")
                last_i = v.value_load(n_pairs[0:1, 0:1], min_val=1, max_val=LAST_MAX)
                pairs = last_i + 1
                with v.Fori(0, pairs, 4) as i:
                    for q in range(2):
                        v.wait_ge(er_in[q], i * 16 + 64)
                        v.wait_ge(er_v, i + 2 * q + 1)
                        v.tensor_copy(erf[q][:, :], eri[q][:, :]).then_inc(er_v, 1)
                        v.wait_ge(er_ps, i + 2 * q + 3)
                        v.tensor_copy(idx_all[:, bass.ds(i * (4 * KT) + q * 8 * KT, 8 * KT)],
                                      bk[q][:, 0:8 * KT]).then_inc(er_v, 1)

            @block.tensor
            def _(pe):
                start(pe, "tensor")
                last_i = pe.value_load(n_pairs[0:1, 0:1], min_val=1, max_val=LAST_MAX)
                pairs = last_i + 1
                with pe.Fori(0, pairs, 4) as i:
                    for q in range(2):
                        pe.wait_ge(er_v, i + 2 * q + 2)
                        pe.sem_inc(passed, 1)
                        for half in range(2):
                            cols = slice(4 * KT * half, 4 * KT * half + 4 * KT)
                            pe.matmul(bk[q][:, cols], erf[q][:, :], ident[0:8 * KT, cols], start=True, stop=True).then_inc(er_ps, 1)

        with ExitStack() as sc:
            def tmp(name, shape, dt=F32):
                return sc.enter_context(nc.sbuf_tensor(name, shape, dt))

            def dma_sem(name):
                return sc.enter_context(nc.semaphore(name))

            hin = [tmp(f"hin{s}", [TN, D]) for s in range(2)]
            xin = [tmp(f"xin{s}", [TN, D]) for s in range(2)]
            rows_hi = [tmp(f"rows_hi{s}", [128, KT, AW], F32R) for s in range(2)]
            rows_lo = [tmp(f"rows_lo{s}", [128, KT, AW], F32R) for s in range(2)]
            agg = [tmp(f"agg{s}", [TN, AW]) for s in range(2)]
            mean = [tmp(f"mean{s}", [TN, ED]) for s in range(2)]
            meanT = [tmp(f"meanT{s}", [ED, TN]) for s in range(2)]
            xT = tmp("xT", [128, 4, 2 * TN])
            h1T = tmp("h1T", [128, NJ, 2 * TN])
            gate = [[tmp(f"gate{g}{b}", [128, 2 * TN]) for b in range(2)] for g in "igotc"]
            lstmT = tmp("lstmT", [128, NJ, 2 * TN])
            x1 = [tmp(f"x1{s}", [TN, D]) for s in range(2)]
            h2 = [tmp(f"h2{s}", [TN, D]) for s in range(2)]
            h2T = [tmp(f"h2T{s}", [128, 2, TN]) for s in range(2)]
            xl = [tmp(f"xl{s}", [TN, D]) for s in range(2)]
            rec = [tmp(f"rec{s}", [TN, RECW]) for s in range(2)]
            ss = tmp("ss", [TN, D])
            sk = tmp("sk", [TN, D])

            idx_ready = stage_sem(sc, "idx_ready", "vector")
            norm_v = stage_sem(sc, "norm_v", "vector")
            scale_v = stage_sem(sc, "scale_v", "vector")
            node_v = stage_sem(sc, "node_v", "vector")
            loaded = [dma_sem(f"loaded{s}") for s in range(2)]
            x_loaded = [dma_sem(f"x_loaded{s}") for s in range(2)]
            hi_ready = stage_sem(sc, "hi_ready", "scalar")
            lo_ready = stage_sem(sc, "lo_ready", "vector")
            hot = stage_sem(sc, "hot", "vector")
            agg_ps = stage_sem(sc, "agg_ps", "tensor")
            agg_sb = stage_sem(sc, "agg_sb", "vector")
            xT_ps = stage_sem(sc, "xT_ps", "tensor")
            xT_sb = stage_sem(sc, "xT_sb", "scalar")
            meanT_sb = stage_sem(sc, "meanT_sb", "scalar")
            h1_ps = stage_sem(sc, "h1_ps", "tensor")
            h1_sb = stage_sem(sc, "h1_sb", "scalar")
            gate_ps = stage_sem(sc, "gate_ps", "tensor")
            gate_ig = stage_sem(sc, "gate_ig", "scalar")
            gate_to = stage_sem(sc, "gate_to", "scalar")
            cell = stage_sem(sc, "cell", "vector")
            lstm_sb = stage_sem(sc, "lstm_sb", "vector")
            fc_ps = stage_sem(sc, "fc_ps", "tensor")
            var_sb = stage_sem(sc, "var_sb", "vector")
            std_sb = stage_sem(sc, "std_sb", "scalar")
            h2_sb = stage_sem(sc, "h2_sb", "vector")
            h2T_ps = stage_sem(sc, "h2T_ps", "tensor")
            h2T_sb = stage_sem(sc, "h2T_sb", "scalar")
            xlr_ps = stage_sem(sc, "xlr_ps", "tensor")
            node_out = stage_sem(sc, "node_out", "vector")
            ones_ready = dma_sem("ones_ready")
            stored = dma_sem("stored")
            stored_steps = stage_sem(sc, "stored_steps", "sync")
            block = sc.enter_context(nc.Block())

            @block.sync
            def _(sp):
                start(sp, "sync")
                last_i = sp.value_load(n_pairs[0:1, 0:1], min_val=1, max_val=LAST_MAX)
                pairs = last_i + 1

                def load(i, s):
                    e0 = sp.value_load(table[0:1, bass.ds(i * 4 + 2 * s, 1)], min_val=0, max_val=N_EDGES)
                    v0 = sp.value_load(table[0:1, bass.ds(i * 4 + 2 * s + 1, 1)], min_val=0, max_val=LAST_BASE)
                    sp.dma_start(rows0[s][:, :, D:D + ED], attr[bass.ds(e0, STEP_E), :].rearrange("(k p) c -> p k c", p=128)).then_inc(loaded[s], 16)
                    sp.dma_start(hin[s][:, :], h_rows[bass.ds(v0, TN), :]).then_inc(loaded[s], 16)

                def load_x(i, s):
                    v0 = sp.value_load(table[0:1, bass.ds(i * 4 + 2 * s + 1, 1)], min_val=0, max_val=LAST_BASE)
                    sp.dma_start(xin[s][:, :], x[bass.ds(v0, TN), :]).then_inc(x_loaded[s], 16)

                for s in range(2):
                    load(0, s)
                    load_x(0, s)
                sp.sem_inc(stored_steps, 1)
                with sp.Fori(0, pairs) as i:
                    for s in range(2):
                        sp.wait_ge(xT_ps, i * 2 + s + 2)
                        sp.sem_inc(passed, 1)
                        load(i + 1, s)
                    for s in range(2):
                        v0 = sp.value_load(table[0:1, bass.ds(i * 4 + 2 * s + 1, 1)], min_val=0, max_val=LAST_BASE)
                        sp.wait_ge(node_out, i * 2 + s + 2)
                        sp.sem_inc(passed, 1)
                        sp.dma_start(xl_rows[bass.ds(v0, TN), :], xl[s][:, :]).then_inc(stored, 16)
                        sp.dma_start(node_rec[bass.ds(v0, TN), :], rec[s][:, :]).then_inc(stored, 16)
                        load_x(i + 1, s)
                        sp.wait_ge(stored, i * 64 + 32 * s + 32)
                        sp.sem_inc(passed, 1)
                        sp.sem_inc(stored_steps, 1)
                for s in range(2):
                    sp.wait_ge(loaded[s], pairs * 32 + 32)
                    sp.sem_inc(passed, 1)
                    sp.wait_ge(x_loaded[s], pairs * 16 + 16)
                    sp.sem_inc(passed, 1)

            @block.gpsimd
            def _(pool):
                last_i = pool.value_load(n_pairs[0:1, 0:1], min_val=1, max_val=LAST_MAX)
                pairs = last_i + 1
                with pool.Fori(0, pairs) as i:
                    for s in range(2):
                        pool.wait_ge(idx_ready, i * 2 + s + 2)
                        pool.sem_inc(passed, 1)
                        for k in range(KT):
                            pool.indirect_dma_start(rows0[s][:, k, 0:D], None, h_rows,
                                                    bass.IndirectOffsetOnAxis(ap=idx[s][:, k:k + 1], axis=0)
                                                    ).then_inc(gathered[s], 16)

            def pairs_of_steps(eng, last_i, first, body):
                first(0)
                with eng.Fori(0, last_i) as i:
                    body(i, i + 1)
                body(last_i, None)

            @block.tensor
            def _(pe):
                start(pe, "tensor")
                last_i = pe.value_load(n_pairs[0:1, 0:1], min_val=1, max_val=LAST_MAX)

                def sum_edges(i, s):
                    pe.wait_ge(hot, i * 4 + 2 * s + 3)
                    pe.wait_ge(lo_ready, i * 2 + s + 2)
                    pe.wait_ge(meanT_sb, i * 2 + 1)
                    for k in range(KT):
                        hot_k = onehot[s][:, k, 0:TN].bitcast(F32R)
                        pe.matmul(bk[s][0:TN, 0:AW], hot_k, rows_hi[s][:, k, :], start=(k == 0), stop=False)
                        m = pe.matmul(bk[s][0:TN, 0:AW], hot_k, rows_lo[s][:, k, :], start=False, stop=(k == KT - 1))
                    m.then_inc(agg_ps, 1)

                def turn_x(i, s):
                    pe.wait_ge(loaded[s], i * 32 + 32)
                    pe.wait_ge(agg_sb, i * 8 + 4 * s + 5)
                    for c in range(2):
                        pe.transpose(bk[s][:, TN * c:TN * c + TN], agg[s][:, 128 * c:128 * c + 128], ident[0:TN, 0:TN])
                        pe.transpose(bk[s][:, TN * (2 + c):TN * (3 + c)], hin[s][:, 128 * c:128 * c + 128], ident[0:TN, 0:TN])
                    pe.transpose(bk[s][0:ED, TN * 4:TN * 5], mean[s][:, :], ident[0:TN, 0:TN]).then_inc(xT_ps, 1)

                def hidden(i):
                    pe.wait_ge(xT_sb, i * 2 + 3)
                    for f in range(NJ):
                        if f >= 2:
                            pe.wait_ge(h1_sb, i * NJ + f)
                        for c in range(4):
                            m = pe.matmul(bk[2 + f % 2][:, 0:2 * TN], wrr[:, c, 128 * f:128 * f + 128], xT[:, c, :],
                                          start=(c == 0), stop=(c == 3))
                        m.then_inc(h1_ps, 1)

                def gates(i):
                    pe.wait_ge(h1_sb, i * NJ + NJ + 1)
                    pe.wait_ge(node_v, i * 12 + 1)
                    for j in range(NJ):
                        if j >= 2:
                            pe.wait_ge(gate_to, i * NJ + j)
                        for g, to in enumerate((bk[4 + j % 2][:, 0:2 * TN], bk[4 + j % 2][:, 256:256 + 2 * TN],
                                                bk[6 + j % 2][:, 0:2 * TN])):
                            for f in range(NJ):
                                m = pe.matmul(to, wih[:, f, DH * g + 128 * j:DH * g + 128 * j + 128], h1T[:, f, :],
                                              start=(f == 0), stop=(f == NJ - 1))
                        m.then_inc(gate_ps, 1)

                def output(i, s):
                    pe.wait_ge(lstm_sb, i * NJ + NJ + 1)
                    for j in range(NJ):
                        m = pe.matmul(bk[4 + s][0:TN, 0:D], lstmT[:, j, TN * s:TN * s + TN], wfc[:, j, :],
                                      start=(j == 0), stop=(j == NJ - 1))
                    m.then_inc(fc_ps, 1)

                def turn_h2(i, s):
                    pe.wait_ge(h2_sb, i * 2 + s + 2)
                    for c in range(2):
                        m = pe.transpose(bk[6 + s][:, TN * c:TN * c + TN], h2[s][:, 128 * c:128 * c + 128], ident[0:TN, 0:TN])
                    m.then_inc(h2T_ps, 1)

                def project(i, s):
                    pe.wait_ge(h2T_sb, i * 2 + s + 2)
                    for c in range(2):
                        pe.matmul(bk[4 + s][0:TN, 0:2 * D], h2T[s][:, c, :], wlr[:, c, :], start=(c == 0), stop=(c == 1))
                    pe.matmul(bk[6 + s][0:TN, 0:D], meanT[s][:, :], weT[:, :], start=True, stop=True).then_inc(xlr_ps, 1)

                def first(i):
                    for stage in (sum_edges, turn_x):
                        for s in range(2):
                            stage(i, s)

                def body(i, n):
                    hidden(i)
                    gates(i)
                    if n is not None:
                        sum_edges(n, 0)
                    for s in range(2):
                        output(i, s)
                    if n is not None:
                        sum_edges(n, 1)
                    for s in range(2):
                        turn_h2(i, s)
                    if n is not None:
                        for s in range(2):
                            turn_x(n, s)
                    for s in range(2):
                        project(i, s)

                pairs_of_steps(pe, last_i, first, body)

            @block.scalar
            def _(act):
                start(act, "scalar")
                last_i = act.value_load(n_pairs[0:1, 0:1], min_val=1, max_val=LAST_MAX)
                gi, gg, go, gt, gc = gate

                def take_hi(i, s):
                    act.wait_ge(gathered[s], i * (16 * KT) + 16 * KT)
                    act.wait_ge(loaded[s], i * 32 + 32)
                    act.wait_ge(ones_ready, 1)
                    act.wait_ge(agg_ps, i * 2 + 1)
                    act.activation(rows_hi[s][:, :, :], rows0[s][:, :, :], ACT.Copy).then_inc(hi_ready, 1)

                def take_x(i, s):
                    act.wait_ge(xT_ps, i * 2 + s + 2)
                    act.activation(xT[:, :, TN * s:TN * s + TN],
                                   bk[s][:, 0:4 * TN].rearrange("p (c n) -> p c n", c=4), ACT.Copy).then_inc(xT_sb, 1)

                def take_mean(i, s):
                    act.wait_ge(xlr_ps, i * 2 + 1)
                    act.activation(meanT[s][:, :], bk[s][0:ED, TN * 4:TN * 5], ACT.Copy).then_inc(meanT_sb, 1)

                def first(i):
                    for stage in (take_hi, take_x, take_mean):
                        for s in range(2):
                            stage(i, s)

                def body(i, n):
                    for f in range(NJ):
                        act.wait_ge(h1_ps, i * NJ + f + 2)
                        act.activation(h1T[:, f, :], bk[2 + f % 2][:, 0:2 * TN], ACT.Relu, bias=brel[:, f:f + 1]).then_inc(h1_sb, 1)
                    for j in range(NJ):
                        b = j % 2
                        act.wait_ge(gate_ps, i * NJ + j + 2)
                        act.wait_ge(lstm_sb, i * NJ + max(j - 1, 0) + 1)
                        act.activation(gi[b][:, :], bk[4 + b][:, 0:2 * TN], ACT.Sigmoid, bias=bg[:, j:j + 1])
                        act.activation(gg[b][:, :], bk[4 + b][:, 256:256 + 2 * TN], ACT.Tanh, bias=bg[:, NJ + j:NJ + j + 1]).then_inc(gate_ig, 1)
                        act.activation(go[b][:, :], bk[6 + b][:, 0:2 * TN], ACT.Sigmoid, bias=bg[:, 2 * NJ + j:2 * NJ + j + 1])
                        act.wait_ge(cell, i * NJ + j + 2)
                        act.activation(gt[b][:, :], gc[b][:, :], ACT.Tanh).then_inc(gate_to, 1)
                        if n is not None and j in (0, 2):
                            take_hi(n, j // 2)
                    act.wait_ge(var_sb, i * 2 + 3)
                    for s in range(2):
                        ins = act.activation(stats[s][0:TN, 9:10], stats[s][0:TN, 8:9], ACT.Sqrt)
                    ins.then_inc(std_sb, 1)
                    for s in range(2):
                        act.wait_ge(h2T_ps, i * 2 + s + 2)
                        act.activation(h2T[s][:, :, :], bk[6 + s][:, 0:2 * TN].rearrange("p (c n) -> p c n", c=2), ACT.Copy).then_inc(h2T_sb, 1)
                    if n is not None:
                        for stage in (take_x, take_mean):
                            for s in range(2):
                                stage(n, s)

                pairs_of_steps(act, last_i, first, body)

            @block.vector
            def _(v):
                start(v, "vector")
                last_i = v.value_load(n_pairs[0:1, 0:1], min_val=1, max_val=LAST_MAX)
                pairs = last_i + 1
                gi, gg, go, gt, gc = gate

                def indices(i, s):
                    v.tensor_copy(idx[s][:, :], idx_all[:, bass.ds(i * (4 * KT) + s * 2 * KT, KT)]).then_inc(idx_ready, 1)

                def one_hot(i, s):
                    v.wait_ge(hot, i * 4 + 2 * s + 1)
                    v.tensor_scalar(drel[:, :], idx_all[:, bass.ds(i * (4 * KT) + s * 2 * KT + KT, KT)],
                                    baseT[:, bass.ds(i * 2 + s, 1)], None, ALU.subtract).then_inc(hot, 1)
                    v.wait_ge(hot, i * 4 + 2 * s + 2)
                    v.tensor_tensor(onehot[s][:, :, 0:TN].bitcast(F32R), iota_n[:, 0:TN].unsqueeze(1).broadcast_to([128, KT, TN]),
                                    drel[:, :].unsqueeze(2).broadcast_to([128, KT, TN]), ALU.is_equal).then_inc(hot, 1)

                for s in range(2):
                    indices(0, s)
                v.memset(rows0[0][:, :, D + ED:AW], 1.0)
                v.memset(rows0[1][:, :, D + ED:AW], 1.0).then_inc(ones_ready, 1)
                v.memset(agg[1][:, :], 0.0)

                def hot_of(i):
                    for s in range(2):
                        v.wait_ge(agg_ps, i * 2 + 1)
                        one_hot(i, s)

                def take_lo(i, s):
                    v.wait_ge(hi_ready, i * 2 + s + 2)
                    v.tensor_tensor(rows_lo[s][:, :, :], rows0[s][:, :, :], rows_hi[s][:, :, :], ALU.subtract).then_inc(lo_ready, 1)
                    indices(i + 1, s)

                def take_sums(i, s):
                    v.wait_ge(agg_ps, i * 2 + s + 2)
                    v.wait_ge(xT_ps, i * 2 + 1)
                    v.wait_ge(agg_sb, i * 8 + 4 * s + 1)
                    v.scalar_tensor_tensor(out=agg[s][:, :], in0=agg[1 - s][:, :], scalar=keepT[0:TN, bass.ds(i * 2 + s, 1)],
                                           in1=bk[s][0:TN, 0:AW], op0=ALU.mult, op1=ALU.add).then_inc(agg_sb, 1)
                    v.wait_ge(agg_sb, i * 8 + 4 * s + 2)
                    v.tensor_scalar(small[0:TN, 1:2], agg[s][:, AW - 1:AW], 1.0, None, ALU.max).then_inc(agg_sb, 1)
                    v.wait_ge(agg_sb, i * 8 + 4 * s + 3)
                    v.reciprocal(small[0:TN, 0:1], small[0:TN, 1:2]).then_inc(agg_sb, 1)
                    v.wait_ge(agg_sb, i * 8 + 4 * s + 4)
                    v.tensor_scalar(mean[s][:, :], agg[s][:, D:D + ED], small[0:TN, 0:1], None, ALU.mult).then_inc(agg_sb, 1)

                def first(i):
                    hot_of(i)
                    for s in range(2):
                        take_lo(i, s)
                    for s in range(2):
                        take_sums(i, s)

                def body(i, n):
                    if n is not None:
                        hot_of(n)
                    for j in range(NJ):
                        b = j % 2
                        v.wait_ge(gate_ig, i * NJ + j + 2)
                        v.tensor_tensor(gc[b][:, :], gi[b][:, :], gg[b][:, :], ALU.mult).then_inc(cell, 1)
                        v.wait_ge(gate_to, i * NJ + j + 2)
                        v.tensor_tensor(lstmT[:, j, :], go[b][:, :], gt[b][:, :], ALU.mult).then_inc(lstm_sb, 1)
                        if n is not None and j in (1, 3):
                            take_lo(n, j // 2)
                    for s in range(2):
                        v.wait_ge(norm_v, i * 8 + 4 * s + 1)
                        v.wait_ge(x_loaded[s], i * 16 + 16)
                        v.wait_ge(fc_ps, i * 2 + s + 2)
                        v.tensor_tensor(x1[s][:, :], bk[4 + s][0:TN, 0:D], xin[s][:, :], ALU.add).then_inc(norm_v, 1)
                        v.wait_ge(norm_v, i * 8 + 4 * s + 2)
                        v.tensor_tensor(x1[s][:, :], x1[s][:, :], bfc[0:TN, :], ALU.add).then_inc(norm_v, 1)
                        v.wait_ge(norm_v, i * 8 + 4 * s + 3)
                        v.bn_stats(stats[s][0:TN, 0:6], x1[s][:, :]).then_inc(norm_v, 1)
                        v.wait_ge(norm_v, i * 8 + 4 * s + 4)
                        v.sem_inc(passed, 1)
                        v.bn_aggr(stats[s][0:TN, 6:8], stats[s][0:TN, 0:6]).then_inc(norm_v, 1)
                        v.wait_ge(norm_v, i * 8 + 4 * s + 5)
                        v.tensor_scalar(stats[s][0:TN, 8:9], stats[s][0:TN, 7:8], EPS, None, ALU.add).then_inc(var_sb, 1)
                    for s in range(2):
                        v.wait_ge(scale_v, i * 4 + 2 * s + 1)
                        v.wait_ge(std_sb, i + 2)
                        v.wait_ge(stored_steps, i * 2 + s + 1)
                        v.reciprocal(stats[s][0:TN, 10:11], stats[s][0:TN, 9:10]).then_inc(scale_v, 1)
                        v.wait_ge(scale_v, i * 4 + 2 * s + 2)
                        v.tensor_scalar(h2[s][:, :], x1[s][:, :], stats[s][0:TN, 6:7], stats[s][0:TN, 10:11], ALU.subtract, ALU.mult).then_inc(scale_v, 1)
                        v.wait_ge(scale_v, i * 4 + 2 * s + 3)
                        v.tensor_scalar(h2[s][:, :], h2[s][:, :], 0.0, None, ALU.max).then_inc(h2_sb, 1)
                        v.wait_ge(h2_sb, i * 2 + s + 2)
                        v.tensor_tensor(rec[s][:, D:2 * D], x1[s][:, :], h2[s][:, :], ALU.add)
                    if n is not None:
                        for s in range(2):
                            take_sums(n, s)
                    for s in range(2):
                        v.wait_ge(node_v, i * 12 + 6 * s + 1)
                        v.wait_ge(xlr_ps, i * 2 + s + 2)
                        v.tensor_tensor(xl[s][:, :], bk[4 + s][0:TN, 0:D], blr[0:TN, 0:D], ALU.add).then_inc(node_v, 1)
                        v.tensor_tensor(rec[s][:, 0:D], bk[4 + s][0:TN, D:2 * D], blr[0:TN, D:2 * D], ALU.add).then_inc(node_v, 1)
                        v.wait_ge(node_v, i * 12 + 6 * s + 3)
                        v.tensor_tensor(ss[:, :], xl[s][:, :], rec[s][:, 0:D], ALU.add).then_inc(node_v, 1)
                        v.wait_ge(node_v, i * 12 + 6 * s + 4)
                        v.tensor_tensor(ss[:, :], bk[6 + s][0:TN, 0:D], ss[:, :], ALU.add).then_inc(node_v, 1)
                        v.wait_ge(node_v, i * 12 + 6 * s + 5)
                        v.scalar_tensor_tensor(out=sk[:, :], in0=ss[:, :], scalar=0.2, in1=ss[:, :], op0=ALU.mult, op1=ALU.max).then_inc(node_v, 1)
                        v.wait_ge(node_v, i * 12 + 6 * s + 6)
                        v.tensor_tensor(sk[:, :], sk[:, :], attb[0:TN, :], ALU.mult).then_inc(node_v, 1)
                        v.wait_ge(node_v, i * 12 + 6 * s + 7)
                        v.tensor_reduce(rec[s][:, 2 * D:RECW], sk[:, :].rearrange("p (h c) -> p h c", h=HEADS), AX.X, ALU.add).then_inc(node_out, 1)

                pairs_of_steps(v, last_i, first, body)

        early.close()
        with ExitStack() as sc:
            def tmp(name, shape, dt=F32):
                return sc.enter_context(nc.sbuf_tensor(name, shape, dt))

            def dma_sem(name):
                return sc.enter_context(nc.semaphore(name))

            RW = 5 * KT
            dst85 = [tmp(f"dst85{s}", [RW, 128], I32) for s in range(2)]
            xr_we = [tmp(f"xr_we{s}", [128, D]) for s in range(2)]
            xw_hi = [tmp(f"xw_hi{s}", [128, D], F32R) for s in range(2)]
            xw_lo = [tmp(f"xw_lo{s}", [128, D], F32R) for s in range(2)]
            attr1 = [tmp(f"attr1{s}", [128, KT, ED]) for s in range(2)]
            xo = [tmp(f"xo{s}", [TN, D]) for s in range(2)]
            ro = [tmp(f"ro{s}", [TN, D + HEADS]) for s in range(2)]
            hotT = [tmp(f"hotT{s}", [128, STEP_E], F32R) for s in range(2)]
            relu8 = [tmp(f"relu8{b}", [128, 2, 512]) for b in range(2)]
            leaky = [tmp(f"leaky{b}", [128, 2, 512]) for b in range(2)]
            rows1 = [r[:, 0:KT * XW].rearrange("p (k c) -> p k c", k=KT) for r in rows]
            rows1 += [tmp(f"rows{r}", [128, KT, XW]) for r in (2, 3)]
            onehot4 = onehot + [tmp(f"onehot{r}", [128, KT, 128]) for r in (2, 3)]
            idx4 = [tmp(f"idx4{r}", [128, KT], I32) for r in range(4)]
            score = tmp("score", [128, 5, KT])
            begins = tmp("begins", [RW, 129])
            ends = tmp("ends", [RW, 128])
            runmax = tmp("runmax", [RW, 128])
            runT = tmp("runT", [128, 10, KT], F32R)
            pen = tmp("pen", [TN, KT])
            cand = tmp("cand", [TN, KT, HEADS])
            stepmax = tmp("stepmax", [TN, HEADS])
            prevmax = tmp("prevmax", [TN, HEADS])
            nmax = [tmp(f"nmax{s}", [TN, HEADS]) for s in range(2)]
            nmax_hl = tmp("nmax_hl", [TN, 2 * HEADS], F32R)
            gap = tmp("gap", [TN, HEADS])
            corr = tmp("corr", [TN, HEADS])
            expo = tmp("expo", [128, HEADS, KT])
            acc = [tmp(f"acc{s}", [TN, XW]) for s in range(2)]
            scaled = tmp("scaled", [TN, XW])
            selfm = tmp("selfm", [TN, HEADS])
            gap2 = tmp("gap2", [TN, 2, HEADS])
            c2 = tmp("c2", [TN, 2, HEADS])
            tot = tmp("tot", [TN, XW])
            own = tmp("own", [TN, D])
            rden = tmp("rden", [TN, HEADS])
            y = tmp("y", [TN, D])
            em = tmp("em", [TN, D])
            res = [tmp(f"res{s}", [TN, D]) for s in range(2)]

            silu_v = stage_sem(sc, "silu_v", "vector")
            loadedH = [dma_sem(f"loadedH{s}") for s in range(2)]
            loadedD = [dma_sem(f"loadedD{s}") for s in range(2)]
            loadedB = [dma_sem(f"loadedB{s}") for s in range(2)]
            gathered1 = [dma_sem(f"gathered1_{r}") for r in range(4)]
            idx_ready1 = stage_sem(sc, "idx_ready1", "vector")
            hot1 = stage_sem(sc, "hot1", "vector")
            hotT_ps = stage_sem(sc, "hotT_ps", "tensor")
            hotT_sb = stage_sem(sc, "hotT_sb", "scalar")
            s_ps = stage_sem(sc, "s_ps", "tensor")
            relu_sb = stage_sem(sc, "relu_sb", "scalar")
            leaky_sb = stage_sem(sc, "leaky_sb", "vector")
            score_ps = stage_sem(sc, "score_ps", "tensor")
            score_sb = stage_sem(sc, "score_sb", "vector")
            scoreT_ps = stage_sem(sc, "scoreT_ps", "tensor")
            runs = stage_sem(sc, "runs", "vector")
            runT_ps = stage_sem(sc, "runT_ps", "tensor")
            runT_sb = stage_sem(sc, "runT_sb", "vector")
            cand_ps = stage_sem(sc, "cand_ps", "tensor")
            maxs = stage_sem(sc, "maxs", "vector")
            corr_sb = stage_sem(sc, "corr_sb", "scalar")
            shift_ps = stage_sem(sc, "shift_ps", "tensor")
            expos = stage_sem(sc, "expos", "vector")
            ex_sb = stage_sem(sc, "ex_sb", "scalar")
            weighted = stage_sem(sc, "weighted", "vector")
            out_ps = stage_sem(sc, "out_ps", "tensor")
            fin1 = stage_sem(sc, "fin1", "vector")
            self_exp = stage_sem(sc, "self_exp", "scalar")
            y_tanh = stage_sem(sc, "y_tanh", "scalar")
            res_ready = stage_sem(sc, "res_ready", "vector")
            we_in = dma_sem("we_in")
            stored1 = dma_sem("stored1")
            stored_steps1 = stage_sem(sc, "stored_steps1", "sync")
            block = sc.enter_context(nc.Block())

            KH = KT // 4 + 1
            NMAX = 11
            S_PS = [[bk[0], bk[1]], [bk[2], bk[3]]]
            SCORE = bk[6][:, 0:HEADS * KT].rearrange("p (h k) -> p h k", h=HEADS)
            SHIFT = bk[7][:, 152:152 + 2 * HEADS * KT].rearrange("p (k h) -> p k h", k=KT)
            SCORET = bk[7][0:RW, 272:400]
            RUNT = bk[7][:, 400:400 + RW]
            OUT = bk[7][0:TN, 0:XW]
            CAND = bk[7][0:TN, 0:2 * RW].rearrange("p (k h) -> p k h", k=KT)

            @block.sync
            def _(sp):
                start(sp, "sync")
                last_i = sp.value_load(n_pairs[0:1, 0:1], min_val=1, max_val=LAST_MAX)
                pairs = last_i + 1

                def load_hot(i, s):
                    e0 = sp.value_load(table[0:1, bass.ds(i * 4 + 2 * s, 1)], min_val=0, max_val=N_EDGES)
                    v0 = sp.value_load(table[0:1, bass.ds(i * 4 + 2 * s + 1, 1)], min_val=0, max_val=LAST_BASE)
                    sp.dma_start(attr1[s][:, :, :], attr[bass.ds(e0, STEP_E), :].rearrange("(k p) c -> p k c", p=128)).then_inc(loadedH[s], 16)
                    sp.dma_start(xr_we[s][0:TN, :], node_rec[bass.ds(v0, TN), 0:D]).then_inc(loadedH[s], 16)

                def load_dst(i, s):
                    e0 = sp.value_load(table[0:1, bass.ds(i * 4 + 2 * s, 1)], min_val=0, max_val=N_EDGES)
                    sp.dma_start(dst85[s][:, :], edge_rows(1, e0).broadcast_to([5, KT, 128])).then_inc(loadedD[s], 16)

                def load_back(i, s):
                    v0 = sp.value_load(table[0:1, bass.ds(i * 4 + 2 * s + 1, 1)], min_val=0, max_val=LAST_BASE)
                    sp.dma_start(ro[s][:, :], node_rec[bass.ds(v0, TN), D:RECW]).then_inc(loadedB[s], 16)
                    sp.dma_start(xo[s][:, :], xl_rows[bass.ds(v0, TN), :]).then_inc(loadedB[s], 16)

                for s in range(2):
                    for n in (TN, TN + ED):
                        sp.dma_start(xr_we[s][n:n + ED, :], w_eT).then_inc(we_in, 16)
                    load_hot(0, s)
                    load_dst(0, s)
                    load_back(0, s)
                sp.sem_inc(stored_steps1, 1)

                def renew_dst(i, s):
                    sp.wait_ge(weighted, i * 4 + 2 * s + 3)
                    sp.sem_inc(passed, 1)
                    load_dst(i + 1, s)

                def renew_hot(i, s):
                    sp.wait_ge(hot1, i * 12 + 6 * s + 7)
                    sp.sem_inc(passed, 1)
                    load_hot(i + 1, s)

                def store(i, s):
                    v0 = sp.value_load(table[0:1, bass.ds(i * 4 + 2 * s + 1, 1)], min_val=0, max_val=LAST_BASE)
                    sp.wait_ge(res_ready, i * 2 + s + 2)
                    sp.sem_inc(passed, 1)
                    sp.dma_start(out[bass.ds(v0, TN), :], res[s][:, :]).then_inc(stored1, 16)

                def stored(i, s):
                    sp.wait_ge(stored1, i * 32 + 16 * s + 16)
                    sp.sem_inc(passed, 1)
                    sp.sem_inc(stored_steps1, 1)

                renew_hot(0, 0)
                renew_hot(0, 1)
                renew_dst(0, 0)
                renew_hot(1, 0)
                with sp.Fori(0, last_i) as i:
                    renew_dst(i, 1)
                    store(i, 0)
                    load_back(i + 1, 0)
                    stored(i, 0)
                    renew_hot(i + 1, 1)
                    renew_dst(i + 1, 0)
                    store(i, 1)
                    load_back(i + 1, 1)
                    stored(i, 1)
                    renew_hot(i + 2, 0)
                for s in range(2):
                    store(last_i, s)
                    stored(last_i, s)
                sp.wait_ge(we_in, 64)
                for s in range(2):
                    sp.wait_ge(loadedH[s], pairs * 32 + 32 * (2 - s))
                    sp.sem_inc(passed, 1)
                    sp.wait_ge(loadedD[s], pairs * 16 + 16 * (1 - s))
                    sp.sem_inc(passed, 1)
                for s in range(2):
                    sp.wait_ge(loadedB[s], pairs * 32)
                    sp.sem_inc(passed, 1)

            @block.gpsimd
            def _(pool):
                last_i = pool.value_load(n_pairs[0:1, 0:1], min_val=1, max_val=LAST_MAX)
                pairs = last_i + 1
                with pool.Fori(0, pairs, 2) as i:
                    for r in range(4):
                        pool.wait_ge(idx_ready1, i * 2 + r + 2)
                        pool.sem_inc(passed, 1)
                        for k in range(KT):
                            pool.indirect_dma_start(rows1[r][:, k, 0:D], None, xl_rows,
                                                    bass.IndirectOffsetOnAxis(ap=idx4[r][:, k:k + 1], axis=0)
                                                    ).then_inc(gathered1[r], 16)

            def later(i, s):
                return not isinstance(i, int) or i * 2 + s > 0

            def at(i, s, r=None):
                return i, s, i * 2 + s if r is None and i * 2 + s < 4 else r or 0

            def steps(eng, last_i, first, turn, last):
                first()
                turn(at(0, 0), at(0, 1), at(1, 0), None)
                turn(at(0, 1), at(1, 0), at(1, 1), at(0, 0))
                turn(at(1, 0), at(1, 1), at(2, 0), at(0, 1))
                with eng.Fori(1, last_i, 2) as i:
                    turn(at(i, 1, 3), at(i + 1, 0, 0), at(i + 1, 1, 1), at(i, 0, 2))
                    turn(at(i + 1, 0, 0), at(i + 1, 1, 1), at(i + 2, 0, 2), at(i, 1, 3))
                    turn(at(i + 1, 1, 1), at(i + 2, 0, 2), at(i + 2, 1, 3), at(i + 1, 0, 0))
                    turn(at(i + 2, 0, 2), at(i + 2, 1, 3), at(i + 3, 0, 0), at(i + 1, 1, 1))
                last(at(last_i, 1, 3), at(last_i, 0, 2))

            @block.tensor
            def _(pe):
                start(pe, "tensor")
                last_i = pe.value_load(n_pairs[0:1, 0:1], min_val=1, max_val=LAST_MAX)
                pairs = last_i + 1

                def turn_hot(i, s, r):
                    pe.wait_ge(hot1, i * 12 + 6 * s + 7)
                    for q, ks in enumerate(QS):
                        if q >= 2:
                            pe.wait_ge(hotT_sb, i * (2 * NQ) + s * NQ + q)
                        for n, k in enumerate(ks):
                            m = pe.transpose(bk[4 + q % 2][:, 128 * n:128 * n + 128], onehot4[r][:, k, :], ident[:, :])
                        m.then_inc(hotT_ps, 1)

                def sums(i, s, r, q, halves=(0, 1)):
                    ks = QS[q]
                    e0, n = 128 * ks[0], 128 * len(ks)
                    if q == 0 and 0 in halves:
                        pe.wait_ge(gathered1[r], i * (8 * KT) + (2 - r // 2) * 8 * KT)
                    if 0 in halves:
                        pe.wait_ge(hotT_sb, i * (2 * NQ) + s * NQ + q + 2)
                        pe.wait_ge(leaky_sb, i * (2 * NQ) + s * NQ + max(q - 1, 0) + 1)
                    for c in halves:
                        to = S_PS[q % 2][c]
                        for m, k in enumerate(ks):
                            pe.matmul(to[:, 128 * m:128 * m + 128], rows1[r][:, k, 128 * c:128 * c + 128],
                                      ident[:, :], is_transpose=True, start=(m == 0), stop=False, skip_group_check=True)
                        pe.matmul(to[:, 0:n], xw_hi[s][:, 128 * c:128 * c + 128], hotT[s][:, e0:e0 + n],
                                  start=False, stop=False, skip_group_check=True)
                        m = pe.matmul(to[:, 0:n], xw_lo[s][:, 128 * c:128 * c + 128], hotT[s][:, e0:e0 + n],
                                      start=False, stop=True, skip_group_check=True)
                    if 1 in halves:
                        m.then_inc(s_ps, 1)

                def scores(i, s, r, q):
                    pe.wait_ge(leaky_sb, i * (2 * NQ) + s * NQ + q + 2)
                    for n, k in enumerate(QS[q]):
                        for c in range(2):
                            m = pe.matmul(SCORE[:, :, k], leaky[q % 2][:, c, 128 * n:128 * n + 128], attc[:, c, :],
                                          start=(c == 0), stop=(c == 1))
                    m.then_inc(score_ps, 1)

                def turn_scores(i, s, r):
                    pe.wait_ge(score_sb, i * 2 + s + 2)
                    pe.transpose(SCORET, score[:, :, :], ident[:, :]).then_inc(scoreT_ps, 1)

                def turn_runs(i, s, r):
                    pe.wait_ge(runs, i * 14 + 7 * s + 8)
                    pe.transpose(RUNT, runmax[:, :], ident[0:RW, 0:RW]).then_inc(runT_ps, 1)

                def candidates(i, s, r):
                    pe.wait_ge(runT_sb, i * 4 + 2 * s + 3)
                    for k in range(KT):
                        m = pe.matmul(CAND[:, k, :], onehot4[r][:, k, 0:TN].bitcast(F32R), runT[:, :, k], start=True, stop=True)
                    m.then_inc(cand_ps, 1)

                def shifts(i, s, r):
                    pe.wait_ge(maxs, i * (2 * NMAX) + s * NMAX + NMAX)
                    for k in range(KT):
                        m = pe.matmul(SHIFT[:, k, :], hotT[s][0:TN, 128 * k:128 * k + 128], nmax_hl[:, :], start=True, stop=True)
                    m.then_inc(shift_ps, 1)

                def outputs(i, s, r):
                    for k in range(KT):
                        if k in (0, KH):
                            pe.wait_ge(weighted, i * 4 + 2 * s + (2 if k == 0 else 3))
                        m = pe.matmul(OUT, onehot4[r][:, k, 0:TN], rows1[r][:, k, :], start=(k == 0), stop=(k == KT - 1))
                    m.then_inc(out_ps, 1)

                def first():
                    turn_hot(*at(0, 0))
                    sums(*at(0, 0), 0)
                    for q in range(1, NQ):
                        sums(*at(0, 0), q)
                        scores(*at(0, 0), q - 1)
                    turn_hot(*at(0, 1))
                    scores(*at(0, 0), NQ - 1)

                def turn(b, f, g, p):
                    turn_scores(*b)
                    sums(*f, 0)
                    turn_runs(*b)
                    sums(*f, 1, (0,))
                    candidates(*b)
                    sums(*f, 1, (1,))
                    scores(*f, 0)
                    shifts(*b)
                    sums(*f, 2)
                    scores(*f, 1)
                    sums(*f, 3)
                    outputs(*b)
                    scores(*f, 2)
                    scores(*f, 3)
                    turn_hot(*g)

                def last(b, p):
                    for stage in (turn_scores, turn_runs, candidates, shifts, outputs):
                        stage(*b)

                steps(pe, last_i, first, turn, last)

            @block.scalar
            def _(act):
                start(act, "scalar")
                last_i = act.value_load(n_pairs[0:1, 0:1], min_val=1, max_val=LAST_MAX)
                pairs = last_i + 1

                def turned(i, s, r):
                    if later(i, s):
                        act.wait_ge(shift_ps, i * 2 + s)
                    for q, ks in enumerate(QS):
                        n = 128 * len(ks)
                        act.wait_ge(hotT_ps, i * (2 * NQ) + s * NQ + q + 2)
                        act.activation(hotT[s][:, 128 * ks[0]:128 * ks[0] + n], bk[4 + q % 2][:, 0:n], ACT.Copy).then_inc(hotT_sb, 1)

                def relu(i, s, r, q):
                    n = 128 * len(QS[q])
                    act.wait_ge(s_ps, i * (2 * NQ) + s * NQ + q + 2)
                    act.wait_ge(leaky_sb, i * (2 * NQ) + s * NQ + max(q - 1, 0) + 1)
                    act.activation(relu8[q % 2][:, 0, 0:n], S_PS[q % 2][0][:, 0:n], ACT.Relu, scale=0.8)
                    act.activation(relu8[q % 2][:, 1, 0:n], S_PS[q % 2][1][:, 0:n], ACT.Relu, scale=0.8).then_inc(relu_sb, 1)

                def correction(i, s, r):
                    act.wait_ge(maxs, i * (2 * NMAX) + s * NMAX + NMAX + 1)
                    if later(i, s):
                        act.wait_ge(fin1, i * 30 + 15 * s - 11)
                    act.activation(corr[:, :], gap[:, :], ACT.Exp).then_inc(corr_sb, 1)

                def weights(i, s, r):
                    act.wait_ge(expos, i * 6 + 3 * s + 4)
                    act.activation(rows1[r][:, :, D:XW].rearrange("p k h -> p h k"), expo[:, :, :], ACT.Exp).then_inc(ex_sb, 1)

                def self_weights(i, s, r):
                    act.wait_ge(fin1, i * 30 + 15 * s + 6)
                    act.activation(c2[:, :, :], gap2[:, :, :], ACT.Exp).then_inc(self_exp, 1)

                def silu_tanh(i, s, r):
                    act.wait_ge(fin1, i * 30 + 15 * s + 16)
                    act.activation(em[:, :], y[:, :], ACT.Tanh, scale=0.5).then_inc(y_tanh, 1)

                def first():
                    turned(*at(0, 0))
                    for q in range(NQ):
                        relu(*at(0, 0), q)
                    turned(*at(0, 1))

                def turn(b, f, g, p):
                    relu(*f, 0)
                    relu(*f, 1)
                    correction(*b)
                    if p:
                        silu_tanh(*p)
                    weights(*b)
                    relu(*f, 2)
                    relu(*f, 3)
                    self_weights(*b)
                    turned(*g)

                def last(b, p):
                    correction(*b)
                    weights(*b)
                    silu_tanh(*p)
                    self_weights(*b)
                    silu_tanh(*b)

                steps(act, last_i, first, turn, last)

            @block.vector
            def _(v):
                start(v, "vector")
                last_i = v.value_load(n_pairs[0:1, 0:1], min_val=1, max_val=LAST_MAX)
                pairs = last_i + 1

                def indices(i, s, r):
                    v.tensor_copy(idx4[r][:, :], idx_all[:, bass.ds(i * (4 * KT) + s * 2 * KT, KT)]).then_inc(idx_ready1, 1)

                def one_hot(i, s, r):
                    v.wait_ge(hot1, i * 12 + 6 * s + 1)
                    v.wait_ge(loadedH[s], i * 32 + 32)
                    v.tensor_scalar(drel[:, :], idx_all[:, bass.ds(i * (4 * KT) + s * 2 * KT + KT, KT)],
                                    baseT[:, bass.ds(i * 2 + s, 1)], None, ALU.subtract).then_inc(hot1, 1)
                    v.tensor_copy(onehot4[r][:, :, TN:TN + ED].bitcast(F32R), attr1[s][:, :, :]).then_inc(hot1, 1)
                    v.tensor_copy(xw_hi[s][:, :], xr_we[s][:, :]).then_inc(hot1, 1)
                    v.wait_ge(hot1, i * 12 + 6 * s + 4)
                    v.tensor_tensor(onehot4[r][:, :, TN + ED:].bitcast(F32R), attr1[s][:, :, :], onehot4[r][:, :, TN:TN + ED],
                                    ALU.subtract).then_inc(hot1, 1)
                    v.tensor_tensor(xw_lo[s][:, :], xr_we[s][:, :], xw_hi[s][:, :], ALU.subtract).then_inc(hot1, 1)
                    v.tensor_tensor(onehot4[r][:, :, 0:TN].bitcast(F32R), iota_n[:, 0:TN].unsqueeze(1).broadcast_to([128, KT, TN]),
                                    drel[:, :].unsqueeze(2).broadcast_to([128, KT, TN]), ALU.is_equal).then_inc(hot1, 1)

                def leak(i, s, r, q):
                    n = 128 * len(QS[q])
                    v.wait_ge(relu_sb, i * (2 * NQ) + s * NQ + q + 2)
                    v.wait_ge(score_ps, i * (2 * NQ) + s * NQ + max(q - 1, 0) + 1)
                    for c in range(2):
                        ins = v.scalar_tensor_tensor(out=leaky[q % 2][:, c, 0:n], in0=S_PS[q % 2][c][:, 0:n], scalar=0.2,
                                                     in1=relu8[q % 2][:, c, 0:n], op0=ALU.mult, op1=ALU.add)
                    ins.then_inc(leaky_sb, 1)

                def take_scores(i, s, r):
                    v.wait_ge(score_ps, i * (2 * NQ) + s * NQ + NQ + 1)
                    v.tensor_copy(score[:, 0:HEADS, :], SCORE).then_inc(score_sb, 1)

                def mark_runs(i, s, r):
                    v.wait_ge(loadedD[s], i * 16 + 16)
                    v.wait_ge(runs, i * 14 + 7 * s + 1)
                    v.tensor_tensor(begins[:, 1:128], dst85[s][:, 1:128], dst85[s][:, 0:127], ALU.not_equal).then_inc(runs, 1)
                    v.wait_ge(runs, i * 14 + 7 * s + 2)
                    v.tensor_copy(ends[:, :], begins[:, 1:129]).then_inc(runs, 1)
                    v.memset(begins[:, 0:1], 1.0).then_inc(runs, 1)
                    v.wait_ge(runs, i * 14 + 7 * s + 4)
                    v.tensor_scalar(begins[:, 0:128], begins[:, 0:128], -BIG, None, ALU.mult).then_inc(runs, 1)

                def run_maxima(i, s, r):
                    v.wait_ge(runs, i * 14 + 7 * s + 5)
                    v.wait_ge(scoreT_ps, i * 2 + s + 2)
                    v.tensor_tensor_scan(runmax[:, :], begins[:, 0:128], SCORET, 0.0, ALU.add, ALU.max).then_inc(runs, 1)
                    v.wait_ge(runs, i * 14 + 7 * s + 6)
                    v.tensor_tensor(runmax[:, :], runmax[:, :], ends[:, :], ALU.mult).then_inc(runs, 1)
                    v.wait_ge(runs, i * 14 + 7 * s + 7)
                    v.memset(begins[:, 0:1], 1.0).then_inc(runs, 1)

                def take_runs(i, s, r):
                    v.wait_ge(runT_ps, i * 2 + s + 2)
                    v.tensor_copy(runT[:, 0:5, :], RUNT.rearrange("p (h k) -> p h k", h=5)).then_inc(runT_sb, 1)
                    v.wait_ge(runT_sb, i * 4 + 2 * s + 2)
                    v.tensor_tensor(runT[:, 5:10, :], RUNT.rearrange("p (h k) -> p h k", h=5), runT[:, 0:5, :],
                                    ALU.subtract).then_inc(runT_sb, 1)

                def maxima(i, s, r):
                    n = i * (2 * NMAX) + s * NMAX
                    keep = keepT[0:TN, bass.ds(i * 2 + s, 1)]
                    v.wait_ge(maxs, n + 1)
                    v.wait_ge(cand_ps, i * 2 + s + 2)
                    v.tensor_scalar(pen[:, :], CAND[:, :, HEADS], 1.0, BIG, ALU.subtract, ALU.mult).then_inc(maxs, 1)
                    v.tensor_scalar(prevmax[:, :], keep.broadcast_to([TN, HEADS]), 1.0, BIG, ALU.subtract, ALU.mult).then_inc(maxs, 1)
                    v.tensor_copy(cand[:, :, :], CAND[:, :, 0:HEADS]).then_inc(maxs, 1)
                    v.wait_ge(maxs, n + 4)
                    v.scalar_tensor_tensor(out=prevmax[:, :], in0=nmax[1 - s][:, :], scalar=keep, in1=prevmax[:, :],
                                           op0=ALU.mult, op1=ALU.add).then_inc(maxs, 1)
                    v.tensor_tensor(cand[:, :, :], CAND[:, :, 5:5 + HEADS], cand[:, :, :], ALU.add).then_inc(maxs, 1)
                    v.wait_ge(maxs, n + 6)
                    v.tensor_tensor(cand[:, :, :], cand[:, :, :], pen[:, :].unsqueeze(2).broadcast_to([TN, KT, HEADS]), ALU.add).then_inc(maxs, 1)
                    v.wait_ge(maxs, n + 7)
                    v.tensor_reduce(stepmax[:, :], cand[:, :, :].rearrange("p k h -> p h k"), AX.X, ALU.max).then_inc(maxs, 1)
                    v.wait_ge(maxs, n + 8)
                    v.tensor_tensor(nmax[s][:, :], stepmax[:, :], prevmax[:, :], ALU.max).then_inc(maxs, 1)
                    v.wait_ge(maxs, n + 9)
                    v.tensor_copy(nmax_hl[:, 0:HEADS], nmax[s][:, :]).then_inc(maxs, 1)
                    v.wait_ge(maxs, n + 10)
                    v.tensor_tensor(nmax_hl[:, HEADS:], nmax[s][:, :], nmax_hl[:, 0:HEADS], ALU.subtract).then_inc(maxs, 1)
                    v.wait_ge(corr_sb, i * 2 + s + 1)
                    v.tensor_tensor(gap[:, :], prevmax[:, :], nmax[s][:, :], ALU.subtract).then_inc(maxs, 1)

                def exponents(i, s, r):
                    v.wait_ge(expos, i * 6 + 3 * s + 1)
                    v.wait_ge(shift_ps, i * 2 + s + 2)
                    v.tensor_tensor(expo[:, :, :], score[:, 0:HEADS, :], SHIFT[:, :, 0:HEADS].rearrange("p k h -> p h k"),
                                    ALU.subtract).then_inc(expos, 1)
                    v.wait_ge(expos, i * 6 + 3 * s + 2)
                    v.tensor_tensor(expo[:, :, :], expo[:, :, :], SHIFT[:, :, HEADS:].rearrange("p k h -> p h k"),
                                    ALU.subtract).then_inc(expos, 1)
                    v.wait_ge(expos, i * 6 + 3 * s + 3)
                    v.tensor_scalar(expo[:, :, :], expo[:, :, :], 0.0, None, ALU.min).then_inc(expos, 1)

                def weigh(i, s, r):
                    v.wait_ge(ex_sb, i * 2 + s + 2)
                    by_tile = rows1[r][:, :, D:XW]
                    for k0, k1 in ((0, KH), (KH, KT)):
                        v.tensor_tensor(rows1[r][:, k0:k1, 0:D].rearrange("p k (h c) -> p k h c", h=HEADS),
                                        rows1[r][:, k0:k1, 0:D].rearrange("p k (h c) -> p k h c", h=HEADS),
                                        by_tile[:, k0:k1, :].unsqueeze(3).broadcast_to([128, k1 - k0, HEADS, HD]),
                                        ALU.mult).then_inc(weighted, 1)

                def by_head(a):
                    return a.rearrange("p (h c) -> p h c", h=HEADS)

                def wide(a):
                    return a.unsqueeze(2).broadcast_to([TN, HEADS, HD])

                def add_up(i, s, r):
                    v.wait_ge(fin1, i * 30 + 15 * s + 1)
                    keep = keepT[0:TN, bass.ds(i * 2 + s, 1)]

                    v.wait_ge(loadedB[s], i * 32 + 32)
                    v.wait_ge(corr_sb, i * 2 + s + 2)
                    v.tensor_tensor(selfm[:, :], nmax[s][:, :], ro[s][:, D:D + HEADS], ALU.max).then_inc(fin1, 1)
                    v.scalar_tensor_tensor(out=by_head(scaled[:, 0:D]), in0=by_head(acc[1 - s][:, 0:D]), scalar=keep,
                                           in1=wide(corr[:, :]), op0=ALU.mult, op1=ALU.mult).then_inc(fin1, 1)
                    v.scalar_tensor_tensor(out=scaled[:, D:XW], in0=acc[1 - s][:, D:XW], scalar=keep,
                                           in1=corr[:, :], op0=ALU.mult, op1=ALU.mult).then_inc(fin1, 1)
                    v.wait_ge(fin1, i * 30 + 15 * s + 4)
                    v.tensor_tensor(gap2[:, 0, :], nmax[s][:, :], selfm[:, :], ALU.subtract).then_inc(fin1, 1)
                    v.tensor_tensor(gap2[:, 1, :], ro[s][:, D:D + HEADS], selfm[:, :], ALU.subtract).then_inc(fin1, 1)
                    v.wait_ge(out_ps, i * 2 + s + 2)
                    v.tensor_tensor(acc[s][:, :], scaled[:, :], OUT, ALU.add).then_inc(fin1, 1)
                    indices(i + 2, s, r)
                    v.wait_ge(fin1, i * 30 + 15 * s + 7)

                def finish(i, s, r):
                    v.wait_ge(self_exp, i * 2 + s + 2)
                    v.tensor_tensor(by_head(tot[:, 0:D]), by_head(acc[s][:, 0:D]), wide(c2[:, 0, :]), ALU.mult).then_inc(fin1, 1)
                    v.tensor_tensor(tot[:, D:XW], acc[s][:, D:XW], c2[:, 0, :], ALU.mult).then_inc(fin1, 1)
                    v.tensor_tensor(by_head(own[:, :]), by_head(xo[s][:, :]), wide(c2[:, 1, :]), ALU.mult).then_inc(fin1, 1)
                    v.wait_ge(fin1, i * 30 + 15 * s + 10)
                    v.tensor_tensor(tot[:, 0:D], tot[:, 0:D], own[:, :], ALU.add).then_inc(fin1, 1)
                    v.tensor_tensor(rden[:, :], tot[:, D:XW], c2[:, 1, :], ALU.add).then_inc(fin1, 1)
                    v.wait_ge(fin1, i * 30 + 15 * s + 12)
                    v.tensor_scalar(rden[:, :], rden[:, :], 1e-16, None, ALU.add).then_inc(fin1, 1)
                    v.wait_ge(fin1, i * 30 + 15 * s + 13)
                    v.reciprocal(rden[:, :], rden[:, :]).then_inc(fin1, 1)
                    v.wait_ge(fin1, i * 30 + 15 * s + 14)
                    v.tensor_tensor(by_head(y[:, :]), by_head(tot[:, 0:D]), wide(rden[:, :]), ALU.mult).then_inc(fin1, 1)
                    v.wait_ge(fin1, i * 30 + 15 * s + 15)
                    v.tensor_tensor(y[:, :], y[:, :], bout[0:TN, :], ALU.add).then_inc(fin1, 1)

                def silu(i, s, r):
                    v.wait_ge(silu_v, i * 2 + s + 1)
                    v.wait_ge(y_tanh, i * 2 + s + 2)
                    v.scalar_tensor_tensor(out=em[:, :], in0=em[:, :], scalar=1.0, in1=y[:, :],
                                           op0=ALU.add, op1=ALU.mult).then_inc(silu_v, 1)
                    v.wait_ge(silu_v, i * 2 + s + 2)
                    v.wait_ge(stored_steps1, i * 2 + s + 1)
                    v.scalar_tensor_tensor(out=res[s][:, :], in0=em[:, :], scalar=0.5, in1=ro[s][:, 0:D],
                                           op0=ALU.mult, op1=ALU.add).then_inc(res_ready, 1)

                def first():
                    v.wait_ge(we_in, 64)
                    for n in range(4):
                        indices(*at(n // 2, n % 2))
                    v.memset(score[:, HEADS:, :], 1.0)
                    v.memset(begins[:, 0:1], 1.0)
                    v.memset(begins[:, 128:129], 1.0)
                    v.memset(nmax[1][:, :], 0.0)
                    v.memset(acc[1][:, :], 0.0)
                    one_hot(*at(0, 0))
                    for q in range(NQ):
                        leak(*at(0, 0), q)
                    one_hot(*at(0, 1))
                    mark_runs(*at(0, 0))
                    take_scores(*at(0, 0))

                def turn(b, f, g, p):
                    run_maxima(*b)
                    take_runs(*b)
                    leak(*f, 0)
                    maxima(*b)
                    leak(*f, 1)
                    if p:
                        finish(*p)
                    exponents(*b)
                    weigh(*b)
                    leak(*f, 2)
                    if p:
                        silu(*p)
                    one_hot(*g)
                    leak(*f, 3)
                    mark_runs(*f)
                    add_up(*b)
                    take_scores(*f)

                def last(b, p):
                    for stage in (run_maxima, take_runs, maxima, exponents, weigh):
                        stage(*b)
                    finish(*p)
                    silu(*p)
                    add_up(*b)
                    finish(*b)
                    silu(*b)

                steps(v, last_i, first, turn, last)


def kernel(**inputs):
    import concourse.bacc as bacc
    from concourse.bass_utils import run_bass_kernel_spmd as run

    a = {k: np.asarray(v) for k, v in inputs.items()}
    order = np.r_[0:DH, 2 * DH:4 * DH]

    def columns(v, n):
        return np.ascontiguousarray(v.reshape(n, 128).T)

    arrays = {
        "x": np.pad(a["x"], ((0, N_PAD - N_NODES), (0, 0))),
        "edges": np.stack([np.pad(a["src"], (0, STEP_E)), np.pad(a["dst"], (0, STEP_E), constant_values=N_PAD)]),
        "attr": np.pad(a["edge_attr_16"], ((0, STEP_E), (0, 0))),
        "w_rr": np.concatenate([a["L0_gnn_W_rel"], a["L0_gnn_W_root"]]),
        "b_rel": columns(a["L0_gnn_b_rel"], NJ),
        "w_ihT": np.ascontiguousarray(a["L0_gnn_W_ih"][order].T),
        "b_ih": columns(a["L0_gnn_b_ih"][order], 3 * NJ),
        "b_hh": columns(a["L0_gnn_b_hh"][order], 3 * NJ),
        "w_fc": a["L0_gnn_W_fc"],
        "b_fc": a["L0_gnn_b_fc"],
        "w_lr": np.ascontiguousarray(np.concatenate([a["L1_gnn_W_l"].T, a["L1_gnn_W_r"].T], axis=1)),
        "b_l": a["L1_gnn_b_l"],
        "b_r": a["L1_gnn_b_r"],
        "w_eT": np.ascontiguousarray(a["L1_gnn_W_e"].T),
        "att": np.ascontiguousarray(a["L1_gnn_att"].reshape(-1)),
        "bias": a["L1_gnn_bias"],
    }
    nc = bacc.Bacc("TRN2", target_bir_lowering=False, num_devices=1)
    args = [nc.dram_tensor(k, v.shape, mybir.dt.from_np(v.dtype), kind="ExternalInput").ap() for k, v in arrays.items()]
    out = nc.dram_tensor("out", [N_PAD, D], F32, kind="ExternalOutput").ap()
    gnn_layers(nc, *args, out)
    return run(nc, [arrays], core_ids=[0]).results[0]["out"][0:N_NODES]
```
